# Optimizing a Trainium2 kernel written in Bass

```python
import numpy as np
import jax
import jax.numpy as jnp

def _softmax(x, axis=-1):
    return jax.nn.softmax(x, axis=axis)

def _gelu(x):
    return jax.nn.gelu(x, approximate=True)

def _silu(x):
    return jax.nn.silu(x)

def _sigmoid(x):
    return jax.nn.sigmoid(x)

def _layernorm(x, axis=-1, eps=1e-05):
    m = jnp.mean(x, axis=axis, keepdims=True)
    v = jnp.var(x, axis=axis, keepdims=True)
    return (x - m) / jnp.sqrt(v + eps)

def _scatter_add(tgt, idx, src, axis=0):
    return tgt.at[idx].add(src)

def _segment_sum(src, seg, n):
    return jax.ops.segment_sum(src, seg, n)
kernel_name = 'mk_recurrent_d2_jaxref_r4_9887a3'

def setup_inputs(seed: int=0):
    np.random.seed(seed)
    _w = jnp.asarray

    def _L0_attn_setup():
        import jax, jax.numpy as jnp
        import numpy as np
        from jax import lax
        K_STEEP = 10.0
        V_TH_MIN = 0.1
        EK_FLOOR = 0.01

        def _bio_ssm(h, W_xz, W_dt, b_dt, A_log, W_B, W_C, D_skip, W_out, v_th):
            T, B, D = h.shape
            N = A_log.shape[1]
            xz = jnp.einsum('tbd,de->tbe', h, W_xz)
            x, z = jnp.split(xz, 2, axis=-1)
            dt = jax.nn.softplus(jnp.einsum('tbd,de->tbe', x, W_dt) + b_dt)
            A = -jnp.exp(A_log)
            Bm = jnp.einsum('tbd,dn->tbn', h, W_B)
            Cm = jnp.einsum('tbd,dn->tbn', h, W_C)
            decay = jnp.exp(dt[..., None] * A)
            inp = (dt * x)[..., None] * Bm[:, :, None, :]

            def step(s, td):
                dec, ip, c = td
                s = dec * s + ip
                y = jnp.einsum('bdn,bn->bd', s, c)
                return (s, y)
            s0 = jnp.zeros((B, D, N), h.dtype)
            _, y = lax.scan(step, s0, (decay, inp, Cm))
            y = y + D_skip * x
            vth = jnp.maximum(v_th, V_TH_MIN)
            spike_p = jax.nn.sigmoid(K_STEEP * (y - vth))
            y_sp = y * spike_p
            pc = jnp.mean(spike_p)
            efc = jnp.mean(jax.nn.relu(EK_FLOOR - y * y))
            out = jnp.einsum('tbd,de->tbe', y_sp * jax.nn.silu(z), W_out)
            return (out, pc, efc)
        key = jax.random.key(seed)
        ks = jax.random.split(key, 11)
        B, T, D, N = (2, 256, 256, 16)
        s = lambda fan: 1.0 / np.sqrt(fan)
        return {'hidden_states': jax.random.normal(ks[0], (B, T, D), jnp.float32), 'W_xz': jax.random.normal(ks[1], (D, 2 * D), jnp.float32) * s(D), 'W_dt': jax.random.normal(ks[2], (D, D), jnp.float32) * s(D), 'b_dt': jax.random.normal(ks[3], (D,), jnp.float32) * 0.1, 'A_log': jax.random.uniform(ks[4], (D, N), jnp.float32, 0.0, 1.0), 'W_B': jax.random.normal(ks[5], (D, N), jnp.float32) * s(D), 'W_C': jax.random.normal(ks[6], (D, N), jnp.float32) * s(D), 'D_skip': jax.random.normal(ks[7], (D,), jnp.float32) * 0.1, 'W_out': jax.random.normal(ks[8], (D, D), jnp.float32) * s(D), 'v_th': jax.random.uniform(ks[9], (D,), jnp.float32, 0.0, 0.5)}
    _L0_attn_in = _L0_attn_setup()

    def _L0_ffn_setup():
        import jax, jax.numpy as jnp
        import numpy as np
        FEATURES = 256
        D_IN = 256

        def fp8_gemm_optimized(x, input_scale, kernel, kernel_scale):
            s_in = input_scale[0]
            s_k = kernel_scale[0]
            x_q = (x.astype(jnp.float32) / s_in).astype(jnp.float8_e4m3fn)
            k_q = (kernel.astype(jnp.float32) / s_k).astype(jnp.float8_e4m3fn)
            y = jnp.dot(x_q.astype(jnp.float32), k_q.astype(jnp.float32), preferred_element_type=jnp.float32)
            return y * (s_in * s_k)
        key = jax.random.key(seed)
        kx, kk, kb = jax.random.split(key, 3)
        x = jax.random.normal(kx, (4, 2048, D_IN), dtype=jnp.float32)
        limit = np.sqrt(6.0 / (D_IN + FEATURES)).astype(np.float32)
        kernel = jax.random.uniform(kk, (D_IN, FEATURES), dtype=jnp.float32, minval=-limit, maxval=limit).astype(jnp.bfloat16)
        input_scale = jnp.ones((1,), dtype=jnp.float32)
        kernel_scale = jnp.ones((1,), dtype=jnp.float32)
        bias = jnp.zeros((FEATURES,), dtype=jnp.bfloat16)
        return {'x': x, 'kernel': kernel, 'input_scale': input_scale, 'kernel_scale': kernel_scale, 'bias': bias}
    _L0_ffn_in = _L0_ffn_setup()

    def _L1_attn_setup():
        import jax, jax.numpy as jnp
        import numpy as np
        B, T, D, C = (16, 1024, 256, 128)
        key = jax.random.key(seed)
        ks = jax.random.split(key, 15)

        def w(k, out_dim, in_dim):
            return jax.random.normal(k, (out_dim, in_dim), jnp.float32) / np.sqrt(in_dim).astype(np.float32)
        return {'x': jax.random.normal(ks[0], (B, T, D), jnp.float32), 'Wq': w(ks[1], C, D), 'bq': jnp.zeros((C,), jnp.float32), 'Wk': w(ks[2], C, D), 'bk': jnp.zeros((C,), jnp.float32), 'Wv': w(ks[3], C, D), 'bv': jnp.zeros((C,), jnp.float32), 'Wa': w(ks[4], 1, D), 'ba': jnp.zeros((1,), jnp.float32), 'Wb': w(ks[5], 1, D), 'bb': jnp.zeros((1,), jnp.float32), 'Wg': w(ks[6], C, D), 'bg': jnp.zeros((C,), jnp.float32), 'Wo': w(ks[7], D, C), 'bo': jnp.zeros((D,), jnp.float32)}
    _L1_attn_in = _L1_attn_setup()

    def _L1_ffn_setup():
        import jax, jax.numpy as jnp
        import numpy as np
        import math
        D = 256
        H = 16
        E = 8
        TOPK = 2
        LAT = D // 2
        KPH = LAT // H
        HD = D // H

        def _forward(hs, q_w, q_b, k_w, k_b, v_w, v_b, o_w, o_b, router_w, router_b, w1, b1, w2, b2):
            B, S, _ = hs.shape
            Q = (hs @ q_w + q_b).reshape(B, S, H, HD).transpose(0, 2, 1, 3)
            K = (hs @ k_w + k_b).reshape(B, S, H, KPH).transpose(0, 2, 1, 3)
            V = (hs @ v_w + v_b).reshape(B, S, H, KPH).transpose(0, 2, 1, 3)
            scores = jnp.einsum('bhsk,bhtk->bhst', Q[..., :KPH], K) / math.sqrt(KPH)
            attn = jax.nn.softmax(scores, axis=-1)
            ao = jnp.einsum('bhst,bhtv->bhsv', attn, V)
            ao = ao.transpose(0, 2, 1, 3).reshape(B, S, H * KPH)
            ao = jnp.concatenate([ao, jnp.zeros((B, S, D - LAT), ao.dtype)], axis=-1)
            mla_out = ao @ o_w + o_b
            probs = jax.nn.softmax(mla_out @ router_w + router_b, axis=-1)
            topw, topi = jax.lax.top_k(probs, TOPK)
            topw = topw / (topw.sum(-1, keepdims=True) + 1e-08)
            combine = jnp.sum(jax.nn.one_hot(topi, E, dtype=probs.dtype) * topw[..., None], axis=-2)
            h1 = jnp.einsum('bsd,edf->ebsf', mla_out, w1) + b1[:, None, None, :]
            h1 = jax.nn.gelu(h1, approximate=False)
            h2 = jnp.einsum('ebsf,efd->ebsd', h1, w2) + b2[:, None, None, :]
            moe_out = jnp.einsum('bse,ebsd->bsd', combine, h2)
            return hs + 0.3 * moe_out
        key = jax.random.key(seed)
        ks = jax.random.split(key, 16)
        s = 0.02
        inp = {'hidden_states': jax.random.normal(ks[0], (2, 512, D), jnp.float32), 'q_w': jax.random.normal(ks[1], (D, D), jnp.float32) * s, 'q_b': jnp.zeros((D,), jnp.float32), 'k_w': jax.random.normal(ks[2], (D, LAT), jnp.float32) * s, 'k_b': jnp.zeros((LAT,), jnp.float32), 'v_w': jax.random.normal(ks[3], (D, LAT), jnp.float32) * s, 'v_b': jnp.zeros((LAT,), jnp.float32), 'o_w': jax.random.normal(ks[4], (D, D), jnp.float32) * s, 'o_b': jnp.zeros((D,), jnp.float32), 'router_w': jax.random.normal(ks[5], (D, E), jnp.float32) * s, 'router_b': jnp.zeros((E,), jnp.float32), 'w1': jax.random.normal(ks[6], (E, D, 2 * D), jnp.float32) * s, 'b1': jnp.zeros((E, 2 * D), jnp.float32), 'w2': jax.random.normal(ks[7], (E, 2 * D, D), jnp.float32) * s, 'b2': jnp.zeros((E, D), jnp.float32)}
        return inp
    _L1_ffn_in = _L1_ffn_setup()
    _d = {'L0_attn_hidden_states': _L0_attn_in['hidden_states'], 'L0_attn_W_xz': _L0_attn_in['W_xz'], 'L0_attn_W_dt': _L0_attn_in['W_dt'], 'L0_attn_b_dt': _L0_attn_in['b_dt'], 'L0_attn_A_log': _L0_attn_in['A_log'], 'L0_attn_W_B': _L0_attn_in['W_B'], 'L0_attn_W_C': _L0_attn_in['W_C'], 'L0_attn_D_skip': _L0_attn_in['D_skip'], 'L0_attn_W_out': _L0_attn_in['W_out'], 'L0_attn_v_th': _L0_attn_in['v_th'], 'L0_ffn_kernel': _L0_ffn_in['kernel'], 'L0_ffn_input_scale': _L0_ffn_in['input_scale'], 'L0_ffn_kernel_scale': _L0_ffn_in['kernel_scale'], 'L0_ffn_bias': _L0_ffn_in['bias'], 'L1_attn_Wq': _L1_attn_in['Wq'], 'L1_attn_bq': _L1_attn_in['bq'], 'L1_attn_Wk': _L1_attn_in['Wk'], 'L1_attn_bk': _L1_attn_in['bk'], 'L1_attn_Wv': _L1_attn_in['Wv'], 'L1_attn_bv': _L1_attn_in['bv'], 'L1_attn_Wa': _L1_attn_in['Wa'], 'L1_attn_ba': _L1_attn_in['ba'], 'L1_attn_Wb': _L1_attn_in['Wb'], 'L1_attn_bb': _L1_attn_in['bb'], 'L1_attn_Wg': _L1_attn_in['Wg'], 'L1_attn_bg': _L1_attn_in['bg'], 'L1_attn_Wo': _L1_attn_in['Wo'], 'L1_attn_bo': _L1_attn_in['bo'], 'L1_ffn_q_w': _L1_ffn_in['q_w'], 'L1_ffn_q_b': _L1_ffn_in['q_b'], 'L1_ffn_k_w': _L1_ffn_in['k_w'], 'L1_ffn_k_b': _L1_ffn_in['k_b'], 'L1_ffn_v_w': _L1_ffn_in['v_w'], 'L1_ffn_v_b': _L1_ffn_in['v_b'], 'L1_ffn_o_w': _L1_ffn_in['o_w'], 'L1_ffn_o_b': _L1_ffn_in['o_b'], 'L1_ffn_router_w': _L1_ffn_in['router_w'], 'L1_ffn_router_b': _L1_ffn_in['router_b'], 'L1_ffn_w1': _L1_ffn_in['w1'], 'L1_ffn_b1': _L1_ffn_in['b1'], 'L1_ffn_w2': _L1_ffn_in['w2'], 'L1_ffn_b2': _L1_ffn_in['b2']}
    _x0 = _d['L0_attn_hidden_states']
    _d['L0_attn_hidden_states'] = jax.random.normal(jax.random.fold_in(jax.random.key(seed), 1), (8, 1024, 256), dtype=_x0.dtype)
    del _x0
    return _d

def reference(L0_attn_hidden_states, L0_attn_W_xz, L0_attn_W_dt, L0_attn_b_dt, L0_attn_A_log, L0_attn_W_B, L0_attn_W_C, L0_attn_D_skip, L0_attn_W_out, L0_attn_v_th, L0_ffn_kernel, L0_ffn_input_scale, L0_ffn_kernel_scale, L0_ffn_bias, L1_attn_Wq, L1_attn_bq, L1_attn_Wk, L1_attn_bk, L1_attn_Wv, L1_attn_bv, L1_attn_Wa, L1_attn_ba, L1_attn_Wb, L1_attn_bb, L1_attn_Wg, L1_attn_bg, L1_attn_Wo, L1_attn_bo, L1_ffn_q_w, L1_ffn_q_b, L1_ffn_k_w, L1_ffn_k_b, L1_ffn_v_w, L1_ffn_v_b, L1_ffn_o_w, L1_ffn_o_b, L1_ffn_router_w, L1_ffn_router_b, L1_ffn_w1, L1_ffn_b1, L1_ffn_w2, L1_ffn_b2):

    def _L0_attn_ref(hidden_states, W_xz, W_dt, b_dt, A_log, W_B, W_C, D_skip, W_out, v_th):
        import jax, jax.numpy as jnp
        import numpy as np
        from jax import lax
        K_STEEP = 10.0
        V_TH_MIN = 0.1
        EK_FLOOR = 0.01

        def _bio_ssm(h, W_xz, W_dt, b_dt, A_log, W_B, W_C, D_skip, W_out, v_th):
            T, B, D = h.shape
            N = A_log.shape[1]
            xz = jnp.einsum('tbd,de->tbe', h, W_xz)
            x, z = jnp.split(xz, 2, axis=-1)
            dt = jax.nn.softplus(jnp.einsum('tbd,de->tbe', x, W_dt) + b_dt)
            A = -jnp.exp(A_log)
            Bm = jnp.einsum('tbd,dn->tbn', h, W_B)
            Cm = jnp.einsum('tbd,dn->tbn', h, W_C)
            decay = jnp.exp(dt[..., None] * A)
            inp = (dt * x)[..., None] * Bm[:, :, None, :]

            def step(s, td):
                dec, ip, c = td
                s = dec * s + ip
                y = jnp.einsum('bdn,bn->bd', s, c)
                return (s, y)
            s0 = jnp.zeros((B, D, N), h.dtype)
            _, y = lax.scan(step, s0, (decay, inp, Cm))
            y = y + D_skip * x
            vth = jnp.maximum(v_th, V_TH_MIN)
            spike_p = jax.nn.sigmoid(K_STEEP * (y - vth))
            y_sp = y * spike_p
            pc = jnp.mean(spike_p)
            efc = jnp.mean(jax.nn.relu(EK_FLOOR - y * y))
            out = jnp.einsum('tbd,de->tbe', y_sp * jax.nn.silu(z), W_out)
            return (out, pc, efc)
        h = jnp.transpose(hidden_states, (1, 0, 2))
        h_out, pc, efc = _bio_ssm(h, W_xz, W_dt, b_dt, A_log, W_B, W_C, D_skip, W_out, v_th)
        out = h_out - h
        return jnp.transpose(out, (1, 0, 2))

    def _L0_ffn_ref(x, kernel, input_scale, kernel_scale, bias):
        import jax, jax.numpy as jnp
        import numpy as np
        FEATURES = 256
        D_IN = 256

        def fp8_gemm_optimized(x, input_scale, kernel, kernel_scale):
            s_in = input_scale[0]
            s_k = kernel_scale[0]
            x_q = (x.astype(jnp.float32) / s_in).astype(jnp.float8_e4m3fn)
            k_q = (kernel.astype(jnp.float32) / s_k).astype(jnp.float8_e4m3fn)
            y = jnp.dot(x_q.astype(jnp.float32), k_q.astype(jnp.float32), preferred_element_type=jnp.float32)
            return y * (s_in * s_k)
        dtype = jnp.bfloat16
        x = x.astype(dtype)
        orig_shape = x.shape
        x2 = x.reshape(-1, x.shape[-1])
        y = fp8_gemm_optimized(x2, input_scale, kernel, kernel_scale)
        y = y.astype(dtype) + bias
        return y.reshape(orig_shape[:-1] + (FEATURES,))

    def _L1_attn_ref(x, Wq, bq, Wk, bk, Wv, bv, Wa, ba, Wb, bb, Wg, bg, Wo, bo):
        import jax, jax.numpy as jnp
        import numpy as np
        B, T, D, C = (16, 1024, 256, 128)
        q = x @ Wq.T + bq
        k = x @ Wk.T + bk
        k = k / jnp.maximum(jnp.linalg.norm(k, axis=-1, keepdims=True), 1e-12)
        v = x @ Wv.T + bv
        alpha = jax.nn.sigmoid(x @ Wa.T + ba)
        beta = jax.nn.sigmoid(x @ Wb.T + bb)
        gate = jax.nn.sigmoid(x @ Wg.T + bg)
        Bb, Tt, Dd = x.shape
        Cc = q.shape[-1]

        def step(S, inp):
            q_t, k_t, v_t, a_t, b_t = inp
            a = a_t[:, :, None]
            b = b_t[:, :, None]
            Sk = jnp.einsum('bij,bj->bi', S, k_t)
            S = a * (S - b * (Sk[:, :, None] * k_t[:, None, :])) + b * (v_t[:, :, None] * k_t[:, None, :])
            o = jnp.einsum('bi,bij->bj', q_t, S)
            return (S, o)
        xs = (q.swapaxes(0, 1), k.swapaxes(0, 1), v.swapaxes(0, 1), alpha.swapaxes(0, 1), beta.swapaxes(0, 1))
        S0 = jnp.zeros((Bb, Cc, Cc), x.dtype)
        _, o = jax.lax.scan(step, S0, xs)
        o = o.swapaxes(0, 1) * gate
        return o @ Wo.T + bo

    def _L1_ffn_ref(hidden_states, q_w, q_b, k_w, k_b, v_w, v_b, o_w, o_b, router_w, router_b, w1, b1, w2, b2):
        import jax, jax.numpy as jnp
        import numpy as np
        import math
        D = 256
        H = 16
        E = 8
        TOPK = 2
        LAT = D // 2
        KPH = LAT // H
        HD = D // H

        def _forward(hs, q_w, q_b, k_w, k_b, v_w, v_b, o_w, o_b, router_w, router_b, w1, b1, w2, b2):
            B, S, _ = hs.shape
            Q = (hs @ q_w + q_b).reshape(B, S, H, HD).transpose(0, 2, 1, 3)
            K = (hs @ k_w + k_b).reshape(B, S, H, KPH).transpose(0, 2, 1, 3)
            V = (hs @ v_w + v_b).reshape(B, S, H, KPH).transpose(0, 2, 1, 3)
            scores = jnp.einsum('bhsk,bhtk->bhst', Q[..., :KPH], K) / math.sqrt(KPH)
            attn = jax.nn.softmax(scores, axis=-1)
            ao = jnp.einsum('bhst,bhtv->bhsv', attn, V)
            ao = ao.transpose(0, 2, 1, 3).reshape(B, S, H * KPH)
            ao = jnp.concatenate([ao, jnp.zeros((B, S, D - LAT), ao.dtype)], axis=-1)
            mla_out = ao @ o_w + o_b
            probs = jax.nn.softmax(mla_out @ router_w + router_b, axis=-1)
            topw, topi = jax.lax.top_k(probs, TOPK)
            topw = topw / (topw.sum(-1, keepdims=True) + 1e-08)
            combine = jnp.sum(jax.nn.one_hot(topi, E, dtype=probs.dtype) * topw[..., None], axis=-2)
            h1 = jnp.einsum('bsd,edf->ebsf', mla_out, w1) + b1[:, None, None, :]
            h1 = jax.nn.gelu(h1, approximate=False)
            h2 = jnp.einsum('ebsf,efd->ebsd', h1, w2) + b2[:, None, None, :]
            moe_out = jnp.einsum('bse,ebsd->bsd', combine, h2)
            return hs + 0.3 * moe_out
        return _forward(hidden_states, q_w, q_b, k_w, k_b, v_w, v_b, o_w, o_b, router_w, router_b, w1, b1, w2, b2)
    x = L0_attn_hidden_states
    xn = _layernorm(x, axis=-1)
    s = _L0_attn_ref(xn, L0_attn_W_xz, L0_attn_W_dt, L0_attn_b_dt, L0_attn_A_log, L0_attn_W_B, L0_attn_W_C, L0_attn_D_skip, L0_attn_W_out, L0_attn_v_th)
    g = _silu(_L0_ffn_ref(xn, L0_ffn_kernel, L0_ffn_input_scale, L0_ffn_kernel_scale, L0_ffn_bias))
    x = x + s * g
    xn = _layernorm(x, axis=-1)
    s = _L1_attn_ref(xn, L1_attn_Wq, L1_attn_bq, L1_attn_Wk, L1_attn_bk, L1_attn_Wv, L1_attn_bv, L1_attn_Wa, L1_attn_ba, L1_attn_Wb, L1_attn_bb, L1_attn_Wg, L1_attn_bg, L1_attn_Wo, L1_attn_bo)
    g = _silu(_L1_ffn_ref(xn, L1_ffn_q_w, L1_ffn_q_b, L1_ffn_k_w, L1_ffn_k_b, L1_ffn_v_w, L1_ffn_v_b, L1_ffn_o_w, L1_ffn_o_b, L1_ffn_router_w, L1_ffn_router_b, L1_ffn_w1, L1_ffn_b1, L1_ffn_w2, L1_ffn_b2))
    x = x + s * g
    return x

_drawn_inputs = setup_inputs


def setup_inputs(seed=0):
    import zlib

    import numpy as np

    out = dict(_drawn_inputs(seed))
    spreads = {'L0_ffn_bias': (0.0, 0.1),
     'L1_attn_bq': (0.0, 0.539),
     'L1_attn_bk': (0.0, 0.537),
     'L1_attn_bv': (0.0, 0.544),
     'L1_attn_bg': (0.0, 0.8),
     'L1_attn_bo': (0.0, 0.1),
     'L1_ffn_q_b': (0.0, 0.8),
     'L1_ffn_k_b': (0.0, 2.0),
     'L1_ffn_v_b': (0.0, 0.8),
     'L1_ffn_o_b': (0.0, 0.8),
     'L1_ffn_router_b': (0.0, 0.8),
     'L1_ffn_b1': (0.0, 0.8),
     'L1_ffn_b2': (0.0, 2.0)}
    factors = {'L0_attn_D_skip': 3.033,
     'L0_attn_v_th': 8.0,
     'L1_ffn_q_w': 8.0,
     'L1_ffn_k_w': 8.0,
     'L1_ffn_v_w': 8.0,
     'L1_ffn_o_w': 8.0,
     'L1_ffn_router_w': 8.0,
     'L1_ffn_w1': 8.0,
     'L1_ffn_w2': 8.0}
    for name, (base, spread) in spreads.items():
        noise = np.random.default_rng([zlib.crc32(name.encode()), seed]).standard_normal(out[name].shape)
        drawn = base * np.exp(spread * noise) if base else spread * noise
        out[name] = jnp.asarray(drawn.astype(out[name].dtype))
    for name, factor in factors.items():
        out[name] = (out[name] * factor).astype(out[name].dtype)
    return out
```

```python
from contextlib import ExitStack

import numpy as np
import concourse.bass as bass
from concourse import mybir

F32 = mybir.dt.float32
F32R = mybir.dt.float32r
BF16 = mybir.dt.bfloat16
I32 = mybir.dt.int32
U32 = mybir.dt.uint32
ALU = mybir.AluOpType
ACT = mybir.ActivationFunctionType
AX = mybir.AxisListType

B, T, D = 8, 1024, 256
N = B * T
P = 128
H = D // P
S = 16
TILE = 512
SUB = TILE // P
NT = N // TILE
NP = N // P
C = 128
NH, HD = 16, 8
E, TOPK, FF = 8, 2, 512
EPS = 1e-5
FP8_MAX_TIE = 464.0

LOG_A, LOG_G, BETA, EXP_G, NEG_EXP_G, TO_END_BETA, EXP_END = range(7)
NDEC = 7

SCRATCH = {
    "dec": ([P, NP, 7], "float32"),
    "xn0": ([N, D], "float32"), "x_t": ([H, P, N], "float32"), "z_t": ([H, P, N], "float32"),
    "dt_t": ([H, P, N], "float32"), "u_t": ([H, P, N], "float32"), "xq_t": ([H, P, N], "bfloat16"),
    "bc": ([3, 2 * S, N], "bfloat16"), "y_t": ([H, P, N], "float32"), "xmax": ([P, NP], "float32"),
    "x1": ([N, D], "float32"), "xn1": ([N, D], "float32"),
    "qd": ([N, C], "float32"), "kd": ([N, C], "float32"), "vd": ([N, C], "float32"),
    "ab": ([P, NP, 2], "float32"), "gate_t": ([C, N], "float32"),
    "qs": ([3, P, N], "bfloat16"), "ks": ([3, P, N], "bfloat16"), "vf": ([N, P], "float32"),
    "inv": ([NP, P, P], "float32"), "dm": ([NP, P, P], "float32"), "kt": ([NP, P, P], "float32"),
    "qt": ([NP, P, P], "float32"), "qgt": ([NP, P, P], "float32"),
    "s1": ([N, D], "float32"), "ao": ([2, P, N], "float32"),
}


class Chain:

    def __init__(self, sem, per):
        self.sem, self.per, self.base, self.n = sem, per, 0, 0

    def begin(self, i):
        self.base, self.n = i * self.per, 0

    def end(self):
        assert self.n == self.per, (self.n, self.per)

    def link(self, eng, ins):
        self.mark(ins)
        self.wait(eng)

    def mark(self, ins):
        self.n += 1
        ins.then_inc(self.sem, 1)

    def wait(self, eng):
        eng.wait_ge(self.sem, self.base + self.n)


def pairs(eng, count):
    with eng.Fori(0, count // 2) as turn:
        for par in range(2):
            yield turn * 2 + par, par


def load_ahead(sp, count, load, done, per=1):
    load(0, 0)
    if count > 2:
        with sp.Fori(0, count // 2 - 1) as turn:
            i = turn * 2
            sp.wait_ge(done, i * per)
            load(i + 1, 1)
            sp.wait_ge(done, i * per + per)
            load(i + 2, 0)
    sp.wait_ge(done, (count - 2) * per)
    load(count - 1, 1)


class Memory:

    def __init__(self, nc, ctx, phase):
        self.nc, self.ctx, self.phase = nc, ctx, phase
        self.settled = self.sem("settled")

    def settle(self, eng):
        eng.sem_inc(self.settled, 1)

    def sb(self, name, shape, dt=F32):
        return self.ctx.enter_context(self.nc.sbuf_tensor(f"{self.phase}_{name}", shape, dt))

    def ps(self, name, shape, dt=F32):
        return self.ctx.enter_context(self.nc.psum_tensor(f"{self.phase}_{name}", shape, dt))

    def sem(self, name):
        return self.nc.alloc_semaphore(name=f"{self.phase}_{name}")


def halves(ap):
    return ap.rearrange("(h p) n -> p h n", p=P)


def column(ap):
    return ap.rearrange("(h p) -> p h", p=P)


def spread(ap, n):
    return ap.rearrange("(a n) -> a n", a=1).to_broadcast([P, n])


def identity(nc, eng, ident, sem):
    eng.memset(ident[:], 0.0).then_inc(sem, 1)
    eng.wait_ge(sem, 1)
    eng.affine_select(out=ident[:], in_=ident[:], compare_op=ALU.not_equal, fill=1.0, base=0,
                      pattern=[[-1, P]], channel_multiplier=1).then_inc(sem, 1)


def ssm_inputs(nc, A):
    with ExitStack() as ctx:
        m = Memory(nc, ctx, "si")
        wxz, wdt, wbc = m.sb("wxz", [P, H, 2 * D]), m.sb("wdt", [P, H, D]), m.sb("wbc", [P, H, 2 * S])
        bdt, sin, rsin = m.sb("bdt", [P, H]), m.sb("sin", [P, 1]), m.sb("rsin", [P, 1])
        ident = m.sb("ident", [P, P])
        x = [m.sb(f"x{k}", [P, SUB, D]) for k in range(2)]
        xn = m.sb("xn", [P, SUB, D])
        stats, mv = m.sb("stats", [P, SUB, 6]), m.sb("mv", [P, SUB, 2])
        ve, half, rstd = m.sb("ve", [P, SUB]), m.sb("half", [P, SUB]), m.sb("rstd", [P, SUB])
        xmax = m.sb("xmax", [P, NP])
        xnT, xb = m.sb("xnT", [P, H, TILE]), m.sb("xb", [P, H, TILE], BF16)
        xT, zT = m.sb("xT", [P, H, TILE]), m.sb("zT", [P, H, TILE])
        vb, mag, soft = m.sb("vb", [P, H, TILE]), m.sb("mag", [P, H, TILE]), m.sb("soft", [P, H, TILE])
        dtT, uT = m.sb("dtT", [P, H, TILE]), m.sb("uT", [P, H, TILE])
        v8, e8, r8 = m.sb("v8", [P, H, TILE]), m.sb("e8", [P, H, TILE]), m.sb("r8", [P, H, TILE])
        xq = m.sb("xq", [P, H, TILE], BF16)
        b_part = m.sb("b_part", [2 * S, 3, TILE], BF16)
        b_rest = m.sb("b_rest", [2 * S, 2, TILE])
        psT, psX, psZ = m.ps("psT", [P, H, TILE]), m.ps("psX", [P, H, TILE]), m.ps("psZ", [P, H, TILE])
        psD = m.ps("psD", [P, H, TILE])

        weights, x_loaded = m.sem("weights"), m.sem("x_loaded")
        ident_made, consts = m.sem("ident_made"), m.sem("consts")
        var_ready, rstd_ready, xn_ready, xT_psum = m.sem("var"), m.sem("rstd"), m.sem("xn"), m.sem("xT_psum")
        xnT_ready, xb_ready = m.sem("xnT"), m.sem("xb")
        x_psum, z_psum, bc_psum, dt_psum = m.sem("x_psum"), m.sem("z_psum"), m.sem("bc_psum"), m.sem("dt_psum")
        x_ready, z_ready, bc_ready = m.sem("x_ready"), m.sem("z_ready"), m.sem("bc_ready")
        soft_ready, vb_ready, dt_ready, u_ready = m.sem("soft"), m.sem("vb"), m.sem("dt_ready"), m.sem("u_ready")
        v8_ready, e8_ready, xq_ready = m.sem("v8"), m.sem("e8"), m.sem("xq_ready")
        xn_st, x_st, z_st, bc_st, dt_st, u_st, xq_st = (m.sem(f"{n}_st") for n in ("xn", "x", "z", "bc", "dt", "u", "xq"))
        e8_and, rsin_ready = m.sem("e8_and"), m.sem("rsin_ready")
        max_st, max_ready = m.sem("max_st"), m.sem("max_ready")
        act_own, dve_own, pool_own = m.sem("act_own"), m.sem("dve_own"), m.sem("pool_own")
        x_in = A["x"].rearrange("(i s p) d -> i p s d", p=P, s=SUB)
        xn_out = A["xn0"].rearrange("(i s p) d -> i p s d", p=P, s=SUB)

        def tile(name, i):
            return A[name].rearrange("h p (i t) -> i p h t", t=TILE)[i, :, :, :]

        with nc.Block() as block:
            @block.sync
            def _(sp):
                sp.dma_start(wxz[:], halves(A["w_xz"])).then_inc(weights, 16)
                sp.dma_start(wdt[:], halves(A["w_dt"])).then_inc(weights, 16)
                sp.dma_start(wbc[:], halves(A["w_bc"])).then_inc(weights, 16)
                sp.dma_start(bdt[:], column(A["b_dt"])).then_inc(weights, 16)
                sp.dma_start(sin[:], spread(A["s_in"], 1)).then_inc(weights, 16)
                sp.dma_start(x[0][:], x_in[0, :, :, :]).then_inc(x_loaded, 16)
                for i, par in pairs(sp, NT):
                    sp.wait_ge(x_loaded, 16 * i + 16)
                    m.settle(sp)
                    sp.wait_ge(xn_ready, i)
                    m.settle(sp)
                    if par == 0:
                        sp.dma_start(x[1][:], x_in[i + 1, :, :, :]).then_inc(x_loaded, 16)
                    else:
                        sp.dma_start(x[0][:], x_in[(i + 1) % NT, :, :, :]).then_inc(x_loaded, 16)
                    sp.wait_ge(xn_ready, i + 1)
                    m.settle(sp)
                    sp.dma_start(xn_out[i, :, :, :], xn[:]).then_inc(xn_st, 16)
                    sp.wait_ge(x_ready, i + 1)
                    m.settle(sp)
                    sp.dma_start(tile("x_t", i), xT[:]).then_inc(x_st, 16)
                    sp.wait_ge(z_ready, i + 1)
                    m.settle(sp)
                    sp.dma_start(tile("z_t", i), zT[:]).then_inc(z_st, 16)
                    sp.wait_ge(bc_ready, i + 1)
                    m.settle(sp)
                    sp.dma_start(A["bc"].rearrange("k r (i t) -> i r k t", t=TILE)[i, :, :, :], b_part[:]).then_inc(bc_st, 16)
                    sp.wait_ge(dt_ready, i + 1)
                    m.settle(sp)
                    sp.dma_start(tile("dt_t", i), dtT[:]).then_inc(dt_st, 16)
                    sp.wait_ge(u_ready, i + 1)
                    m.settle(sp)
                    sp.dma_start(tile("u_t", i), uT[:]).then_inc(u_st, 16)
                    sp.wait_ge(xq_ready, i + 1)
                    m.settle(sp)
                    sp.dma_start(tile("xq_t", i), xq[:]).then_inc(xq_st, 16)
                sp.wait_ge(max_ready, NT)
                sp.dma_start(A["xmax"], xmax[:]).then_inc(max_st, 16)
                sp.wait_ge(x_loaded, 16 * (NT + 1))
                for sem in (xn_st, x_st, z_st, bc_st, dt_st, u_st, xq_st):
                    sp.wait_ge(sem, 16 * NT)
                    m.settle(sp)
                sp.wait_ge(max_st, 16)

            @block.gpsimd
            def _(pool):
                identity(nc, pool, ident, ident_made)
                pool.memset(half[:], -0.5).then_inc(consts, 1)
                pool.wait_ge(consts, 1)
                for i, par in pairs(pool, NT):
                    pool.wait_ge(var_ready, i + 1)
                    pool.wait_ge(xn_ready, i)
                    m.settle(pool)
                    pool.tensor_scalar_add(ve[:], mv[:, :, 1], EPS).then_inc(pool_own, 1)
                    pool.wait_ge(pool_own, 2 * i + 1)
                    pool.tensor_tensor(rstd[:], ve[:], half[:], ALU.pow).then_inc(rstd_ready, 1)
                    pool.wait_ge(e8_ready, i + 1)
                    pool.wait_ge(xq_st, 16 * i)
                    pool.tensor_tensor(r8[:], v8[:], e8[:], ALU.add).then_inc(pool_own, 1)
                    pool.wait_ge(pool_own, 2 * i + 2)
                    pool.tensor_tensor(xq[:], r8[:], e8[:], ALU.subtract).then_inc(xq_ready, 1)

            @block.vector
            def _(dve):
                own = Chain(dve_own, 14)
                dve.wait_ge(weights, 80)
                dve.reciprocal(rsin[:], sin[:]).then_inc(rsin_ready, 1)
                for i, par in pairs(dve, NT):
                    own.begin(i)
                    dve.wait_ge(x_loaded, 16 * i + 16)
                    for s in range(SUB):
                        own.mark(dve.bn_stats(stats[:, s, :], x[par][:, s, :]))
                    own.wait(dve)
                    dve.wait_ge(rstd_ready, i)
                    for s in range(SUB):
                        m.settle(dve)
                        ins = dve.bn_aggr(mv[:, s, :], stats[:, s, :])
                        if s < SUB - 1:
                            own.mark(ins)
                        else:
                            ins.then_inc(var_ready, 1)
                    own.wait(dve)
                    dve.wait_ge(rstd_ready, i + 1)
                    dve.wait_ge(xn_st, 16 * i)
                    dve.wait_ge(xT_psum, i)
                    for s in range(SUB):
                        ins = dve.tensor_scalar(xn[:, s, :], x[par][:, s, :], mv[:, s, 0:1], rstd[:, s:s + 1],
                                                ALU.subtract, ALU.mult)
                        if s < SUB - 1:
                            own.mark(ins)
                        else:
                            ins.then_inc(xn_ready, 1)
                    own.wait(dve)
                    dve.wait_ge(xn_ready, i + 1)
                    dve.tensor_reduce(xmax[:, bass.ds(i * SUB, SUB)], xn[:], AX.X, ALU.max,
                                      apply_absolute_value=True).then_inc(max_ready, 1)
                    dve.wait_ge(x_psum, i + 1)
                    dve.wait_ge(x_st, 16 * i)
                    dve.wait_ge(u_ready, i)
                    dve.tensor_copy(xT[:], psX[:]).then_inc(x_ready, 1)
                    dve.wait_ge(bc_psum, i + 1)
                    dve.wait_ge(bc_st, 16 * i)
                    bc = psD[0:2 * S, 0, :]
                    own.link(dve, dve.tensor_copy(b_part[:, 0, :], bc))
                    own.link(dve, dve.tensor_tensor(b_rest[:, 0, :], bc, b_part[:, 0, :], ALU.subtract))
                    own.link(dve, dve.tensor_copy(b_part[:, 1, :], b_rest[:, 0, :]))
                    own.link(dve, dve.tensor_tensor(b_rest[:, 1, :], b_rest[:, 0, :], b_part[:, 1, :], ALU.subtract))
                    dve.tensor_copy(b_part[:, 2, :], b_rest[:, 1, :]).then_inc(bc_ready, 1)
                    dve.wait_ge(v8_ready, i + 1)
                    dve.wait_ge(xq_ready, i)
                    dve.tensor_single_scalar(e8[:].bitcast(I32), v8[:].bitcast(I32), 0x7F800000,
                                             ALU.bitwise_and).then_inc(e8_and, 1)
                    dve.wait_ge(e8_and, i + 1)
                    dve.tensor_scalar(e8[:], e8[:], 2.0 ** -6, 1.5 * 2.0 ** 20, ALU.max, ALU.mult).then_inc(e8_ready, 1)
                    dve.wait_ge(soft_ready, i + 1)
                    dve.wait_ge(dt_st, 16 * i)
                    dve.scalar_tensor_tensor(out=dtT[:], in0=vb[:], scalar=0.0, in1=soft[:],
                                             op0=ALU.max, op1=ALU.add).then_inc(dt_ready, 1)
                    dve.wait_ge(dt_ready, i + 1)
                    dve.wait_ge(x_ready, i + 1)
                    dve.wait_ge(u_st, 16 * i)
                    dve.tensor_tensor(uT[:], dtT[:], xT[:], ALU.mult).then_inc(u_ready, 1)
                    own.end()

            @block.scalar
            def _(act):
                own = Chain(act_own, 2)
                act.wait_ge(weights, 80)
                act.wait_ge(rsin_ready, 1)
                for i, par in pairs(act, NT):
                    own.begin(i)
                    act.wait_ge(xT_psum, i + 1)
                    act.wait_ge(dt_psum, i)
                    act.activation(xnT[:], psT[:], ACT.Copy).then_inc(xnT_ready, 1)
                    act.wait_ge(v8_ready, i)
                    act.activation(xb[:], psT[:], ACT.Copy).then_inc(xb_ready, 1)
                    act.wait_ge(xb_ready, i + 1)
                    act.wait_ge(xq_ready, i)
                    act.activation(v8[:], xb[:], ACT.Copy, scale=rsin[:, 0:1]).then_inc(v8_ready, 1)
                    act.wait_ge(z_psum, i + 1)
                    act.wait_ge(z_st, 16 * i)
                    act.activation(zT[:], psZ[:], ACT.Copy).then_inc(z_ready, 1)
                    act.wait_ge(dt_psum, i + 1)
                    act.wait_ge(dt_ready, i)
                    for h in range(H):
                        act.activation(vb[:, h, :], psD[:, h, :], ACT.Identity, bias=bdt[:, h:h + 1]).then_inc(vb_ready, 1)
                    act.wait_ge(vb_ready, H * i + H)
                    own.link(act, act.activation(mag[:], vb[:], ACT.Abs))
                    own.link(act, act.activation(mag[:], mag[:], ACT.Exp, scale=-1.0))
                    act.activation(soft[:], mag[:], ACT.Ln, bias=1.0).then_inc(soft_ready, 1)
                    own.end()

            @block.tensor
            def _(pe):
                pe.wait_ge(ident_made, 2)
                pe.wait_ge(weights, 80)
                for i, par in pairs(pe, NT):
                    pe.wait_ge(xn_ready, i + 1)
                    pe.wait_ge(xnT_ready, i)
                    pe.wait_ge(xb_ready, i)
                    for s in range(SUB):
                        for h in range(H):
                            last = pe.transpose(psT[:, h, s * P:(s + 1) * P], xn[:, s, h * P:(h + 1) * P], ident[:])
                    last.then_inc(xT_psum, 1)
                    pe.wait_ge(xnT_ready, i + 1)

                    def project(dst, weight, src):
                        for k in range(H):
                            out = pe.matmul(dst, weight[k], src[:, k, :], start=(k == 0), stop=(k == H - 1))
                        return out

                    pe.wait_ge(x_ready, i)
                    for h in range(H):
                        last = project(psX[:, h, :], [wxz[:, k, h * P:(h + 1) * P] for k in range(H)], xnT)
                    last.then_inc(x_psum, 1)
                    pe.wait_ge(z_ready, i)
                    for h in range(H):
                        last = project(psZ[:, h, :], [wxz[:, k, D + h * P:D + (h + 1) * P] for k in range(H)], xnT)
                    last.then_inc(z_psum, 1)
                    pe.wait_ge(vb_ready, H * i)
                    project(psD[0:2 * S, 0, :], [wbc[:, k, :] for k in range(H)], xnT).then_inc(bc_psum, 1)
                    pe.wait_ge(bc_ready, i + 1)
                    pe.wait_ge(x_ready, i + 1)
                    for h in range(H):
                        last = project(psD[:, h, :], [wdt[:, k, h * P:(h + 1) * P] for k in range(H)], xT)
                    last.then_inc(dt_psum, 1)


def ssm_scan(nc, A):
    with ExitStack() as ctx:
        m = Memory(nc, ctx, "sc")
        a_neg = m.sb("a_neg", [P, H, S])
        a_exp = m.sb("a_exp", [P, H, S])
        skip = m.sb("skip", [P, H])
        ident = m.sb("ident", [P, P])
        pick = m.sb("pick", [3 * 2 * S, 2 * S, P], BF16)
        bc = [m.sb(f"bc{k}", [3 * 2 * S, T], BF16) for k in range(2)]
        dt, u, x = ([m.sb(f"{n}{k}", [P, T]) for k in range(2)] for n in ("dt", "u", "x"))
        dec, prod = ([m.sb(f"{n}{k}", [P, T]) for k in range(2)] for n in ("dec", "prod"))
        inp, state, y = m.sb("inp", [P, T]), m.sb("state", [P, T]), m.sb("y", [P, T])
        psB = [m.ps(f"psB{k}", [P, T]) for k in range(2)]
        psC, psY = m.ps("psC", [P, T]), m.ps("psY", [P, T])
        weights, ident_made, pick_made = m.sem("weights"), m.sem("ident_made"), m.sem("pick_made")
        a_made, a_exp_made = m.sem("a_made"), m.sem("a_exp_made")
        loaded = [m.sem(f"loaded{k}") for k in range(2)]
        dec_ready, b_psum, c_psum = m.sem("dec"), m.sem("b_psum"), m.sem("c_psum")
        inp_ready, state_ready, prod_ready, y_added, y_ready, y_st = (
            m.sem(n) for n in ("inp", "state", "prod", "y_added", "y_ready", "y_st"))
        UNITS = B * H
        bank = T // TILE

        def unit(name, turn, h):
            return A[name].rearrange("h p (b t) -> b h p t", t=T)[turn, h, :, :]

        with nc.Block() as block:
            @block.sync
            def _(sp):
                with nc.allow_non_contiguous_dma(reason="small"):
                    sp.dma_start(a_exp[:], A["a_log"].rearrange("(h p) n -> p h n", p=P)).then_inc(weights, 16)
                    sp.dma_start(skip[:], column(A["d_skip"])).then_inc(weights, 16)

                def load(b, h):
                    parts = A["bc"].rearrange("k r (b t) -> b k r t", t=T)[b, :, :, :]
                    sp.dma_start(bc[h][:], parts.rearrange("k r t -> (k r) t")).then_inc(loaded[h], 16)
                    sp.dma_start(dt[h][:], unit("dt_t", b, h)).then_inc(loaded[h], 16)
                    sp.dma_start(u[h][:], unit("u_t", b, h)).then_inc(loaded[h], 16)
                    sp.dma_start(x[h][:], unit("x_t", b, h)).then_inc(loaded[h], 16)

                load(0, 0)
                with sp.Fori(0, B - 1) as b:
                    sp.wait_ge(y_ready, b * H)
                    m.settle(sp)
                    load(b, 1)
                    sp.wait_ge(y_ready, b * H + 1)
                    m.settle(sp)
                    load(b + 1, 0)
                sp.wait_ge(y_ready, (B - 1) * H)
                load(B - 1, 1)
                sp.wait_ge(y_st, 16 * UNITS)

            @block.gpsimd
            def _(pool):
                identity(nc, pool, ident, ident_made)
                pool.memset(pick[:], 0.0).then_inc(pick_made, 1)
                for k in range(3):
                    pool.wait_ge(pick_made, k + 1)
                    pool.affine_select(out=pick[:], in_=pick[:], compare_op=ALU.not_equal, fill=1.0,
                                       base=-2 * S * k, pattern=[[-1, 2 * S], [0, P]],
                                       channel_multiplier=1).then_inc(pick_made, 1)
                with pool.Fori(0, B) as b:
                    for h in range(H):
                        pool.wait_ge(y_ready, b * H + h + 1)
                        m.settle(pool)
                        pool.dma_start(unit("y_t", b, h), y[:]).then_inc(y_st, 16)

            @block.scalar
            def _(act):
                act.wait_ge(weights, 32)
                act.activation(a_neg[:], a_exp[:], ACT.Exp).then_inc(a_exp_made, 1)
                act.wait_ge(a_made, 1)
                with act.Fori(0, B) as b:
                    for h in range(H):
                        act.wait_ge(loaded[h], 64 * b + 64)
                        for n in range(S):
                            at = (b * H + h) * S + n
                            if n >= 2 or h > 0:
                                act.wait_ge(state_ready, at - 1)
                            else:
                                act.wait_ge(state_ready, b * H * S)
                            act.activation(dec[n % 2][:], dt[h][:], ACT.Exp,
                                           scale=a_exp[:, h, n:n + 1]).then_inc(dec_ready, 1)

            @block.tensor
            def _(pe):
                pe.wait_ge(ident_made, 2)
                pe.wait_ge(pick_made, 4)

                def broadcast(dst, h, row):
                    for k in range(bank):
                        out = pe.matmul(dst[:, k * TILE:(k + 1) * TILE], pick[:, row, :],
                                        bc[h][:, k * TILE:(k + 1) * TILE], start=True, stop=True)
                    return out

                def add(b, h, n):
                    at = (b * H + h) * S + n
                    pe.wait_ge(prod_ready, at + 1)
                    if n == 0:
                        pe.wait_ge(y_ready, b * H + h)
                    for k in range(bank):
                        out = pe.matmul(psY[:, k * TILE:(k + 1) * TILE], ident[:],
                                        prod[n % 2][:, k * TILE:(k + 1) * TILE], start=(n == 0), stop=(n == S - 1))
                    out.then_inc(y_added, 1)

                with pe.Fori(0, B) as b:
                    for h in range(H):
                        pe.wait_ge(loaded[h], 64 * b + 64)
                        for n in range(S):
                            at = (b * H + h) * S + n
                            if n >= 2 or h > 0:
                                pe.wait_ge(inp_ready, at - 1)
                            else:
                                pe.wait_ge(inp_ready, b * H * S)
                            broadcast(psB[n % 2], h, n).then_inc(b_psum, 1)
                            if n > 0:
                                add(b, h, n - 1)
                            else:
                                pe.wait_ge(prod_ready, at)
                            broadcast(psC, h, S + n).then_inc(c_psum, 1)
                        add(b, h, S - 1)

            @block.vector
            def _(dve):
                dve.wait_ge(a_exp_made, 1)
                dve.tensor_scalar(a_exp[:], a_neg[:], -1.0, None, ALU.mult).then_inc(a_made, 1)
                with dve.Fori(0, B) as b:
                    for h in range(H):
                        dve.wait_ge(loaded[h], 64 * b + 64)
                        for n in range(S):
                            at = (b * H + h) * S + n
                            dve.wait_ge(b_psum, at + 1)
                            dve.wait_ge(state_ready, at)
                            dve.tensor_tensor(inp[:], u[h][:], psB[n % 2][:], ALU.mult).then_inc(inp_ready, 1)
                            dve.wait_ge(inp_ready, at + 1)
                            dve.wait_ge(dec_ready, at + 1)
                            dve.wait_ge(prod_ready, at)
                            dve.tensor_tensor_scan(state[:], dec[n % 2][:], inp[:], 0.0, ALU.mult, ALU.add).then_inc(state_ready, 1)
                            dve.wait_ge(state_ready, at + 1)
                            dve.wait_ge(c_psum, at + 1)
                            if n >= 2 or h > 0:
                                dve.wait_ge(y_added, at - 1)
                            else:
                                dve.wait_ge(y_added, b * H * S)
                            dve.tensor_tensor(prod[n % 2][:], state[:], psC[:], ALU.mult).then_inc(prod_ready, 1)
                        dve.wait_ge(y_added, (b * H + h) * S + S)
                        dve.wait_ge(y_st, 16 * (b * H + h))
                        dve.scalar_tensor_tensor(out=y[:], in0=x[h][:], scalar=skip[:, h:h + 1], in1=psY[:],
                                                 op0=ALU.mult, op1=ALU.add).then_inc(y_ready, 1)


def ssm_output(nc, A):
    with ExitStack() as ctx:
        m = Memory(nc, ctx, "so")
        wout, kern, kq = m.sb("wout", [P, H, D]), m.sb("kern", [P, H, D], BF16), m.sb("kq", [P, H, D], BF16)
        kv, ke, kr = m.sb("kv", [P, H, D]), m.sb("ke", [P, H, D]), m.sb("kr", [P, H, D])
        vth, vbias = m.sb("vth", [P, H]), m.sb("vbias", [P, H])
        bias = m.sb("bias", [P, D], BF16)
        scales, rscale, both = m.sb("scales", [P, 2]), m.sb("rscale", [P, 2]), m.sb("both", [P, 1])
        xmax, per_tok, bad = m.sb("xmax", [P, NP]), m.sb("per_tok", [P, NP]), m.sb("bad", [P, NP])
        tok = m.sb("tok", [P, SUB])
        y, z, xq = ([m.sb(f"{n}{k}", [P, H, TILE], t) for k in range(2)] for n, t in (("y", F32), ("z", F32), ("xq", BF16)))
        x, xn = ([m.sb(f"{n}{k}", [P, SUB, D]) for k in range(2)] for n in ("x", "xn"))
        spike, open_ = m.sb("spike", [P, H, TILE]), m.sb("open", [P, H, TILE])
        ysp, zsp, a = m.sb("ysp", [P, H, TILE]), m.sb("zsp", [P, H, TILE]), [m.sb(f"a{k}", [P, H, TILE]) for k in range(2)]
        g0, g1 = m.sb("g0", [P, SUB, D], BF16), m.sb("g1", [P, SUB, D], BF16)
        gs, gden, grec, g = (m.sb(n, [P, SUB, D], BF16) for n in ("gs", "gden", "grec", "g"))
        s, sg = m.sb("s", [P, SUB, D]), m.sb("sg", [P, SUB, D])
        x1 = [m.sb(f"x1{k}", [P, SUB, D]) for k in range(2)]
        psO = [m.ps(f"psO{k}", [P, SUB, D]) for k in range(2)]
        psG = [m.ps(f"psG{k}", [P, SUB, D]) for k in range(2)]
        weights, loaded = m.sem("weights"), [m.sem(f"loaded{k}") for k in range(2)]
        prep, kq_ready, tok_ready = m.sem("prep"), m.sem("kq"), m.sem("tok_ready")
        vbias_ready = m.sem("vbias")
        spike_ready, open_ready, a_ready, o_psum, g_psum = (m.sem(n) for n in ("spike", "open", "a", "o_psum", "g_psum"))
        g0_ready, g1_ready, gs_ready, x1_ready = (m.sem(n) for n in ("g0", "g1", "gs", "x1_ready"))
        x1_st, gden_ready, grec_ready = m.sem("x1_st"), m.sem("gden"), m.sem("grec")
        step, dve_own, ysp_ready, zsp_ready = m.sem("step"), m.sem("dve_own"), m.sem("ysp"), m.sem("zsp")

        def tile(name, i):
            return A[name].rearrange("h p (i t) -> i p h t", t=TILE)[i, :, :, :]

        def rows(name, i):
            return A[name].rearrange("(i s p) d -> i p s d", p=P, s=SUB)[i, :, :, :]

        with nc.Block() as block:
            @block.sync
            def _(sp):
                sp.dma_start(wout[:], halves(A["w_out"])).then_inc(weights, 16)
                sp.dma_start(kern[:], halves(A["kern"])).then_inc(weights, 16)
                sp.dma_start(vth[:], column(A["v_th"])).then_inc(weights, 16)
                sp.dma_start(bias[:], spread(A["bias"], D)).then_inc(weights, 16)
                sp.dma_start(scales[:, 0:1], spread(A["s_in"], 1)).then_inc(weights, 16)
                sp.dma_start(scales[:, 1:2], spread(A["s_k"], 1)).then_inc(weights, 16)
                sp.dma_start(xmax[:], A["xmax"]).then_inc(weights, 16)

                def load(i, par):
                    sp.dma_start(y[par][:], tile("y_t", i)).then_inc(loaded[par], 16)
                    sp.dma_start(z[par][:], tile("z_t", i)).then_inc(loaded[par], 16)
                    sp.dma_start(xq[par][:], tile("xq_t", i)).then_inc(loaded[par], 16)
                    sp.dma_start(x[par][:], rows("x", i)).then_inc(loaded[par], 16)
                    sp.dma_start(xn[par][:], rows("xn0", i)).then_inc(loaded[par], 16)

                load_ahead(sp, NT, load, x1_ready)
                sp.wait_ge(x1_st, 16 * NT)

            @block.gpsimd
            def _(pool):
                for i, par in pairs(pool, NT):
                    pool.wait_ge(x1_ready, i + 1)
                    m.settle(pool)
                    pool.dma_start(rows("x1", i), x1[par][:]).then_inc(x1_st, 16)

            @block.scalar
            def _(act):
                act.wait_ge(vbias_ready, 1)
                for i, par in pairs(act, NT):
                    act.wait_ge(loaded[par], (i - par) * 40 + 80)
                    act.wait_ge(ysp_ready, i)
                    for h in range(H):
                        act.activation(spike[:, h, :], y[par][:, h, :], ACT.Tanh, bias=vbias[:, h:h + 1],
                                       scale=5.0).then_inc(spike_ready, 1)
                    act.wait_ge(zsp_ready, i)
                    act.activation(open_[:], z[par][:], ACT.Tanh, scale=0.5).then_inc(open_ready, 1)
                    act.wait_ge(g1_ready, i + 1)
                    act.activation(gs[:], g1[:], ACT.Exp, scale=-1.0).then_inc(gs_ready, 1)

            @block.tensor
            def _(pe):
                pe.wait_ge(weights, 112)
                pe.wait_ge(kq_ready, 1)
                for i, par in pairs(pe, NT):
                    pe.wait_ge(loaded[par], (i - par) * 40 + 80)
                    pe.wait_ge(x1_ready, i)
                    for k in range(SUB):
                        for h in range(H):
                            last = pe.matmul(psG[par][:, k, :], xq[par][:, h, k * P:(k + 1) * P], kq[:, h, :],
                                             start=(h == 0), stop=(h == H - 1))
                    last.then_inc(g_psum, 1)
                    pe.wait_ge(a_ready, i + 1)
                    for k in range(SUB):
                        for h in range(H):
                            last = pe.matmul(psO[par][:, k, :], a[par][:, h, k * P:(k + 1) * P], wout[:, h, :],
                                             start=(h == 0), stop=(h == H - 1))
                    last.then_inc(o_psum, 1)

            @block.vector
            def _(dve):
                dve.wait_ge(weights, 112)
                own = Chain(dve_own, 14)
                own.begin(0)
                own.link(dve, dve.reciprocal(rscale[:], scales[:]))
                own.link(dve, dve.tensor_scalar(kv[:], kern[:], rscale[:, 1:2], None, ALU.mult))
                own.link(dve, dve.tensor_single_scalar(ke[:].bitcast(I32), kv[:].bitcast(I32), 0x7F800000, ALU.bitwise_and))
                own.link(dve, dve.tensor_scalar(ke[:], ke[:], 2.0 ** -6, 1.5 * 2.0 ** 20, ALU.max, ALU.mult))
                own.link(dve, dve.tensor_tensor(kr[:], kv[:], ke[:], ALU.add))
                own.link(dve, dve.tensor_tensor(kr[:], kr[:], ke[:], ALU.subtract))
                own.link(dve, dve.tensor_tensor(kv[:], kv[:], kv[:], ALU.mult))
                own.link(dve, dve.tensor_scalar(kv[:], kv[:], FP8_MAX_TIE ** 2, 3e38, ALU.is_gt, ALU.mult))
                own.link(dve, dve.tensor_scalar(kv[:], kv[:], 3e38, 0.0, ALU.mult, ALU.mult))
                dve.tensor_tensor(kq[:], kr[:], kv[:], ALU.add).then_inc(kq_ready, 1)
                own.link(dve, dve.tensor_scalar(vth[:], vth[:], 0.1, -5.0, ALU.max, ALU.mult))
                dve.tensor_copy(vbias[:], vth[:]).then_inc(vbias_ready, 1)
                own.link(dve, dve.tensor_tensor(both[:], scales[:, 0:1], scales[:, 1:2], ALU.mult))
                own.link(dve, dve.tensor_scalar(bad[:], xmax[:], rscale[:, 0:1], None, ALU.mult))
                own.link(dve, dve.tensor_tensor(bad[:], bad[:], bad[:], ALU.mult))
                own.link(dve, dve.tensor_scalar(bad[:], bad[:], FP8_MAX_TIE ** 2, 3e38, ALU.is_gt, ALU.mult))
                own.n = own.per
                dve.tensor_scalar(bad[:], bad[:], 3e38, 0.0, ALU.mult, ALU.mult).then_inc(prep, 1)
                dve.wait_ge(prep, 1)
                dve.tensor_scalar(per_tok[:], bad[:], both[:, 0:1], None, ALU.add).then_inc(prep, 1)
                dve.wait_ge(prep, 2)
                for i, par in pairs(dve, NT):
                    dve.tensor_copy(tok[:], per_tok[:, bass.ds(i * SUB, SUB)]).then_inc(tok_ready, 1)
                    dve.wait_ge(loaded[par], (i - par) * 40 + 80)
                    dve.wait_ge(spike_ready, H * i + H)
                    dve.scalar_tensor_tensor(ysp[:], spike[:], 1.0, y[par][:], ALU.add, ALU.mult).then_inc(ysp_ready, 1)
                    dve.wait_ge(open_ready, i + 1)
                    dve.scalar_tensor_tensor(zsp[:], open_[:], 1.0, z[par][:], ALU.add, ALU.mult).then_inc(zsp_ready, 1)
                    dve.wait_ge(zsp_ready, i + 1)
                    dve.wait_ge(ysp_ready, i + 1)
                    dve.wait_ge(o_psum, i)
                    dve.scalar_tensor_tensor(a[par][:], ysp[:], 0.25, zsp[:], ALU.mult, ALU.mult).then_inc(a_ready, 1)
                    dve.wait_ge(g_psum, i + 1)
                    dve.wait_ge(tok_ready, i + 1)
                    for k in range(SUB):
                        dve.tensor_scalar(g0[:, k, :], psG[par][:, k, :], tok[:, k:k + 1], None, ALU.mult).then_inc(g0_ready, 1)
                    dve.wait_ge(g0_ready, SUB * i + SUB)
                    dve.tensor_tensor(g1[:], g0[:], bias[:].rearrange("p (a d) -> p a d", a=1).to_broadcast([P, SUB, D]), ALU.add).then_inc(g1_ready, 1)
                    dve.wait_ge(gs_ready, i + 1)
                    dve.tensor_scalar(gden[:], gs[:], 1.0, None, ALU.add).then_inc(gden_ready, 1)
                    dve.wait_ge(gden_ready, i + 1)
                    with nc.allow_low_precision(reason="the reference rounds to bfloat16 here"):
                        dve.reciprocal(grec[:], gden[:]).then_inc(grec_ready, 1)
                    dve.wait_ge(grec_ready, i + 1)
                    dve.tensor_tensor(g[:], g1[:], grec[:], ALU.mult).then_inc(step, 1)
                    dve.wait_ge(o_psum, i + 1)
                    dve.tensor_tensor(s[:], psO[par][:], xn[par][:], ALU.subtract).then_inc(step, 1)
                    dve.wait_ge(step, 3 * i + 2)
                    dve.tensor_tensor(sg[:], s[:], g[:], ALU.mult).then_inc(step, 1)
                    dve.wait_ge(step, 3 * i + 3)
                    dve.wait_ge(x1_st, 16 * i)
                    dve.tensor_tensor(x1[par][:], sg[:], x[par][:], ALU.add).then_inc(x1_ready, 1)
                    dve.wait_ge(x1_ready, i + 1)


class Stages:

    def __init__(self, sem, *names):
        self.sem, self.names, self.at = sem, names, 0

    def done(self, ins, name):
        assert self.names[self.at % len(self.names)] == name, (self.names[self.at % len(self.names)], name)
        self.at += 1
        ins.then_inc(self.sem, 1)

    def wait(self, eng, turn, name):
        eng.wait_ge(self.sem, turn * len(self.names) + (self.names.index(name) + 1))

    def wait_before(self, eng, turn):
        eng.wait_ge(self.sem, turn * len(self.names))


def over_chunks(ap, n=SUB):
    return ap.rearrange("p (a d) -> p a d", a=1).to_broadcast([P, n, ap.shape[-1]])


def delta_inputs(nc, A):
    TOK = 3 * C + 2
    with ExitStack() as ctx:
        m = Memory(nc, ctx, "di")
        wtok, btok = m.sb("wtok", [P, H, TOK]), m.sb("btok", [P, TOK])
        wg, bg = m.sb("wg", [P, H, C]), m.sb("bg", [P, 1])
        fq, fk, fv = m.sb("fq", [P, H, P]), m.sb("fk", [P, H, P]), m.sb("fv", [P, H, P])
        fqb, fkb, fvb = m.sb("fqb", [P, 1]), m.sb("fkb", [P, 1]), m.sb("fvb", [P, P])
        fqs = m.sb("fqs", [P, 1])
        ident, half = m.sb("ident", [P, P]), m.sb("half", [P, SUB])
        x = [m.sb(f"x{k}", [P, SUB, D]) for k in range(2)]
        xn = [m.sb(f"xn{k}", [P, SUB, D]) for k in range(2)]
        stats, mv = m.sb("stats", [P, SUB, 6]), m.sb("mv", [P, SUB, 2])
        ve, rstd = m.sb("ve", [P, SUB]), m.sb("rstd", [P, SUB])
        xnT = [m.sb(f"xnT{k}", [P, H, TILE]) for k in range(2)]
        tok = [m.sb(f"tok{k}", [P, SUB, TOK]) for k in range(2)]
        square, ss, rk = m.sb("square", [P, C]), m.sb("ss", [P, SUB]), m.sb("rk", [P, SUB])
        khat, gate, vf = m.sb("khat", [P, SUB, C]), m.sb("gate", [P, TILE]), m.sb("vf", [P, SUB, P])
        qk, rest = m.sb("qk", [P, 2, TILE]), m.sb("rest", [P, 2, 2, TILE])
        part = m.sb("part", [P, 3, 2, TILE], BF16)
        psT, psTok = m.ps("psT", [P, H, TILE]), m.ps("psTok", [P, 2, TILE])
        psV, psG, psQ, psK = (m.ps(n, [P, TILE]) for n in ("psV", "psG", "psQ", "psK"))
        weights, fqs_ready, ident_made, half_made = (m.sem(n) for n in ("weights", "fqs", "ident", "half"))
        loaded = [m.sem(f"loaded{k}") for k in range(2)]
        xn_st, tok_st, khat_st, gate_st, vf_st, part_st = (m.sem(f"{n}_st") for n in ("xn", "tok", "khat", "gate", "vf", "part"))
        pe_at = Stages(m.sem("pe_at"), "xT", "tok01", "gate", "fq", "fk", "fv", "tok23")
        dve_own, square_done = m.sem("dve_own"), m.sem("square_done")
        dve_at = Stages(m.sem("dve_at"), "stats", "var", "xn", "tok01", "vf", "tok23", "khat")
        act_at = Stages(m.sem("act_at"), "xnT", "gate", "fq", "fk", "part0", "ss", "part1", "part2")
        pool_at = Stages(m.sem("pool_at"), "ve", "rstd", "rest0", "rk0", "rk", "rest1")

        def rows(name, i):
            return A[name].rearrange("(i s p) d -> i p s d", p=P, s=SUB)[i, :, :, :]

        with nc.Block() as block:
            @block.sync
            def _(sp):
                with nc.allow_non_contiguous_dma(reason="small"):
                    for dst, src in ((wtok[:], halves(A["w_tok"])), (btok[:], spread(A["b_tok"], TOK)),
                                     (wg[:], halves(A["w_gate"])), (bg[:], A["b_gate"].rearrange("(p a) -> p a", a=1)),
                                     (fq[:], halves(A["fq"])), (fk[:], halves(A["fk"])), (fv[:], halves(A["fv"])),
                                     (fqb[:], A["fqb"].rearrange("(p a) -> p a", a=1)),
                                     (fkb[:], A["fkb"].rearrange("(p a) -> p a", a=1)), (fvb[:], spread(A["fvb"], P))):
                        sp.dma_start(dst, src).then_inc(weights, 16)

                def load(i, par):
                    sp.dma_start(x[par][:], rows("x1", i)).then_inc(loaded[par], 16)

                load_ahead(sp, NT, load, dve_at.sem, len(dve_at.names))
                for sem, n in ((xn_st, 1), (tok_st, 3), (khat_st, 1), (gate_st, 1), (vf_st, 1), (part_st, 2)):
                    sp.wait_ge(sem, 16 * n * NT)
                    m.settle(sp)

            @block.gpsimd
            def _(pool):
                identity(nc, pool, ident, ident_made)
                pool.memset(half[:], -0.5).then_inc(half_made, 1)
                pool.wait_ge(half_made, 1)
                for i, par in pairs(pool, NT):
                    dve_at.wait(pool, i, "var")
                    m.settle(pool)
                    pool_at.done(pool.tensor_scalar_add(ve[:], mv[:, :, 1], EPS), "ve")
                    pool_at.wait(pool, i, "ve")
                    pool_at.done(pool.tensor_tensor(rstd[:], ve[:], half[:], ALU.pow), "rstd")
                    dve_at.wait(pool, i, "xn")
                    m.settle(pool)
                    pool.dma_start(rows("xn1", i), xn[par][:]).then_inc(xn_st, 16)
                    act_at.wait(pool, i, "part0")
                    pool_at.done(pool.tensor_tensor(rest[:, 0, :, :], qk[:], part[:, 0, :, :], ALU.subtract), "rest0")
                    act_at.wait(pool, i, "ss")
                    pool_at.done(pool.tensor_tensor(rk[:], ss[:], half[:], ALU.pow), "rk0")
                    pool_at.wait(pool, i, "rk0")
                    m.settle(pool)
                    pool_at.done(pool.tensor_scalar_min(rk[:], rk[:], 1e12), "rk")
                    act_at.wait(pool, i, "part1")
                    pool_at.done(pool.tensor_tensor(rest[:, 1, :, :], rest[:, 0, :, :], part[:, 1, :, :], ALU.subtract), "rest1")
                    dve_at.wait(pool, i, "khat")
                    m.settle(pool)
                    pool.dma_start(rows("qd", i), tok[par][:, :, 0:C]).then_inc(tok_st, 16)
                    m.settle(pool)
                    pool.dma_start(rows("vd", i), tok[par][:, :, 2 * C:3 * C]).then_inc(tok_st, 16)
                    m.settle(pool)
                    pool.dma_start(A["ab"].rearrange("p (i s) c -> i p s c", s=SUB)[i, :, :, :],
                                   tok[par][:, :, 3 * C:TOK]).then_inc(tok_st, 16)
                    m.settle(pool)
                    pool.dma_start(rows("kd", i), khat[:]).then_inc(khat_st, 16)
                    m.settle(pool)
                    pool.dma_start(rows("vf", i), vf[:]).then_inc(vf_st, 16)

            @block.scalar
            def _(act):
                act.wait_ge(fqs_ready, 1)
                act.wait_ge(weights, 160)
                for i, par in pairs(act, NT):
                    pe_at.wait(act, i, "xT")
                    act_at.done(act.activation(xnT[par][:], psT[:], ACT.Copy), "xnT")
                    pe_at.wait(act, i, "gate")
                    act.wait_ge(gate_st, 16 * i)
                    act_at.done(act.activation(gate[:], psG[:], ACT.Sigmoid, bias=bg[:, 0:1]), "gate")
                    act_at.wait(act, i, "gate")
                    act.dma_start(A["gate_t"].rearrange("c (i t) -> i c t", t=TILE)[i, :, :], gate[:]).then_inc(gate_st, 16)
                    pe_at.wait(act, i, "fq")
                    pool_at.wait_before(act, i)
                    act_at.done(act.activation(qk[:, 0, :], psQ[:], ACT.Identity, bias=fqs[:, 0:1], scale=float(HD) ** -0.5), "fq")
                    pe_at.wait(act, i, "fk")
                    act_at.done(act.activation(qk[:, 1, :], psK[:], ACT.Identity, bias=fkb[:, 0:1]), "fk")
                    act_at.wait(act, i, "fk")
                    act.wait_ge(part_st, 32 * i)
                    act_at.done(act.activation(part[:, 0, :, :], qk[:], ACT.Copy), "part0")
                    dve_at.wait(act, i, "tok23")
                    for s in range(SUB):
                        if s:
                            act.wait_ge(square_done, i * (SUB - 1) + s)
                        ins = act.activation(square[:], tok[par][:, s, C:2 * C], ACT.Square, accum_out=ss[:, s:s + 1])
                        if s < SUB - 1:
                            ins.then_inc(square_done, 1)
                        else:
                            act_at.done(ins, "ss")
                    pool_at.wait(act, i, "rest0")
                    act_at.done(act.activation(part[:, 1, :, :], rest[:, 0, :, :], ACT.Copy), "part1")
                    pool_at.wait(act, i, "rest1")
                    act_at.done(act.activation(part[:, 2, :, :], rest[:, 1, :, :], ACT.Copy), "part2")
                    act_at.wait(act, i, "part2")
                    for n, name in enumerate(("qs", "ks")):
                        act.dma_start(A[name].rearrange("k p (i t) -> i p k t", t=TILE)[i, :, :, :],
                                      part[:, :, n, :]).then_inc(part_st, 16)

            @block.tensor
            def _(pe):
                pe.wait_ge(ident_made, 2)
                pe.wait_ge(weights, 160)
                for i, par in pairs(pe, NT):
                    dve_at.wait(pe, i, "xn")
                    act_at.wait_before(pe, i)
                    for s in range(SUB):
                        for h in range(H):
                            last = pe.transpose(psT[:, h, s * P:(s + 1) * P], xn[par][:, s, h * P:(h + 1) * P], ident[:])
                    pe_at.done(last, "xT")
                    act_at.wait(pe, i, "xnT")

                    def tokens(dst, weight, s):
                        for h in range(H):
                            out = pe.matmul(dst, xnT[par][:, h, s * P:(s + 1) * P], weight[:, h, :], start=(h == 0), stop=(h == H - 1))
                        return out

                    def features(dst, weight):
                        for h in range(H):
                            out = pe.matmul(dst, weight[:, h, :], xnT[par][:, h, :], start=(h == 0), stop=(h == H - 1))
                        return out

                    dve_at.wait_before(pe, i)
                    tokens(psTok[:, 0, 0:TOK], wtok, 0)
                    pe_at.done(tokens(psTok[:, 1, 0:TOK], wtok, 1), "tok01")
                    pe_at.done(features(psG[:], wg), "gate")
                    pe_at.done(features(psQ[:], fq), "fq")
                    pe_at.done(features(psK[:], fk), "fk")
                    for s in range(SUB):
                        last = tokens(psV[:, s * P:(s + 1) * P], fv, s)
                    pe_at.done(last, "fv")
                    dve_at.wait(pe, i, "tok01")
                    tokens(psTok[:, 0, 0:TOK], wtok, 2)
                    pe_at.done(tokens(psTok[:, 1, 0:TOK], wtok, 3), "tok23")

            @block.vector
            def _(dve):
                own = Chain(dve_own, 12)
                dve.wait_ge(weights, 160)
                dve.tensor_scalar(fqs[:], fqb[:], float(HD) ** -0.5, None, ALU.mult).then_inc(fqs_ready, 1)
                for i, par in pairs(dve, NT):
                    own.begin(i)
                    dve.wait_ge(loaded[par], (i - par) * 8 + 16)
                    for s in range(SUB):
                        ins = dve.bn_stats(stats[:, s, :], x[par][:, s, :])
                        own.mark(ins) if s < SUB - 1 else dve_at.done(ins, "stats")
                    own.wait(dve)
                    dve_at.wait(dve, i, "stats")
                    pool_at.wait_before(dve, i)
                    for s in range(SUB):
                        m.settle(dve)
                        ins = dve.bn_aggr(mv[:, s, :], stats[:, s, :])
                        own.mark(ins) if s < SUB - 1 else dve_at.done(ins, "var")
                    own.wait(dve)
                    dve_at.wait(dve, i, "var")
                    pool_at.wait(dve, i, "rstd")
                    dve.wait_ge(xn_st, 16 * i)
                    for s in range(SUB):
                        ins = dve.tensor_scalar(xn[par][:, s, :], x[par][:, s, :], mv[:, s, 0:1], rstd[:, s:s + 1],
                                                ALU.subtract, ALU.mult)
                        own.mark(ins) if s < SUB - 1 else dve_at.done(ins, "xn")
                    pe_at.wait(dve, i, "tok01")
                    dve.wait_ge(tok_st, 48 * i)
                    dve_at.done(dve.tensor_tensor(tok[par][:, 0:2, :], psTok[:, :, 0:TOK], over_chunks(btok[:], 2), ALU.add), "tok01")
                    pe_at.wait(dve, i, "fv")
                    dve.wait_ge(vf_st, 16 * i)
                    dve_at.done(dve.tensor_tensor(vf[:], psV[:].rearrange("p (s c) -> p s c", s=SUB), over_chunks(fvb[:]), ALU.add), "vf")
                    pe_at.wait(dve, i, "tok23")
                    dve_at.done(dve.tensor_tensor(tok[par][:, 2:4, :], psTok[:, :, 0:TOK], over_chunks(btok[:], 2), ALU.add), "tok23")
                    pool_at.wait(dve, i, "rk")
                    dve.wait_ge(khat_st, 16 * i)
                    for s in range(SUB):
                        ins = dve.tensor_scalar(khat[:, s, :], tok[par][:, s, C:2 * C], rk[:, s:s + 1], None, ALU.mult)
                        own.mark(ins) if s < SUB - 1 else dve_at.done(ins, "khat")
                    own.end()
                    own.wait(dve)


def delta_invert(nc, A):
    with ExitStack() as ctx:
        m = Memory(nc, ctx, "dv")
        ident, ones, tri, strict = (m.sb(n, [P, P]) for n in ("ident", "ones", "tri", "strict"))
        same = [m.sb(f"same{w}", [P, P]) for w in (16, 32, 64)]
        ring = [m.sb(f"ring{k}", [P, P]) for k in range(3)]
        ab = m.sb("ab", [P, NP, 2])
        mag, soft, la, be = (m.sb(n, [P, NP]) for n in ("mag", "soft", "la", "be"))
        g, gl, diff, dw = (m.sb(n, [P, NP]) for n in ("g", "gl", "diff", "dw"))
        dec = m.sb("dec", [P, NP, NDEC])
        W = [P, SUB, P]
        two = range(2)
        kd, qd, qg, c4 = ([m.sb(f"{n}{k}", W) for k in two] for n in ("kd", "qd", "qg", "c4"))
        col = [m.sb(f"col{k}", [P, SUB, NDEC]) for k in two]
        tl, df, dd, ds, dm = ([m.sb(f"{n}{k}", W) for k in two] for n in ("tl", "df", "dd", "ds", "dm"))
        kt, qt, qgt = ([m.sb(f"{n}{k}", W) for k in two] for n in ("kt", "qt", "qgt"))
        nf, ntf, nb, ntb = ([m.sb(f"{n}{k}", W) for k in two] for n in ("nf", "ntf", "nb", "ntb"))
        nto = [[m.sb(f"nto{k}{l}", W) for l in range(3)] for k in two]
        n2, n2t, n4, n4t, n8t = ([m.sb(f"{n}{k}", W) for k in two] for n in ("n2", "n2t", "n4", "n4t", "n8t"))
        z, xt = ([m.sb(f"{n}{k}", W) for k in two] for n in ("z", "xt"))
        X = [[m.sb(f"X{k}{l}", W) for l in range(2)] for k in two]
        ps = [[m.ps(f"ps{k}{l}", W) for l in range(4)] for k in two]
        loaded = [m.sem(f"loaded{k}") for k in two]
        ab_in, masks, pre_act, pre_dve, pre_pe = (m.sem(n) for n in ("ab_in", "masks", "pre_act", "pre_dve", "pre_pe"))
        own = [m.sem(f"own{k}") for k in two]
        act_own = [m.sem(f"act_own{k}") for k in two]
        st = [m.sem(f"st{k}") for k in two]
        dec_st = m.sem("dec_st")
        pe_at = [Stages(m.sem(f"pe_at{k}"), "kT", "qT", "gbc", "gram", "qgT", "nT", "n2", "n2t", "x1", "n4", "n4t", "x2", "n8t", "x3",
                        "z0", "xt0", "y0", "z1", "xt1", "y1", "z2", "xt2", "y2") for k in two]
        act_at = [Stages(m.sem(f"act_at{k}"), "qg", "qt", "dd", "qgt", "ntf", "n2", "n4", "n8t", "z0", "z1", "z2") for k in two]
        dve_at = [Stages(m.sem(f"dve_at{k}"), "col", "tl", "kt", "df", "nf", "nb", "x0", "ntb", "n2t", "x1", "n4t", "x2", "x3",
                         "xt0", "y0", "xt1", "y1", "xt2", "y2") for k in two]
        pool_at = [Stages(m.sem(f"pool_at{k}"), "ds", "dm", "nto0", "nto1", "nto2") for k in two]

        def rows(name, i):
            return A[name].rearrange("(i s p) d -> i p s d", p=P, s=SUB)[i, :, :, :]

        def mats(name, i):
            return A[name].rearrange("(i s) p d -> i p s d", s=SUB)[i, :, :, :]

        with nc.Block() as block:
            @block.sync
            def _(sp):
                sp.dma_start(ab[:], A["ab"]).then_inc(ab_in, 16)
                with sp.Fori(0, NT // 2) as turn:
                    for par in two:
                        i = turn * 2 + par
                        dve_at[par].wait_before(sp, turn)
                        m.settle(sp)
                        pe_at[par].wait_before(sp, turn)
                        m.settle(sp)
                        act_at[par].wait_before(sp, turn)
                        m.settle(sp)
                        sp.dma_start(kd[par][:], rows("kd", i)).then_inc(loaded[par], 16)
                        sp.dma_start(qd[par][:], rows("qd", i)).then_inc(loaded[par], 16)
                for par in two:
                    sp.wait_ge(st[par], 80 * (NT // 2))
                    m.settle(sp)
                sp.wait_ge(dec_st, 16)

            @block.gpsimd
            def _(pool):
                pool.memset(ones[:], 1.0).then_inc(masks, 1)
                pool.memset(ident[:], 0.0).then_inc(masks, 1)
                for t_ in same:
                    pool.memset(t_[:], 1.0).then_inc(masks, 1)
                pool.wait_ge(masks, 5)
                pool.affine_select(out=ident[:], in_=ident[:], compare_op=ALU.not_equal, fill=1.0, base=0,
                                   pattern=[[-1, P]], channel_multiplier=1).then_inc(masks, 1)
                pool.affine_select(out=tri[:], in_=ones[:], compare_op=ALU.is_ge, fill=0.0, base=0,
                                   pattern=[[1, P]], channel_multiplier=-1).then_inc(masks, 1)
                pool.affine_select(out=strict[:], in_=ones[:], compare_op=ALU.is_ge, fill=0.0, base=-1,
                                   pattern=[[1, P]], channel_multiplier=-1).then_inc(masks, 1)
                for w, t_ in zip((16, 32, 64), same):
                    view = t_[:].rearrange("p (n w) -> p n w", w=w)
                    pool.affine_select(out=view, in_=view, compare_op=ALU.is_ge, fill=0.0, base=0,
                                       pattern=[[-w, P // w], [0, w]], channel_multiplier=1).then_inc(masks, 1)
                pool.wait_ge(masks, 11)
                for w, t_ in zip((16, 32, 64), same):
                    view = t_[:].rearrange("p (n w) -> p n w", w=w)
                    pool.affine_select(out=view, in_=view, compare_op=ALU.is_ge, fill=0.0, base=w - 1,
                                       pattern=[[w, P // w], [0, w]], channel_multiplier=-1).then_inc(masks, 1)
                pool.wait_ge(masks, 14)
                wide = [same[1], same[2], ones]
                for k in range(3):
                    pool.tensor_tensor(ring[k][:], wide[k][:], same[k][:], ALU.subtract).then_inc(masks, 1)
                pool.wait_ge(masks, 17)
                pool.wait_ge(pre_dve, 10)
                m.settle(pool)
                pool.dma_start(A["dec"], dec[:]).then_inc(dec_st, 16)
                with pool.Fori(0, NT // 2) as turn:
                    for par in two:
                        act_at[par].wait(pool, turn, "dd")
                        dve_at[par].wait_before(pool, turn)
                        pool.wait_ge(st[par], turn * 80)
                        pool_at[par].done(pool.tensor_tensor(ds[par][:], dd[par][:], over_chunks(strict[:]), ALU.mult), "ds")
                        pool_at[par].wait(pool, turn, "ds")
                        pool_at[par].done(pool.tensor_tensor(dm[par][:], ds[par][:], over_chunks(ident[:]), ALU.add), "dm")
                    for par in two:
                        act_at[par].wait(pool, turn, "ntf")
                        pe_at[par].wait_before(pool, turn)
                        for l in range(3):
                            pool_at[par].done(pool.tensor_tensor(nto[par][l][:], ntf[par][:], over_chunks(ring[l][:]), ALU.mult), f"nto{l}")
                    for par in two:
                        i = turn * 2 + par
                        act_at[par].wait(pool, turn, "qgt")
                        dve_at[par].wait(pool, turn, "kt")
                        pool_at[par].wait(pool, turn, "dm")
                        m.settle(pool)
                        pool.dma_start(mats("dm", i), dm[par][:]).then_inc(st[par], 16)
                        m.settle(pool)
                        pool.dma_start(mats("kt", i), kt[par][:]).then_inc(st[par], 16)
                        m.settle(pool)
                        pool.dma_start(mats("qt", i), qt[par][:]).then_inc(st[par], 16)
                        m.settle(pool)
                        pool.dma_start(mats("qgt", i), qgt[par][:]).then_inc(st[par], 16)
                    for par in two:
                        dve_at[par].wait(pool, turn, "y2")
                        m.settle(pool)
                        pool.dma_start(mats("inv", turn * 2 + par), X[par][0][:]).then_inc(st[par], 16)

            @block.scalar
            def _(act):
                act.wait_ge(ab_in, 16)
                act.activation(mag[:], ab[:, :, 0], ACT.Abs).then_inc(pre_act, 1)
                act.wait_ge(pre_act, 1)
                act.activation(mag[:], mag[:], ACT.Exp, scale=-1.0).then_inc(pre_act, 1)
                act.activation(be[:], ab[:, :, 1], ACT.Exp, scale=-1.0).then_inc(pre_act, 1)
                act.wait_ge(pre_act, 2)
                act.activation(soft[:], mag[:], ACT.Ln, bias=1.0).then_inc(pre_act, 1)
                act.wait_ge(pre_dve, 5)
                act.activation(dec[:, :, EXP_G], g[:], ACT.Exp).then_inc(pre_act, 1)
                act.activation(dec[:, :, EXP_END], gl[:], ACT.Exp).then_inc(pre_act, 1)
                act.activation(dw[:], diff[:], ACT.Exp).then_inc(pre_act, 1)
                with act.Fori(0, NT // 2) as turn:
                    for par in two:
                        act.wait_ge(loaded[par], turn * 32 + 32)
                        dve_at[par].wait(act, turn, "col")
                        pe_at[par].wait_before(act, turn)
                        act.wait_ge(st[par], turn * 80)
                        for s in range(SUB):
                            ins = act.activation(qg[par][:, s, :], qd[par][:, s, :], ACT.Copy, scale=col[par][:, s, EXP_G:EXP_G + 1])
                            if s < SUB - 1:
                                ins.then_inc(act_own[par], 1)
                        act.wait_ge(act_own[par], turn * (SUB - 1) + SUB - 1)
                        act_at[par].done(ins, "qg")
                    for par in two:
                        pe_at[par].wait(act, turn, "qT")
                        act_at[par].done(act.activation(qt[par][:], ps[par][1][:], ACT.Copy), "qt")
                    for par in two:
                        dve_at[par].wait(act, turn, "df")
                        pool_at[par].wait_before(act, turn)
                        act_at[par].done(act.activation(dd[par][:], df[par][:], ACT.Exp), "dd")
                    for par in two:
                        pe_at[par].wait(act, turn, "qgT")
                        act_at[par].done(act.activation(qgt[par][:], ps[par][2][:], ACT.Copy), "qgt")
                    for par in two:
                        pe_at[par].wait(act, turn, "nT")
                        dve_at[par].wait_before(act, turn)
                        act_at[par].done(act.activation(ntf[par][:], ps[par][1][:], ACT.Copy), "ntf")
                    for name, dst, bank in (("n2", n2, 0), ("n4", n4, 3), ("n8t", n8t, 1)):
                        for par in two:
                            pe_at[par].wait(act, turn, name)
                            act_at[par].done(act.activation(dst[par][:], ps[par][bank][:], ACT.Copy), name)
                    for l in range(3):
                        for par in two:
                            pe_at[par].wait(act, turn, f"z{l}")
                            act_at[par].done(act.activation(z[par][:], ps[par][3][:], ACT.Copy), f"z{l}")

            @block.tensor
            def _(pe):
                pe.wait_ge(masks, 17)
                pe.wait_ge(pre_dve, 2)
                pe.matmul(ps[0][0][:, 0, 0:NP], tri[:], la[:], start=True, stop=True).then_inc(pre_pe, 1)
                pe.matmul(ps[0][1][:, 0, 0:NP], ones[:], la[:], start=True, stop=True).then_inc(pre_pe, 1)
                pe.wait_ge(pre_dve, 5)

                def each(par, bank, left, right, name):
                    for s in range(SUB):
                        out = pe.matmul(ps[par][bank][:, s, :], left[:, s, :], right[:, s, :], start=True, stop=True)
                    pe_at[par].done(out, name)

                def turned(par, bank, src, name):
                    for s in range(SUB):
                        out = pe.transpose(ps[par][bank][:, s, :], src[:, s, :], ident[:])
                    pe_at[par].done(out, name)

                with pe.Fori(0, NT // 2) as turn:
                    for par in two:
                        pe.wait_ge(loaded[par], turn * 32 + 32)
                        dve_at[par].wait_before(pe, turn)
                        act_at[par].wait_before(pe, turn)
                        turned(par, 0, kd[par], "kT")
                        turned(par, 1, qd[par], "qT")
                        dve_at[par].wait(pe, turn, "tl")
                        pe_at[par].done(pe.matmul(ps[par][3][:], ones[:], tl[par][:], start=True, stop=True), "gbc")
                    for par in two:
                        dve_at[par].wait(pe, turn, "kt")
                        each(par, 0, kt[par], kt[par], "gram")
                        act_at[par].wait(pe, turn, "qg")
                        turned(par, 2, qg[par], "qgT")
                    for par in two:
                        dve_at[par].wait(pe, turn, "nf")
                        act_at[par].wait(pe, turn, "qt")
                        turned(par, 1, nf[par], "nT")
                    for par in two:
                        dve_at[par].wait(pe, turn, "ntb")
                        each(par, 0, ntb[par], nb[par], "n2")
                        act_at[par].wait(pe, turn, "ntf")
                        each(par, 1, nb[par], ntb[par], "n2t")
                    for par in two:
                        dve_at[par].wait(pe, turn, "n2t")
                        act_at[par].wait(pe, turn, "n2")
                        each(par, 2, n2t[par], X[par][0], "x1")
                        each(par, 3, n2t[par], n2[par], "n4")
                        each(par, 0, n2[par], n2t[par], "n4t")
                    for par in two:
                        dve_at[par].wait(pe, turn, "n4t")
                        act_at[par].wait(pe, turn, "n4")
                        each(par, 2, n4t[par], X[par][1], "x2")
                        each(par, 1, n4[par], n4t[par], "n8t")
                    for par in two:
                        act_at[par].wait(pe, turn, "n8t")
                        dve_at[par].wait(pe, turn, "x2")
                        each(par, 2, n8t[par], X[par][0], "x3")
                    for l in range(3):
                        cur = (l + 1) % 2
                        for par in two:
                            dve_at[par].wait(pe, turn, "x3" if l == 0 else f"y{l - 1}")
                            pool_at[par].wait(pe, turn, f"nto{l}")
                            if l:
                                act_at[par].wait(pe, turn, f"z{l - 1}")
                            each(par, 3, nto[par][l], X[par][cur], f"z{l}")
                            turned(par, 1, X[par][cur], f"xt{l}")
                        for par in two:
                            act_at[par].wait(pe, turn, f"z{l}")
                            dve_at[par].wait(pe, turn, f"xt{l}")
                            each(par, 2, xt[par], z[par], f"y{l}")

            @block.vector
            def _(dve):
                dve.wait_ge(pre_act, 4)
                dve.scalar_tensor_tensor(out=la[:], in0=ab[:, :, 0], scalar=0.0, in1=soft[:], op0=ALU.min,
                                         op1=ALU.subtract).then_inc(pre_dve, 1)
                dve.tensor_scalar(be[:], be[:], 1.0, None, ALU.add).then_inc(pre_dve, 1)
                dve.wait_ge(pre_pe, 2)
                dve.tensor_copy(g[:], ps[0][0][:, 0, 0:NP]).then_inc(pre_dve, 1)
                dve.tensor_copy(gl[:], ps[0][1][:, 0, 0:NP]).then_inc(pre_dve, 1)
                dve.wait_ge(pre_dve, 4)
                dve.tensor_tensor(diff[:], gl[:], g[:], ALU.subtract).then_inc(pre_dve, 1)
                dve.reciprocal(dec[:, :, BETA], be[:]).then_inc(pre_dve, 1)
                dve.tensor_copy(dec[:, :, LOG_A], la[:]).then_inc(pre_dve, 1)
                dve.tensor_copy(dec[:, :, LOG_G], g[:]).then_inc(pre_dve, 1)
                dve.wait_ge(pre_act, 7)
                dve.tensor_scalar(dec[:, :, NEG_EXP_G], dec[:, :, EXP_G], -1.0, None, ALU.mult).then_inc(pre_dve, 1)
                dve.wait_ge(pre_dve, 6)
                dve.tensor_tensor(dec[:, :, TO_END_BETA], dw[:], dec[:, :, BETA], ALU.mult).then_inc(pre_dve, 1)
                dve.wait_ge(pre_dve, 10)
                dve.wait_ge(masks, 17)
                with dve.Fori(0, NT // 2) as turn:
                    def parts(par, op, count, name):
                        for s in range(SUB):
                            ins = op(s)
                            if s < SUB - 1:
                                ins.then_inc(own[par], 1)
                        dve.wait_ge(own[par], turn * 3 * (SUB - 1) + count * (SUB - 1))
                        dve_at[par].done(ins, name)

                    for par in two:
                        act_at[par].wait_before(dve, turn)
                        dve_at[par].done(dve.tensor_copy(col[par][:], dec[:, bass.ds((turn * 2 + par) * SUB, SUB), :]), "col")
                        dve_at[par].wait(dve, turn, "col")
                        pe_at[par].wait_before(dve, turn)
                        parts(par, lambda s: dve.tensor_scalar(tl[par][:, s, :], tri[:], col[par][:, s, LOG_A:LOG_A + 1], None, ALU.mult), 1, "tl")
                    for par in two:
                        pe_at[par].wait(dve, turn, "kT")
                        dve.wait_ge(st[par], turn * 80)
                        dve_at[par].done(dve.tensor_copy(kt[par][:], ps[par][0][:]), "kt")
                    for par in two:
                        pe_at[par].wait(dve, turn, "gbc")
                        parts(par, lambda s: dve.tensor_scalar(df[par][:, s, :], ps[par][3][:, s, :], col[par][:, s, LOG_G:LOG_G + 1],
                                                               0.0, ALU.subtract, ALU.min), 2, "df")
                    for par in two:
                        pe_at[par].wait(dve, turn, "gram")
                        pool_at[par].wait(dve, turn, "ds")
                        parts(par, lambda s: dve.scalar_tensor_tensor(
                            out=nf[par][:, s, :], in0=ps[par][0][:, s, :], scalar=col[par][:, s, BETA:BETA + 1],
                            in1=ds[par][:, s, :], op0=ALU.mult, op1=ALU.mult), 3, "nf")
                        dve_at[par].wait(dve, turn, "nf")
                        dve_at[par].done(dve.tensor_tensor(nb[par][:], nf[par][:], over_chunks(same[0][:]), ALU.mult), "nb")
                        dve_at[par].wait(dve, turn, "nb")
                        dve_at[par].done(dve.tensor_tensor(X[par][0][:], over_chunks(ident[:]), nb[par][:], ALU.subtract), "x0")
                    for par in two:
                        act_at[par].wait(dve, turn, "ntf")
                        dve_at[par].done(dve.tensor_tensor(ntb[par][:], ntf[par][:], over_chunks(same[0][:]), ALU.mult), "ntb")
                    for par in two:
                        pe_at[par].wait(dve, turn, "n2t")
                        dve_at[par].done(dve.tensor_copy(n2t[par][:], ps[par][1][:]), "n2t")
                    for k, (name, bank, last) in enumerate((("x1", 2, "n4t"), ("x2", 2, None), ("x3", 2, None))):
                        for par in two:
                            pe_at[par].wait(dve, turn, name)
                            dve_at[par].wait(dve, turn, "x0" if k == 0 else f"x{k}")
                            dve_at[par].done(dve.tensor_tensor(X[par][(k + 1) % 2][:], X[par][k % 2][:], ps[par][2][:], ALU.add), name)
                            if last:
                                pe_at[par].wait(dve, turn, last)
                                dve_at[par].done(dve.tensor_copy(n4t[par][:], ps[par][0][:]), last)
                    for l in range(3):
                        cur = (l + 1) % 2
                        for par in two:
                            pe_at[par].wait(dve, turn, f"xt{l}")
                            dve_at[par].done(dve.tensor_copy(xt[par][:], ps[par][1][:]), f"xt{l}")
                        for par in two:
                            pe_at[par].wait(dve, turn, f"y{l}")
                            dve_at[par].done(dve.tensor_tensor(X[par][1 - cur][:], X[par][cur][:], ps[par][2][:], ALU.subtract), f"y{l}")


def delta_chunks(nc, A):
    G = B // SUB
    Q = 2 * G
    TURNS = T // P // 2
    with ExitStack() as ctx:
        m = Memory(nc, ctx, "dc")
        W = [P, SUB, P]
        dec, wo, bo = m.sb("dec", [P, NP, NDEC]), m.sb("wo", [P, D]), m.sb("bo", [P, D])
        names = ("kd", "vd", "kt", "qt", "qgt", "inv", "dm", "gate")
        buf = {n: [m.sb(f"{n}{q}", W) for q in range(Q)] for n in names}
        state, stateT = ([m.sb(f"{n}{g}", W) for g in range(G)] for n in ("state", "stateT"))
        col = [m.sb(f"col{k}", [P, SUB, NDEC]) for k in range(Q)]
        r, wd, wt, am, og = (m.sb(n, W) for n in ("r", "wd", "wt", "am", "og"))
        out = [m.sb(f"out{k}", [P, SUB, D]) for k in range(2)]
        psK, psW, psWT, psA, psS, psO = (m.ps(n, W) for n in ("psK", "psW", "psWT", "psA", "psS", "psO"))
        psOut = m.ps("psOut", [P, SUB, D])
        weights, zeroed = m.sem("weights"), m.sem("zeroed")
        out_st = [m.sem(f"out_st{q}") for q in range(Q)]
        loaded = [m.sem(f"loaded{q}") for q in range(Q)]
        dve_own, act_own = m.sem("dve_own"), m.sem("act_own")
        pe_at = [Stages(m.sem(f"pe_at{q}"), "ks", "w", "wt", "a", "s", "st", "o", "out") for q in range(Q)]
        dve_at = [Stages(m.sem(f"dve_at{q}"), "col", "r", "wt", "am", "s", "st", "og", "out") for q in range(Q)]
        act_at = [Stages(m.sem(f"act_at{q}"), "wd") for q in range(Q)]

        def before(at, eng, turn, q, name):
            if q:
                at[q - 1].wait(eng, turn, name)
            else:
                at[Q - 1].wait_before(eng, turn)

        def place(name, c, g):
            if name == "gate":
                return A["gate_t"].rearrange("f (b c t) -> c f b t", b=B, t=P)[c, :, g * SUB:(g + 1) * SUB, :]
            if name in ("kd", "vd", "s1"):
                return A[name].rearrange("(b c p) d -> c p b d", b=B, p=P)[c, :, g * SUB:(g + 1) * SUB, :]
            return A[name].rearrange("(b c) p d -> c p b d", b=B)[c, :, g * SUB:(g + 1) * SUB, :]

        with nc.Block() as block:
            @block.sync
            def _(sp):
                sp.dma_start(dec[:], A["dec"]).then_inc(weights, 16)
                sp.dma_start(wo[:], A["w_o"]).then_inc(weights, 16)
                sp.dma_start(bo[:], spread(A["b_o"], D)).then_inc(weights, 16)
                with sp.Fori(0, TURNS) as turn:
                    for q in range(Q):
                        dve_at[q].wait_before(sp, turn)
                        m.settle(sp)
                        pe_at[q].wait_before(sp, turn)
                        m.settle(sp)
                        for n in names:
                            sp.dma_start(buf[n][q][:], place(n, turn * 2 + q // G, q % G)).then_inc(loaded[q], 16)
                for q in range(Q):
                    sp.wait_ge(out_st[q], 16 * TURNS)
                    m.settle(sp)

            @block.gpsimd
            def _(pool):
                for t_ in state + stateT:
                    pool.memset(t_[:], 0.0).then_inc(zeroed, 1)
                with pool.Fori(0, TURNS) as turn:
                    for q in range(Q):
                        dve_at[q].wait(pool, turn, "out")
                        m.settle(pool)
                        pool.dma_start(place("s1", turn * 2 + q // G, q % G), out[q % 2][:]).then_inc(out_st[q], 16)

            @block.scalar
            def _(act):
                with act.Fori(0, TURNS) as turn:
                    for q in range(Q):
                        pe_at[q].wait(act, turn, "w")
                        dve_at[q].wait(act, turn, "col")
                        before(pe_at, act, turn, q, "st")
                        for s in range(SUB):
                            ins = act.activation(wd[:, s, :], psW[:, s, :], ACT.Copy, scale=col[q][:, s, TO_END_BETA:TO_END_BETA + 1])
                            if s < SUB - 1:
                                ins.then_inc(act_own, 1)
                        act.wait_ge(act_own, (turn * Q + q + 1) * (SUB - 1))
                        act_at[q].done(ins, "wd")

            @block.tensor
            def _(pe):
                pe.wait_ge(weights, 48)
                pe.wait_ge(zeroed, 2 * G)

                def each(dst, left, right, **flags):
                    flags = flags or dict(start=True, stop=True)
                    for s in range(SUB):
                        last = pe.matmul(dst[:, s, :], left[:, s, :], right[:, s, :], **flags)
                    return last

                with pe.Fori(0, TURNS) as turn:
                    for q in range(Q):
                        g = q % G
                        pe.wait_ge(loaded[q], turn * 128 + 128)
                        if q >= G:
                            dve_at[q - G].wait(pe, turn, "st")
                        else:
                            dve_at[q + G].wait_before(pe, turn)
                        before(dve_at, pe, turn, q, "st")
                        pe_at[q].done(each(psK, buf["kt"][q], stateT[g]), "ks")
                        dve_at[q].wait(pe, turn, "r")
                        before(act_at, pe, turn, q, "wd")
                        pe_at[q].done(each(psW, buf["inv"][q], r), "w")
                        pe_at[q].done(each(psWT, r, buf["inv"][q]), "wt")
                        dve_at[q].wait(pe, turn, "wt")
                        pe_at[q].done(each(psA, wt, buf["qt"][q]), "a")
                        act_at[q].wait(pe, turn, "wd")
                        pe_at[q].done(each(psS, wd, buf["kd"][q]), "s")
                        pe_at[q].done(each(psK, buf["kd"][q], wd), "st")
                        dve_at[q].wait(pe, turn, "am")
                        for s in range(SUB):
                            pe.matmul(psO[:, s, :], state[g][:, s, :], buf["qgt"][q][:, s, :], start=True, stop=False)
                            last = pe.matmul(psO[:, s, :], buf["kd"][q][:, s, :], am[:, s, :], start=False, stop=True)
                        pe_at[q].done(last, "o")
                        dve_at[q].wait(pe, turn, "og")
                        before(dve_at, pe, turn, q, "out") if q == 0 else None
                        for s in range(SUB):
                            last = pe.matmul(psOut[:, s, :], og[:, s, :], wo[:], start=True, stop=True)
                        pe_at[q].done(last, "out")

            @block.vector
            def _(dve):
                dve.wait_ge(weights, 48)
                dve.wait_ge(zeroed, 2 * G)
                with dve.Fori(0, TURNS) as turn:
                    for q in range(Q):
                        g = q % G
                        count = [0]

                        def parts(op, name):
                            for s in range(SUB):
                                ins = op(s)
                                if s < SUB - 1:
                                    ins.then_inc(dve_own, 1)
                                    count[0] += 1
                            dve.wait_ge(dve_own, (turn * Q + q) * 4 * (SUB - 1) + count[0])
                            dve_at[q].done(ins, name)

                        view = dec[:].rearrange("p (b c) f -> p b c f", b=B)
                        c = turn * 2 + q // G
                        act_at[q].wait_before(dve, turn)
                        dve_at[q].done(dve.tensor_copy(col[q][:].rearrange("p b (a f) -> p b a f", a=1),
                                                       view[:, g * SUB:(g + 1) * SUB, bass.ds(c, 1), :]), "col")
                        dve.wait_ge(loaded[q], turn * 128 + 128)
                        pe_at[q].wait(dve, turn, "ks")
                        dve_at[q].wait(dve, turn, "col")
                        before(pe_at, dve, turn, q, "wt")

                        def scaled(dst, src, col_at, plus, op1=ALU.add):
                            return lambda s: dve.scalar_tensor_tensor(
                                out=dst[:, s, :], in0=src[:, s, :], scalar=col[q][:, s, col_at:col_at + 1],
                                in1=plus[:, s, :], op0=ALU.mult, op1=op1)

                        parts(scaled(r, psK, NEG_EXP_G, buf["vd"][q]), "r")
                        pe_at[q].wait(dve, turn, "wt")
                        dve_at[q].done(dve.tensor_copy(wt[:], psWT[:]), "wt")
                        pe_at[q].wait(dve, turn, "a")
                        parts(scaled(am, psA, BETA, buf["dm"][q], ALU.mult), "am")
                        pe_at[q].wait(dve, turn, "o")
                        parts(scaled(state[g], state[g], EXP_END, psS), "s")
                        parts(scaled(stateT[g], stateT[g], EXP_END, psK), "st")
                        dve_at[q].done(dve.tensor_tensor(og[:], psO[:], buf["gate"][q][:], ALU.mult), "og")
                        pe_at[q].wait(dve, turn, "out")
                        if q >= 2:
                            dve.wait_ge(out_st[q - 2], turn * 16 + 16)
                        else:
                            dve.wait_ge(out_st[q + 2], turn * 16)
                        dve_at[q].done(dve.tensor_tensor(out[q % 2][:], psOut[:], over_chunks(bo[:]), ALU.add), "out")


def attention(nc, A):
    QUAD = 4
    ROWS = 9 * HD
    MAXROW = 96
    ALL = MAXROW + 3
    NQ = NH // QUAD
    KC = T // P
    NHALF = T // TILE
    with ExitStack() as ctx:
        m = Memory(nc, ctx, "at")
        q4, k4 = ([m.sb(f"{n}{j}", [ALL, QUAD, T], BF16) for j in range(NQ)] for n in ("q4", "k4"))
        vraw = [m.sb(f"vraw{j}", [P, KC, QUAD * HD]) for j in range(NQ)]
        v4 = [m.sb(f"v4{j}", [P, KC, QUAD, 32]) for j in range(NQ)]
        ident = m.sb("ident", [P, P], BF16)
        half_max = m.sb("half_max", [P, QUAD, KC, NHALF])
        top = m.sb("top", [P, QUAD * KC])
        rest = m.sb("rest", [P, 2, QUAD * KC])
        top3 = m.sb("top3", [P, 4, QUAD * KC], BF16)
        topT = m.sb("topT", [P, P], BF16)
        probs = [m.sb(f"probs{j}", [P, 2, TILE]) for j in range(2 * QUAD)]
        sums = [m.sb(f"sums{j}", [P, TILE]) for j in range(NHALF)]
        psM = [m.ps(f"psM{j}", [P, TILE]) for j in range(2)]
        psS = [m.ps(f"psS{j}", [P, 2, TILE]) for j in range(2)]
        psT, psV = m.ps("psT", [P, P]), m.ps("psV", [P, TILE])
        ident_made, ready_made = m.sem("ident_made"), m.sem("ready_made")
        loaded = [m.sem(f"loaded{j}") for j in range(NQ)]
        top_in = [m.sem(f"top_in{j}") for j in range(NQ)]
        v_ready, scored, maxed = m.sem("v_ready"), m.sem("scored"), m.sem("maxed")
        top_at = Stages(m.sem("top_at"), "top", "part0", "rest0", "part1", "rest1", "part2")
        filled, turned, topT_ready = m.sem("filled"), m.sem("turned"), m.sem("topT_ready")
        keyed, probs_ready, summed, sums_ready = m.sem("keyed"), m.sem("probs_ready"), m.sem("summed"), m.sem("sums_ready")
        sums_st = [m.sem(f"sums_st{j}") for j in range(NHALF)]
        LOADS = 2 * 9 + 1
        TILES1 = QUAD * KC * NHALF
        TILES2 = NHALF * (KC // 2) * QUAD
        GROUPS = TILES2 // QUAD
        UNITS = B * NQ

        with nc.Block() as block:
            @block.sync
            def _(sp):
                def load(b, j):
                    for name, dst, outer in (("qs", q4, True), ("ks", k4, False)):
                        for n in range(9):
                            part = n // 3 if outer else n % 3
                            src = A[name].rearrange("k (h r) (b t) -> k b r h t", r=HD, t=T)[part, b, :, j * QUAD:(j + 1) * QUAD, :]
                            sp.dma_start(dst[j][n * HD:(n + 1) * HD, :, :], src).then_inc(loaded[j], 16)
                    src = A["vf"].rearrange("(b c p) n -> b p c n", b=B, p=P)[b, :, :, j * QUAD * HD:(j + 1) * QUAD * HD]
                    sp.dma_start(vraw[j][:], src).then_inc(loaded[j], 16)

                for j in range(NQ):
                    sp.wait_ge(ready_made, 3 * j + 3)
                    m.settle(sp)
                    load(0, j)

                def sequence(b, final):
                    for j in range(NQ):
                        u = b * NQ + j
                        sp.wait_ge(topT_ready, u + 1)
                        m.settle(sp)
                        for k in range(3):
                            dst = q4[j][MAXROW + k:MAXROW + k + 1, :, :].rearrange("a h (c s) -> a (h c) s", s=P)
                            sp.dma_start(dst, topT[k * QUAD * KC:(k + 1) * QUAD * KC, :]).then_inc(top_in[j], 16)
                        for half in range(NHALF):
                            sp.wait_ge(sums_ready, u * NHALF + half + 1)
                            m.settle(sp)
                            for h in range(QUAD):
                                head = (j * QUAD + h) * HD
                                for k in range(2):
                                    dst = A["ao"].rearrange("k r (b s t) -> b k s r t", b=B, t=TILE)[b, k, half, head:head + HD, :]
                                    sp.dma_start(dst, sums[half][32 * h + HD * k:32 * h + HD * (k + 1), :]).then_inc(sums_st[half], 16)
                        if not final:
                            load(b + 1, j)

                with sp.Fori(0, B - 1) as b:
                    sequence(b, False)
                sequence(B - 1, True)
                for half in range(NHALF):
                    sp.wait_ge(sums_st[half], UNITS * QUAD * 2 * 16)
                    m.settle(sp)

            @block.gpsimd
            def _(pool):
                pool.memset(ident[:], 0.0).then_inc(ident_made, 1)
                pool.wait_ge(ident_made, 1)
                pool.affine_select(out=ident[:], in_=ident[:], compare_op=ALU.not_equal, fill=1.0, base=0,
                                   pattern=[[-1, P]], channel_multiplier=1).then_inc(ident_made, 1)
                pool.wait_ge(ident_made, 2)
                for j in range(NQ):
                    for n, (rows, value) in enumerate(((q4[j][64:96, :, :], 0.0), (k4[j][64:96, :, :], 0.0),
                                                       (k4[j][MAXROW:ALL, :, :], 1.0))):
                        pool.memset(rows, value).then_inc(ready_made, 1)
                        pool.wait_ge(ready_made, 3 * j + n + 1)
                for j in range(NQ):
                    pool.memset(v4[j][:], 0.0).then_inc(v_ready, 1)
                    pool.wait_ge(v_ready, 2 * j + 1)
                    pool.memset(v4[j][:, :, :, HD:2 * HD], 1.0).then_inc(v_ready, 1)
                    pool.wait_ge(v_ready, 2 * j + 2)
                with pool.Fori(0, B) as b:
                    for j in range(NQ):
                        pool.wait_ge(loaded[j], (b + 1) * 16 * LOADS)
                        pool.wait_ge(summed, (b * NQ + j) * GROUPS if j == 0 else (b * NQ + j) * GROUPS - GROUPS)
                        m.settle(pool)
                        pool.tensor_copy(v4[j][:, :, :, 0:HD], vraw[j][:].rearrange("p c (h r) -> p c h r", r=HD)).then_inc(v_ready, 1)

            STEPS = TILES2
            share = [TILES1 * (n + 1) // STEPS for n in range(STEPS)]

            @block.tensor
            def _(pe):
                pe.wait_ge(ident_made, 2)

                def maxima(u, j, t):
                    h, c, half = t // (KC * NHALF), t // NHALF % KC, t % NHALF
                    pe.wait_ge(maxed, u * TILES1 + t - 1) if t else pe.wait_ge(maxed, u * TILES1)
                    pe.matmul(psM[t % 2][:], q4[j][0:ROWS, h, c * P:(c + 1) * P],
                              k4[j][0:ROWS, h, half * TILE:(half + 1) * TILE], start=True, stop=True).then_inc(scored, 1)

                def turn(u):
                    top_at.wait(pe, u, "part2")
                    pe.wait_ge(topT_ready, u)
                    pe.matmul(psT[:], top3[:].rearrange("p k n -> p (k n)"), ident[:],
                              start=True, stop=True).then_inc(turned, 1)

                def second(u, j, g, h):
                    half, pair = g // (KC // 2), g % (KC // 2)
                    if g == 0 and h < 2:
                        pe.wait_ge(probs_ready, u * TILES2)
                    else:
                        pe.wait_ge(probs_ready, u * TILES2 + g * QUAD + h - 1)
                    for k in range(2):
                        c = pair * 2 + k
                        last = pe.matmul(psS[h % 2][:, k, :], k4[j][:, h, c * P:(c + 1) * P],
                                         q4[j][:, h, half * TILE:(half + 1) * TILE], start=True, stop=True)
                    last.then_inc(keyed, 1)

                def values(u, j, g, k):
                    half, pair = g // (KC // 2), g % (KC // 2)
                    c = pair * 2 + k
                    pe.wait_ge(probs_ready, u * TILES2 + (g + 1) * QUAD)
                    if c == 0:
                        pe.wait_ge(sums_ready, u * NHALF + half)
                    for h in range(QUAD):
                        last = pe.matmul(psV[32 * h:32 * h + 32, :], v4[j][:, c, h, :], probs[(g % 2) * QUAD + h][:, k, :],
                                         start=(c == 0), stop=(c == KC - 1))
                    if k == 1:
                        last.then_inc(summed, 1)

                pe.wait_ge(loaded[0], 16 * LOADS)
                for t in range(TILES1):
                    maxima(0, 0, t)
                turn(0)

                def sequence(b, final):
                    for j in range(NQ):
                        u = b * NQ + j
                        pe.wait_ge(top_in[j], b * 48 + 48)
                        pe.wait_ge(v_ready, 2 * NQ + u + 1)
                        more = not (final and j == NQ - 1)
                        nj = (j + 1) % NQ
                        if more:
                            pe.wait_ge(loaded[nj], ((b + 1) if nj else (b + 2)) * 16 * LOADS)
                        done = 0
                        for g in range(GROUPS):
                            for h in range(QUAD):
                                second(u, j, g, h)
                                while more and done < share[g * QUAD + h]:
                                    maxima(u + 1, nj, done)
                                    done += 1
                                if g and h >= 2:
                                    values(u, j, g - 1, h - 2)
                        for k in range(2):
                            values(u, j, GROUPS - 1, k)
                        if more:
                            turn(u + 1)

                with pe.Fori(0, B - 1) as b:
                    sequence(b, False)
                sequence(B - 1, True)

            @block.scalar
            def _(act):
                with act.Fori(0, B) as b:
                    for j in range(NQ):
                        u = b * NQ + j
                        act.wait_ge(turned, u + 1)
                        if j == 0:
                            act.wait_ge(top_in[NQ - 1], b * 48)
                        else:
                            act.wait_ge(top_in[j - 1], b * 48 + 48)
                        act.activation(topT[:], psT[:], ACT.Copy).then_inc(topT_ready, 1)
                        for g in range(GROUPS):
                            for h in range(QUAD):
                                act.wait_ge(keyed, u * TILES2 + g * QUAD + h + 1)
                                if h == 0:
                                    act.wait_ge(summed, u * GROUPS + g - 1 if g else u * GROUPS)
                                act.activation(probs[(g % 2) * QUAD + h][:], psS[h % 2][:], ACT.Exp).then_inc(probs_ready, 1)

            @block.vector
            def _(dve):
                def maxima(u, t):
                    h, c, half = t // (KC * NHALF), t // NHALF % KC, t % NHALF
                    dve.wait_ge(scored, u * TILES1 + t + 1)
                    dve.reduce_max(half_max[:, h, c, half:half + 1], psM[t % 2][:], AX.X).then_inc(maxed, 1)

                def minus_max(u):
                    dve.wait_ge(maxed, u * TILES1 + TILES1)
                    dve.wait_ge(turned, u)
                    top_at.done(dve.tensor_reduce(top[:], half_max[:].rearrange("p h c n -> p (h c) n"), AX.X, ALU.max, negate=True), "top")
                    top_at.wait(dve, u, "top")
                    top_at.done(dve.tensor_copy(top3[:, 0, :], top[:]), "part0")
                    top_at.wait(dve, u, "part0")
                    top_at.done(dve.tensor_tensor(rest[:, 0, :], top[:], top3[:, 0, :], ALU.subtract), "rest0")
                    top_at.wait(dve, u, "rest0")
                    top_at.done(dve.tensor_copy(top3[:, 1, :], rest[:, 0, :]), "part1")
                    top_at.wait(dve, u, "part1")
                    top_at.done(dve.tensor_tensor(rest[:, 1, :], rest[:, 0, :], top3[:, 1, :], ALU.subtract), "rest1")
                    top_at.wait(dve, u, "rest1")
                    top_at.done(dve.tensor_copy(top3[:, 2, :], rest[:, 1, :]), "part2")
                    top_at.wait(dve, u, "part2")

                def collect(u, half):
                    dve.wait_ge(summed, u * GROUPS + (half + 1) * GROUPS // NHALF)
                    dve.wait_ge(sums_st[half], u * QUAD * 2 * 16)
                    dve.tensor_copy(sums[half][:], psV[:]).then_inc(sums_ready, 1)

                dve.memset(top3[:, 3, :], 0.0).then_inc(filled, 1)
                dve.wait_ge(filled, 1)
                for t in range(TILES1):
                    maxima(0, t)
                minus_max(0)

                def sequence(b, final):
                    for j in range(NQ):
                        u = b * NQ + j
                        more = not (final and j == NQ - 1)
                        done = 0
                        for g in range(GROUPS):
                            while more and done < share[g * QUAD + QUAD - 1]:
                                maxima(u + 1, done)
                                done += 1
                            if g == GROUPS // NHALF:
                                collect(u, 0)
                        if more:
                            minus_max(u + 1)
                        collect(u, 1)

                with dve.Fori(0, B - 1) as b:
                    sequence(b, False)
                sequence(B - 1, True)


def experts(nc, A):
    TILE, SUB = 256, 2
    NT = N // TILE
    FT = FF // P
    STAGED = max(H * FF, FT * D)
    with ExitStack() as ctx:
        m = Memory(nc, ctx, "ex")
        two = range(2)
        wo, ob, wr, br = m.sb("wo", [P, D]), m.sb("ob", [P, H]), m.sb("wr", [P, H, E]), m.sb("br", [P, E])
        b1, b2 = m.sb("b1", [P, E, FT]), m.sb("b2", [E, D])
        w1 = [m.sb(f"w1{k}", [P, E, H, FF], F32R) for k in two]
        w2 = [m.sb(f"w2{k}", [P, E, FT, D], F32R) for k in two]
        ident, number = m.sb("ident", [P, P]), m.sb("number", [P, E])
        ao = [m.sb(f"ao{k}", [P, 2, TILE]) for k in two]
        x1, xn, s1 = ([m.sb(f"{n}{k}", [P, SUB, D]) for k in two] for n in ("x1", "xn", "s1"))
        rs, aon = m.sb("rs", [P, TILE]), m.sb("aon", [P, TILE])
        mla = m.sb("mla", [P, H, TILE])
        mla2 = [[m.sb(f"mla2{k}{part}", [P, H, TILE], F32R) for part in two] for k in two]
        R = [P, SUB, E]
        lg, ex, pr, top, pick0, pick1 = (m.sb(n, R) for n in ("lg", "ex", "pr", "top", "pick0", "pick1"))
        index, indexf = m.sb("index", R, U32), m.sb("indexf", R)
        comb = [m.sb(f"comb{k}", R) for k in two]
        mx, total, share = m.sb("mx", [P, SUB]), m.sb("total", [P, SUB]), m.sb("share", [P, SUB, 2])
        combT = m.sb("combT", [E, SUB, P])
        hid = [m.sb(f"hid{k}", [P, FT, TILE]) for k in two]
        hid2 = [[m.sb(f"hid2{k}{part}", [P, FT, TILE], F32R) for part in two] for k in two]
        acc = [m.sb(f"acc{k}", [P, SUB, D]) for k in two]
        gin, th, res = (m.sb(n, [P, SUB, D]) for n in ("gin", "th", "res"))
        psH = [m.ps(f"psH{k}", [P, 2, TILE]) for k in range(FT)]
        psE = [m.ps(f"psE{k}", [P, SUB, D]) for k in two]
        psM, psB = m.ps("psM", [P, H, TILE]), m.ps("psB", [P, SUB, D])
        weights, consts, split = m.sem("weights"), m.sem("consts"), m.sem("split")
        staged = [m.sem(f"staged{k}") for k in two]
        ao_loaded = [m.sem(f"ao_loaded{k}") for k in two]
        end_loaded = [m.sem(f"end_loaded{k}") for k in two]
        out_st, half1 = m.sem("out_st"), m.sem("half1")
        pe_pre = Stages(m.sem("pe_pre"), "mla", "logits", "combT", "bias")
        act_pre = Stages(m.sem("act_pre"), "mla", "ex")
        dve_pre = Stages(m.sem("dve_pre"), "rs", "aon", "head", "rest", "lg", "mx", "sub", "total", "rtotal", "pr", "top",
                         "index", "indexf", "sum2", "rsum2", "share", "pick0", "pick1", "comb", "combT", "bias")
        hid_psum, hid_ready, out_psum, added = m.sem("hid_psum"), m.sem("hid_ready"), m.sem("out_psum"), m.sem("added")
        head_ready, rest_ready = m.sem("head_ready"), m.sem("rest_ready")
        gin_ready, th_ready, res_ready, act_own, dve_own, pre_own = (
            m.sem(n) for n in ("gin", "th", "res", "act_own", "dve_own", "pre_own"))
        NSTAGED = 2 * E

        def rows(ap, i):
            return ap.rearrange("(i s p) d -> i p s d", p=P, s=SUB)[i, :, :, :]

        def flat(ap):
            return ap.rearrange("p a b -> p (a b)")

        def products(pe, out, parts, start, stop):
            for n, (a, b) in enumerate(parts):
                last = pe.matmul(out, a, b, start=start and n == 0, stop=stop and n == len(parts) - 1)
            return last

        def run(eng, step):
            step(0, 0, True, True)
            with eng.Fori(0, NT // 2 - 1) as turn:
                step(turn * 2 + 1, 1, False, True)
                step(turn * 2 + 2, 0, False, True)
            step(NT - 1, 1, False, False)

        with nc.Block() as block:
            @block.sync
            def _(sp):
                with nc.allow_non_contiguous_dma(reason="small"):
                    for dst, src in ((wo[:], A["fo"][0:P, :]), (ob[:], column(A["fob"])), (wr[:], halves(A["rw"])),
                                     (br[:], spread(A["rb"], E)), (b2[:], A["b2"]),
                                     (b1[:], A["b1"].rearrange("e (f p) -> p e f", p=P))):
                        sp.dma_start(dst, src).then_inc(weights, 16)

                def load_ao(i, par):
                    sp.dma_start(ao[par][:], A["ao"].rearrange("k p (i t) -> i p k t", t=TILE)[i, :, :, :]).then_inc(ao_loaded[par], 16)

                def load_end(i, par):
                    for name, buf in (("xn1", xn), ("x1", x1), ("s1", s1)):
                        sp.dma_start(buf[par][:], rows(A[name], i)).then_inc(end_loaded[par], 16)

                for i in two:
                    load_ao(i, i)
                    load_end(i, i)
                w1_in = A["w1"].rearrange("e (h p) f -> e p h f", p=P)
                w2_in = A["w2"].rearrange("e (f p) d -> e p f d", p=P)
                for n in range(NSTAGED):
                    if n >= 2:
                        sp.wait_ge(split, 2 * n - 2)
                    src = w1_in[n // 2, :, :, :] if n % 2 == 0 else w2_in[n // 2, :, :, :]
                    dst = flat(hid[n % 2][:]).rearrange("p (a b) -> p a b", a=src.shape[1])
                    sp.dma_start(dst, src).then_inc(staged[n % 2], 16)

                with sp.Fori(0, NT // 2 - 1) as turn:
                    for par in two:
                        i = turn * 2 + par
                        dve_pre.wait(sp, i, "aon")
                        m.settle(sp)
                        load_ao(i + 2, par)
                        sp.wait_ge(res_ready, i + 1)
                        m.settle(sp)
                        load_end(i + 2, par)
                sp.wait_ge(out_st, 16 * NT)

            @block.gpsimd
            def _(pool):
                identity(nc, pool, ident, consts)
                pool.wait_ge(consts, 2)
                pool.iota(number[:], pattern=[[1, E]], base=0, channel_multiplier=0,
                          allow_small_or_imprecise_dtypes=True).then_inc(consts, 1)
                with pool.Fori(0, NT) as i:
                    pool.wait_ge(res_ready, i + 1)
                    m.settle(pool)
                    pool.dma_start(rows(A["out"], i), res[:]).then_inc(out_st, 16)

            @block.scalar
            def _(act):
                def prepare(i, slot):
                    if slot == 3:
                        pe_pre.wait(act, i, "mla")
                        if isinstance(i, int) and i == 0:
                            pass
                        else:
                            dve_pre.wait(act, i - 1, "rest")
                            pe_pre.wait(act, i - 1, "logits")
                        act.activation(mla[:, 0, :], psM[:, 0, :], ACT.Identity, bias=ob[:, 0:1]).then_inc(act_own, 1)
                        act_pre.done(act.activation(mla[:, 1, :], psM[:, 1, :], ACT.Identity, bias=ob[:, 1:2]), "mla")
                        act.wait_ge(act_own, i + 1)
                    if slot == 5:
                        dve_pre.wait(act, i, "sub")
                        act_pre.done(act.activation(ex[:], lg[:], ACT.Exp), "ex")

                def gelu(i, e):
                    if e >= 2:
                        act.wait_ge(rest_ready, i * E + (e - 1))
                    elif isinstance(i, int) and i == 0:
                        act.wait_ge(split, 2 * NSTAGED)
                    else:
                        act.wait_ge(rest_ready, i * E + e - 1)
                    for f in range(FT):
                        act.wait_ge(hid_psum, (i * E + e) * FT + f + 1)
                        act.activation(hid[e % 2][:, f, :], psH[f][:, 0, :], ACT.Gelu,
                                       bias=b1[:, e, f:f + 1]).then_inc(hid_ready, 1)

                def finish(i):
                    act.wait_ge(gin_ready, i + 1)
                    act.activation(th[:], gin[:], ACT.Tanh, scale=0.5).then_inc(th_ready, 1)

                def step(i, par, first, more):
                    for e in range(E):
                        if e + 1 < E:
                            gelu(i, e + 1)
                        elif more:
                            gelu(i + 1, 0)
                        if e == 1 and not first:
                            finish(i - 1)
                        if more:
                            prepare(i + 1, e)

                act.wait_ge(weights, 96)
                for slot in range(E):
                    prepare(0, slot)
                gelu(0, 0)
                run(act, step)
                finish(NT - 1)

            @block.tensor
            def _(pe):
                def prepare(i, par, slot):
                    if slot == 2:
                        dve_pre.wait(pe, i, "aon")
                        for h in range(H):
                            last = pe.matmul(psM[:, h, :], wo[:, h * P:(h + 1) * P], aon[:], start=True, stop=True)
                        pe_pre.done(last, "mla")
                    if slot == 4:
                        act_pre.wait(pe, i, "mla")
                        for s in range(SUB):
                            for h in range(H):
                                last = pe.matmul(psB[:, s, 0:E], mla[:, h, s * P:(s + 1) * P], wr[:, h, :],
                                                 start=(h == 0), stop=(h == H - 1))
                        pe_pre.done(last, "logits")
                    if slot == 6:
                        dve_pre.wait(pe, i, "comb")
                        for s in range(SUB):
                            last = pe.transpose(psM[0:E, 0, s * P:(s + 1) * P], comb[par][:, s, :], ident[:])
                        pe_pre.done(last, "combT")
                    if slot == 7:
                        dve_pre.wait(pe, i, "combT")
                        for s in range(SUB):
                            last = pe.matmul(psB[:, s, :], combT[:, s, :], b2[:], start=True, stop=True)
                        pe_pre.done(last, "bias")

                def hidden(i, par, e):
                    if e == 0:
                        dve_pre.wait(pe, i, "rest")
                    for f in range(FT):
                        if e:
                            pe.wait_ge(hid_ready, i * E * FT + ((e - 1) * FT + f + 1))
                        elif not (isinstance(i, int) and i == 0):
                            pe.wait_ge(hid_ready, i * E * FT + (f + 1) - FT)
                        fs = slice(f * P, (f + 1) * P)
                        for h in range(H):
                            xh, xl = (mla2[par][k][:, h, :] for k in two)
                            wh, wl = (w1[k][:, e, h, fs] for k in two)
                            last = products(pe, psH[f][:, 0, :], ((wh, xh), (wh, xl), (wl, xh)), h == 0, h == H - 1)
                        last.then_inc(hid_psum, 1)

                def output(i, e):
                    pe.wait_ge(rest_ready, i * E + (e + 1))
                    if e >= 2:
                        pe.wait_ge(added, i * E + (e - 1))
                    elif not (isinstance(i, int) and i == 0):
                        pe.wait_ge(added, i * E + e - 1)
                    for s in range(SUB):
                        ss = slice(s * P, (s + 1) * P)
                        for f in range(FT):
                            xh, xl = (hid2[e % 2][k][:, f, ss] for k in two)
                            wh, wl = (w2[k][:, e, f, :] for k in two)
                            last = products(pe, psE[e % 2][:, s, :], ((xh, wh), (xh, wl), (xl, wh)), f == 0, f == FT - 1)
                    last.then_inc(out_psum, 1)

                def step(i, par, first, more):
                    for e in range(E):
                        if e + 1 < E:
                            hidden(i, par, e + 1)
                        elif more:
                            hidden(i + 1, 1 - par, 0)
                        if more:
                            prepare(i + 1, 1 - par, e)
                        output(i, e)

                pe.wait_ge(weights, 96)
                pe.wait_ge(consts, 3)
                for slot in range(E):
                    prepare(0, 0, slot)
                pe.wait_ge(split, 2 * NSTAGED)
                hidden(0, 0, 0)
                run(pe, step)

            @block.vector
            def _(dve):
                def divide(head, rest, whole, head_sem, rest_sem, wait):
                    head_sem(dve.tensor_copy(head, whole))
                    wait()
                    rest_sem(dve.tensor_tensor(rest, whole, head.bitcast(F32), ALU.subtract))

                def prepare(i, par, slot):
                    own = Chain(pre_own, 2 * (SUB - 1) + 4)
                    if slot == 1:
                        dve.wait_ge(ao_loaded[par], (i - par) * 8 + 16)
                        dve_pre.done(dve.reciprocal(rs[:], ao[par][:, 1, :]), "rs")
                        dve_pre.wait(dve, i, "rs")
                        dve_pre.done(dve.tensor_tensor(aon[:], ao[par][:, 0, :], rs[:], ALU.mult), "aon")
                    if slot == 3:
                        act_pre.wait(dve, i, "mla")
                        head, rest = (flat(mla2[par][k][:]) for k in two)
                        divide(head, rest, flat(mla[:]), lambda ins: dve_pre.done(ins, "head"),
                               lambda ins: dve_pre.done(ins, "rest"), lambda: dve_pre.wait(dve, i, "head"))
                    if slot == 4:
                        pe_pre.wait(dve, i, "logits")
                        wide = lambda t: t[:].rearrange("p (s a) -> p s a", a=1).to_broadcast([P, SUB, E])
                        dve_pre.done(dve.tensor_tensor(lg[:], psB[:, :, 0:E], over_chunks(br[:], SUB), ALU.add), "lg")
                        dve_pre.wait(dve, i, "lg")
                        dve_pre.done(dve.tensor_reduce(mx[:], lg[:], AX.X, ALU.max), "mx")
                        dve_pre.wait(dve, i, "mx")
                        dve_pre.done(dve.tensor_tensor(lg[:], lg[:], wide(mx), ALU.subtract), "sub")
                    if slot == 5:
                        own.begin(i)
                        wide = lambda t: t[:].rearrange("p (s a) -> p s a", a=1).to_broadcast([P, SUB, E])
                        act_pre.wait(dve, i, "ex")
                        dve_pre.done(dve.tensor_reduce(total[:], ex[:], AX.X, ALU.add), "total")
                        dve_pre.wait(dve, i, "total")
                        dve_pre.done(dve.reciprocal(total[:], total[:]), "rtotal")
                        dve_pre.wait(dve, i, "rtotal")
                        dve_pre.done(dve.tensor_tensor(pr[:], ex[:], wide(total), ALU.mult), "pr")
                        dve_pre.wait(dve, i, "pr")
                        for s in range(SUB):
                            m.settle(dve)
                            ins = dve.max(top[:, s, :], pr[:, s, :])
                            own.mark(ins) if s < SUB - 1 else dve_pre.done(ins, "top")
                        own.wait(dve)
                        dve_pre.wait(dve, i, "top")
                        for s in range(SUB):
                            m.settle(dve)
                            ins = dve.max_index(index[:, s, :], top[:, s, :], pr[:, s, :])
                            own.mark(ins) if s < SUB - 1 else dve_pre.done(ins, "index")
                        own.wait(dve)
                        dve_pre.wait(dve, i, "index")
                        dve_pre.done(dve.tensor_copy(indexf[:], index[:]), "indexf")
                        dve_pre.done(dve.tensor_tensor(mx[:], top[:, :, 0], top[:, :, 1], ALU.add), "sum2")
                        dve_pre.wait(dve, i, "sum2")
                        dve_pre.done(dve.tensor_scalar(mx[:], mx[:], 1e-8, None, ALU.add), "rsum2")
                        dve_pre.wait(dve, i, "rsum2")
                        own.link(dve, dve.reciprocal(mx[:], mx[:]))
                        own.link(dve, dve.tensor_tensor(share[:, :, 0], top[:, :, 0], mx[:], ALU.mult))
                        dve_pre.done(dve.tensor_tensor(share[:, :, 1], top[:, :, 1], mx[:], ALU.mult), "share")
                        dve_pre.wait(dve, i, "share")
                        chosen = lambda t, k: t[:, :, k:k + 1].to_broadcast([P, SUB, E])
                        own.link(dve, dve.tensor_tensor(pick0[:], over_chunks(number[:], SUB), chosen(indexf, 0), ALU.is_equal))
                        own.link(dve, dve.tensor_tensor(pick1[:], over_chunks(number[:], SUB), chosen(indexf, 1), ALU.is_equal))
                        dve_pre.done(dve.tensor_tensor(pick0[:], pick0[:], chosen(share, 0), ALU.mult), "pick0")
                        dve_pre.done(dve.tensor_tensor(pick1[:], pick1[:], chosen(share, 1), ALU.mult), "pick1")
                        dve_pre.wait(dve, i, "pick1")
                        dve_pre.done(dve.tensor_tensor(comb[par][:], pick0[:], pick1[:], ALU.add), "comb")
                        own.end()
                    if slot == 6:
                        pe_pre.wait(dve, i, "combT")
                        dve_pre.done(dve.tensor_copy(combT[:].rearrange("e s t -> e (s t)"), psM[0:E, 0, :]), "combT")
                    if slot == 7:
                        pe_pre.wait(dve, i, "bias")
                        dve_pre.done(dve.tensor_copy(acc[par][:], psB[:]), "bias")

                def split_hidden(i, e):
                    dve.wait_ge(hid_ready, (i * E + e + 1) * FT)
                    if not (isinstance(i, int) and i == 0 and e < 2):
                        dve.wait_ge(out_psum, i * E + (e - 1) if e else i * E - 1)
                    head, rest = (flat(hid2[e % 2][k][:]) for k in two)
                    divide(head, rest, flat(hid[e % 2][:]), lambda ins: ins.then_inc(head_ready, 1),
                           lambda ins: ins.then_inc(rest_ready, 1), lambda: dve.wait_ge(head_ready, i * E + e + 1))

                def add(i, par, e):
                    dve.wait_ge(out_psum, i * E + e + 1)
                    if e == 0:
                        dve_pre.wait(dve, i, "bias")
                    else:
                        dve.wait_ge(added, i * E + e)
                    for s in range(SUB):
                        ins = dve.scalar_tensor_tensor(
                            out=acc[par][:, s, :], in0=psE[e % 2][:, s, :], scalar=comb[par][:, s, e:e + 1],
                            in1=acc[par][:, s, :], op0=ALU.mult, op1=ALU.add)
                        if s == 0:
                            ins.then_inc(dve_own, 1)
                    dve.wait_ge(dve_own, i * E + e + 1)
                    ins.then_inc(added, 1)

                def finish_a(i, par):
                    dve.wait_ge(added, (i + 1) * E)
                    dve.wait_ge(end_loaded[par], (i - par) * 24 + 48)
                    dve.scalar_tensor_tensor(out=gin[:], in0=acc[par][:], scalar=0.3, in1=xn[par][:],
                                             op0=ALU.mult, op1=ALU.add).then_inc(gin_ready, 1)

                def finish_b(i, par):
                    dve.wait_ge(gin_ready, i + 1)
                    dve.wait_ge(th_ready, i + 1)
                    dve.wait_ge(out_st, 16 * i)
                    dve.scalar_tensor_tensor(out=res[:], in0=th[:], scalar=1.0, in1=gin[:],
                                             op0=ALU.add, op1=ALU.mult).then_inc(half1, 1)
                    dve.wait_ge(half1, 2 * i + 1)
                    dve.scalar_tensor_tensor(out=res[:], in0=res[:], scalar=0.5, in1=s1[par][:],
                                             op0=ALU.mult, op1=ALU.mult).then_inc(half1, 1)
                    dve.wait_ge(half1, 2 * i + 2)
                    dve.tensor_tensor(res[:], res[:], x1[par][:], ALU.add).then_inc(res_ready, 1)

                def step(i, par, first, more):
                    for e in range(E):
                        if e + 1 < E:
                            split_hidden(i, e + 1)
                        elif more:
                            split_hidden(i + 1, 0)
                        add(i, par, e)
                        if more:
                            prepare(i + 1, 1 - par, e)
                        if not first and e == 0:
                            finish_a(i - 1, 1 - par)
                        if not first and e == 2:
                            finish_b(i - 1, 1 - par)

                for n in range(NSTAGED):
                    k, e = n % 2, n // 2
                    dve.wait_ge(staged[k], 16 * (e + 1))
                    head, rest = (((w2 if k else w1)[part][:, e, :, :].rearrange("p a b -> p (a b)")) for part in two)
                    divide(head, rest, flat(hid[k][:]), lambda ins: ins.then_inc(split, 1),
                           lambda ins: ins.then_inc(split, 1), lambda: dve.wait_ge(split, 2 * n + 1))
                dve.wait_ge(weights, 96)
                dve.wait_ge(consts, 3)
                for slot in range(E):
                    prepare(0, 0, slot)
                split_hidden(0, 0)
                run(dve, step)
                finish_a(NT - 1, 1)
                finish_b(NT - 1, 1)


PHASES = [ssm_inputs, ssm_scan, ssm_output, delta_inputs, delta_invert, delta_chunks, attention, experts]


def build(nc, A, phases=None):
    for phase in PHASES:
        if phases is None or phase.__name__ in phases:
            with nc.cleanup_on_exit(), nc.allow_non_contiguous_dma(reason="small vectors of weights"):
                phase(nc, A)


def _layout(inputs):
    a = {k: np.asarray(v) for k, v in inputs.items()}

    def of(block):
        return lambda name: a[f"{block}_{name}"]

    ssm, fp8, delta, moe = of("L0_attn"), of("L0_ffn"), of("L1_attn"), of("L1_ffn")
    used = np.arange(2 * P).reshape(NH, 2 * HD)[:, :HD].reshape(-1)
    laid = dict(
        x=ssm("hidden_states").reshape(N, D), w_xz=ssm("W_xz"), w_dt=ssm("W_dt"), b_dt=ssm("b_dt"),
        w_bc=np.concatenate([ssm("W_B"), ssm("W_C")], 1), a_log=ssm("A_log"), d_skip=ssm("D_skip"),
        w_out=ssm("W_out"), v_th=ssm("v_th"),
        kern=fp8("kernel"), s_in=fp8("input_scale"), s_k=fp8("kernel_scale"), bias=fp8("bias"),
        w_tok=np.concatenate([delta(n) for n in ("Wq", "Wk", "Wv", "Wa", "Wb")], 0).T,
        b_tok=np.concatenate([delta(n) for n in ("bq", "bk", "bv", "ba", "bb")]),
        w_gate=delta("Wg").T, b_gate=delta("bg"), w_o=delta("Wo").T, b_o=delta("bo"),
        fq=moe("q_w")[:, used], fqb=moe("q_b")[used], fk=moe("k_w"), fkb=moe("k_b"), fv=moe("v_w"), fvb=moe("v_b"),
        fo=moe("o_w"), fob=moe("o_b"), rw=moe("router_w"), rb=moe("router_b"),
        w1=moe("w1"), b1=moe("b1"), w2=moe("w2"), b2=moe("b2"))
    return {k: np.ascontiguousarray(v) for k, v in laid.items()}


def kernel(**inputs):
    import concourse.bacc as bacc
    from concourse.bass_utils import run_bass_kernel_spmd

    nc = bacc.Bacc("TRN2", target_bir_lowering=False, num_devices=1)
    arrays, A = {}, {}
    for name, value in _layout(inputs).items():
        arrays[f"in_{name}"] = value
        A[name] = nc.dram_tensor(f"in_{name}", value.shape, mybir.dt.from_np(value.dtype), kind="ExternalInput").ap()
    kinds = {"float32": F32, "bfloat16": BF16}
    for name, (shape, dtype) in SCRATCH.items():
        A[name] = nc.dram_tensor(f"scratch_{name}", shape, kinds[dtype]).ap()
    A["out"] = nc.dram_tensor("out_dram", (N, D), F32, kind="ExternalOutput").ap()
    build(nc, A)
    r = run_bass_kernel_spmd(nc, [arrays], core_ids=[0])
    return r.results[0]["out_dram"].reshape(B, T, D)
```

```python
from contextlib import ExitStack

import numpy as np
import concourse.bass as bass
from concourse import mybir

F32 = mybir.dt.float32
F32R = mybir.dt.float32r
BF16 = mybir.dt.bfloat16
I32 = mybir.dt.int32
U32 = mybir.dt.uint32
ALU = mybir.AluOpType
ACT = mybir.ActivationFunctionType
AX = mybir.AxisListType

B, T, D = 8, 1024, 256
N = B * T
P = 128
H = D // P
S = 16
TILE = 512
SUB = TILE // P
NT = N // TILE
NP = N // P
C = 128
NH, HD = 16, 8
E, TOPK, FF = 8, 2, 512
EPS = 1e-5
FP8_MAX_TIE = 464.0

LOG_A, LOG_G, BETA, EXP_G, NEG_EXP_G, TO_END_BETA, EXP_END = range(7)
NDEC = 7

SCRATCH = {
    "dec": ([P, NP, 7], "float32"),
    "xn0": ([N, D], "float32"), "x_t": ([H, P, N], "float32"), "z_t": ([H, P, N], "float32"),
    "dt_t": ([H, P, N], "float32"), "u_t": ([H, P, N], "float32"), "xq_t": ([H, P, N], "bfloat16"),
    "bc": ([3, 2 * S, N], "bfloat16"), "y_t": ([H, P, N], "float32"), "xmax": ([P, NP], "float32"),
    "x1": ([N, D], "float32"), "xn1": ([N, D], "float32"),
    "qd": ([N, C], "float32"), "kd": ([N, C], "float32"), "vd": ([N, C], "float32"),
    "ab": ([P, NP, 2], "float32"), "gate_t": ([C, N], "float32"),
    "qs": ([B, NH // 4, 3, 32, T], "bfloat16"), "ks": ([B, NH // 4, 3, 32, T], "bfloat16"), "vf": ([N, P], "float32"),
    "inv": ([NP, P, P], "float32"), "dm": ([NP, P, P], "float32"), "kt": ([NP, P, P], "float32"),
    "qt": ([NP, P, P], "float32"), "qgt": ([NP, P, P], "float32"),
    "s1": ([N, D], "float32"), "ao": ([NH, 2 * HD, N], "float32"),
}


class Chain:

    def __init__(self, sem, per):
        self.sem, self.per, self.base, self.n = sem, per, 0, 0

    def begin(self, i):
        self.base, self.n = i * self.per, 0

    def end(self):
        assert self.n == self.per, (self.n, self.per)

    def link(self, eng, ins):
        self.mark(ins)
        self.wait(eng)

    def mark(self, ins):
        self.n += 1
        ins.then_inc(self.sem, 1)

    def wait(self, eng):
        eng.wait_ge(self.sem, self.base + self.n)


def pairs(eng, count):
    with eng.Fori(0, count // 2) as turn:
        for par in range(2):
            yield turn * 2 + par, par


def one_ahead(eng, step, count=NT):
    with eng.Fori(0, count // 2 - 1) as turn:
        for par in range(2):
            step(turn * 2 + par, par, True)
    step(count - 2, 0, True)
    step(count - 1, 1, False)


def load_ahead(sp, count, load, done, per=1):
    load(0, 0)
    if count > 2:
        with sp.Fori(0, count // 2 - 1) as turn:
            i = turn * 2
            sp.wait_ge(done, i * per)
            load(i + 1, 1)
            sp.wait_ge(done, i * per + per)
            load(i + 2, 0)
    sp.wait_ge(done, (count - 2) * per)
    load(count - 1, 1)


class Memory:

    def __init__(self, nc, ctx, phase):
        self.nc, self.ctx, self.phase = nc, ctx, phase
        self.settled = self.sem("settled")

    def settle(self, eng):
        eng.sem_inc(self.settled, 1)

    def sb(self, name, shape, dt=F32):
        return self.ctx.enter_context(self.nc.sbuf_tensor(f"{self.phase}_{name}", shape, dt))

    def ps(self, name, shape, dt=F32):
        return self.ctx.enter_context(self.nc.psum_tensor(f"{self.phase}_{name}", shape, dt))

    def sem(self, name):
        return self.nc.alloc_semaphore(name=f"{self.phase}_{name}")


def halves(ap):
    return ap.rearrange("(h p) n -> p h n", p=P)


def column(ap):
    return ap.rearrange("(h p) -> p h", p=P)


def spread(ap, n):
    return ap.rearrange("(a n) -> a n", a=1).to_broadcast([P, n])


def identity(nc, eng, ident, sem):
    eng.memset(ident[:], 0.0).then_inc(sem, 1)
    eng.wait_ge(sem, 1)
    eng.affine_select(out=ident[:], in_=ident[:], compare_op=ALU.not_equal, fill=1.0, base=0,
                      pattern=[[-1, P]], channel_multiplier=1).then_inc(sem, 1)


def ssm_inputs(nc, A):
    with ExitStack() as ctx:
        m = Memory(nc, ctx, "si")
        wxz, wdt, wbc = m.sb("wxz", [P, H, 2 * D]), m.sb("wdt", [P, H, D]), m.sb("wbc", [P, H, 2 * S])
        bdt, sin, rsin = m.sb("bdt", [P, H]), m.sb("sin", [P, 1]), m.sb("rsin", [P, 1])
        ident = m.sb("ident", [P, P])
        x = [m.sb(f"x{k}", [P, SUB, D]) for k in range(2)]
        xn = m.sb("xn", [P, SUB, D])
        stats, mv = m.sb("stats", [P, SUB, 6]), m.sb("mv", [P, SUB, 2])
        ve, half, rstd = m.sb("ve", [P, SUB]), m.sb("half", [P, SUB]), m.sb("rstd", [P, SUB])
        xmax = m.sb("xmax", [P, NP])
        xnT, xb = m.sb("xnT", [P, H, TILE]), m.sb("xb", [P, H, TILE], BF16)
        xT, zT = m.sb("xT", [P, H, TILE]), m.sb("zT", [P, H, TILE])
        vb, mag, soft = m.sb("vb", [P, H, TILE]), m.sb("mag", [P, H, TILE]), m.sb("soft", [P, H, TILE])
        dtT, uT = m.sb("dtT", [P, H, TILE]), m.sb("uT", [P, H, TILE])
        v8, e8, r8 = m.sb("v8", [P, H, TILE]), m.sb("e8", [P, H, TILE]), m.sb("r8", [P, H, TILE])
        xq = m.sb("xq", [P, H, TILE], BF16)
        b_part = m.sb("b_part", [2 * S, 3, TILE], BF16)
        b_rest = m.sb("b_rest", [2 * S, 2, TILE])
        psT, psX, psZ = m.ps("psT", [P, H, TILE]), m.ps("psX", [P, H, TILE]), m.ps("psZ", [P, H, TILE])
        psD = m.ps("psD", [P, H, TILE])

        weights, x_loaded = m.sem("weights"), [m.sem(f"x_loaded{k}") for k in range(2)]
        ident_made, consts = m.sem("ident_made"), m.sem("consts")
        var_ready, rstd_ready, xn_ready, xT_psum = m.sem("var"), m.sem("rstd"), m.sem("xn"), m.sem("xT_psum")
        xnT_ready, xb_ready = m.sem("xnT"), m.sem("xb")
        x_psum, z_psum, bc_psum, dt_psum = m.sem("x_psum"), m.sem("z_psum"), m.sem("bc_psum"), m.sem("dt_psum")
        x_ready, z_ready, bc_ready = m.sem("x_ready"), m.sem("z_ready"), m.sem("bc_ready")
        soft_ready, vb_ready, dt_ready, u_ready = m.sem("soft"), m.sem("vb"), m.sem("dt_ready"), m.sem("u_ready")
        v8_ready, e8_ready, xq_ready = m.sem("v8"), m.sem("e8"), m.sem("xq_ready")
        xn_st, x_st, z_st, bc_st, dt_st, u_st, xq_st = (m.sem(f"{n}_st") for n in ("xn", "x", "z", "bc", "dt", "u", "xq"))
        e8_and, rsin_ready = m.sem("e8_and"), m.sem("rsin_ready")
        max_st, max_ready = m.sem("max_st"), m.sem("max_ready")
        act_own, dve_own, dve_split, pool_own = (m.sem(n) for n in ("act_own", "dve_own", "dve_split", "pool_own"))
        x_in = A["x"].rearrange("(i s p) d -> i p s d", p=P, s=SUB)
        xn_out = A["xn0"].rearrange("(i s p) d -> i p s d", p=P, s=SUB)

        def tile(name, i):
            return A[name].rearrange("h p (i t) -> i p h t", t=TILE)[i, :, :, :]

        with nc.Block() as block:
            @block.sync
            def _(sp):
                sp.dma_start(wxz[:], halves(A["w_xz"])).then_inc(weights, 16)
                sp.dma_start(wdt[:], halves(A["w_dt"])).then_inc(weights, 16)
                sp.dma_start(wbc[:], halves(A["w_bc"])).then_inc(weights, 16)
                sp.dma_start(bdt[:], column(A["b_dt"])).then_inc(weights, 16)
                sp.dma_start(sin[:], spread(A["s_in"], 1)).then_inc(weights, 16)

                def load(i, par):
                    sp.dma_start(x[par][:], x_in[i, :, :, :]).then_inc(x_loaded[par], 16)

                def front(i, par, then_load):
                    sp.wait_ge(xn_ready, i + 1)
                    m.settle(sp)
                    sp.dma_start(xn_out[i, :, :, :], xn[:]).then_inc(xn_st, 16)
                    if then_load:
                        load(i + 2, par)

                def step(i, par, more):
                    for ready, name, buf, sem in ((x_ready, "x_t", xT, x_st), (z_ready, "z_t", zT, z_st)):
                        sp.wait_ge(ready, i + 1)
                        m.settle(sp)
                        sp.dma_start(tile(name, i), buf[:]).then_inc(sem, 16)
                    if more:
                        front(i + 1, 1 - par, more == "loads")
                    sp.wait_ge(bc_ready, i + 1)
                    m.settle(sp)
                    sp.dma_start(A["bc"].rearrange("k r (i t) -> i r k t", t=TILE)[i, :, :, :], b_part[:]).then_inc(bc_st, 16)
                    for ready, name, buf, sem in ((xq_ready, "xq_t", xq, xq_st), (dt_ready, "dt_t", dtT, dt_st), (u_ready, "u_t", uT, u_st)):
                        sp.wait_ge(ready, i + 1)
                        m.settle(sp)
                        sp.dma_start(tile(name, i), buf[:]).then_inc(sem, 16)

                load(0, 0)
                load(1, 1)
                front(0, 0, True)
                with sp.Fori(0, NT // 2 - 2) as turn:
                    step(turn * 2, 0, "loads")
                    step(turn * 2 + 1, 1, "loads")
                step(NT - 4, 0, "loads")
                step(NT - 3, 1, "no loads")
                step(NT - 2, 0, "no loads")
                step(NT - 1, 1, None)
                sp.wait_ge(max_ready, NT)
                sp.dma_start(A["xmax"], xmax[:]).then_inc(max_st, 16)
                for sem in (xn_st, x_st, z_st, bc_st, dt_st, u_st, xq_st):
                    sp.wait_ge(sem, 16 * NT)
                    m.settle(sp)
                sp.wait_ge(max_st, 16)

            @block.gpsimd
            def _(pool):
                identity(nc, pool, ident, ident_made)
                pool.memset(half[:], -0.5).then_inc(consts, 1)
                pool.wait_ge(consts, 1)

                def front(i, par):
                    pool.wait_ge(var_ready, i + 1)
                    pool.wait_ge(xn_ready, i)
                    m.settle(pool)
                    pool.tensor_scalar_add(ve[:], mv[:, :, 1], EPS).then_inc(pool_own, 1)
                    pool.wait_ge(pool_own, 2 * i + 1)
                    pool.tensor_tensor(rstd[:], ve[:], half[:], ALU.pow).then_inc(rstd_ready, 1)
                    pool.wait_ge(e8_ready, i + 1)
                    pool.wait_ge(xq_st, 16 * i)
                    pool.tensor_tensor(r8[:], v8[:], e8[:], ALU.add).then_inc(pool_own, 1)
                    pool.wait_ge(pool_own, 2 * i + 2)
                    pool.tensor_tensor(xq[:], r8[:], e8[:], ALU.subtract).then_inc(xq_ready, 1)

                for i, par in pairs(pool, NT):
                    front(i, par)

            @block.vector
            def _(dve):
                own, split = Chain(dve_own, 3 * SUB - 2), Chain(dve_split, 4)
                dve.wait_ge(weights, 80)
                dve.reciprocal(rsin[:], sin[:]).then_inc(rsin_ready, 1)

                def variance(i, par):
                    own.begin(i)
                    dve.wait_ge(x_loaded[par], (i - par) * 8 + 16)
                    for s in range(SUB):
                        own.mark(dve.bn_stats(stats[:, s, :], x[par][:, s, :]))
                    own.wait(dve)
                    dve.wait_ge(rstd_ready, i)
                    for s in range(SUB):
                        m.settle(dve)
                        ins = dve.bn_aggr(mv[:, s, :], stats[:, s, :])
                        if s < SUB - 1:
                            own.mark(ins)
                        else:
                            ins.then_inc(var_ready, 1)
                    own.wait(dve)

                def normalise(i, par):
                    own.base, own.n = i * own.per, 2 * SUB - 1
                    dve.wait_ge(rstd_ready, i + 1)
                    dve.wait_ge(xn_st, 16 * i)
                    dve.wait_ge(xT_psum, i)
                    for s in range(SUB):
                        ins = dve.tensor_scalar(xn[:, s, :], x[par][:, s, :], mv[:, s, 0:1], rstd[:, s:s + 1],
                                                ALU.subtract, ALU.mult)
                        if s < SUB - 1:
                            own.mark(ins)
                        else:
                            ins.then_inc(xn_ready, 1)
                    own.wait(dve)
                    dve.wait_ge(xn_ready, i + 1)
                    dve.tensor_reduce(xmax[:, bass.ds(i * SUB, SUB)], xn[:], AX.X, ALU.max,
                                      apply_absolute_value=True).then_inc(max_ready, 1)

                def x_part(i):
                    dve.wait_ge(x_psum, i + 1)
                    dve.wait_ge(x_st, 16 * i)
                    dve.wait_ge(u_ready, i)
                    dve.tensor_copy(xT[:], psX[:]).then_inc(x_ready, 1)

                def bc_part(i):
                    split.begin(i)
                    dve.wait_ge(bc_psum, i + 1)
                    dve.wait_ge(bc_st, 16 * i)
                    bc = psD[0:2 * S, 0, :]
                    split.link(dve, dve.tensor_copy(b_part[:, 0, :], bc))
                    split.link(dve, dve.tensor_tensor(b_rest[:, 0, :], bc, b_part[:, 0, :], ALU.subtract))
                    split.link(dve, dve.tensor_copy(b_part[:, 1, :], b_rest[:, 0, :]))
                    split.link(dve, dve.tensor_tensor(b_rest[:, 1, :], b_rest[:, 0, :], b_part[:, 1, :], ALU.subtract))
                    dve.tensor_copy(b_part[:, 2, :], b_rest[:, 1, :]).then_inc(bc_ready, 1)
                    split.end()

                def fp8_step(i):
                    dve.wait_ge(v8_ready, i + 1)
                    dve.wait_ge(xq_ready, i)
                    dve.tensor_single_scalar(e8[:].bitcast(I32), v8[:].bitcast(I32), 0x7F800000,
                                             ALU.bitwise_and).then_inc(e8_and, 1)
                    dve.wait_ge(e8_and, i + 1)
                    dve.tensor_scalar(e8[:], e8[:], 2.0 ** -6, 1.5 * 2.0 ** 20, ALU.max, ALU.mult).then_inc(e8_ready, 1)

                def dt_part(i):
                    dve.wait_ge(soft_ready, i + 1)
                    dve.wait_ge(dt_st, 16 * i)
                    dve.scalar_tensor_tensor(out=dtT[:], in0=vb[:], scalar=0.0, in1=soft[:],
                                             op0=ALU.max, op1=ALU.add).then_inc(dt_ready, 1)
                    dve.wait_ge(dt_ready, i + 1)
                    dve.wait_ge(x_ready, i + 1)
                    dve.wait_ge(u_st, 16 * i)
                    dve.tensor_tensor(uT[:], dtT[:], xT[:], ALU.mult).then_inc(u_ready, 1)

                def step(i, par, more):
                    x_part(i)
                    if more:
                        normalise(i + 1, 1 - par)
                    bc_part(i)
                    if more:
                        fp8_step(i + 1)
                    if more and not (isinstance(i, int) and i == NT - 2):
                        variance(i + 2, par)
                    dt_part(i)

                variance(0, 0)
                normalise(0, 0)
                fp8_step(0)
                variance(1, 1)
                one_ahead(dve, step)

            @block.scalar
            def _(act):
                own = Chain(act_own, 2)

                def front(i):
                    act.wait_ge(xT_psum, i + 1)
                    act.wait_ge(bc_psum, i)
                    act.activation(xnT[:], psT[:], ACT.Copy).then_inc(xnT_ready, 1)
                    act.wait_ge(v8_ready, i)
                    act.activation(xb[:], psT[:], ACT.Copy).then_inc(xb_ready, 1)
                    act.wait_ge(xb_ready, i + 1)
                    act.wait_ge(xq_ready, i)
                    act.activation(v8[:], xb[:], ACT.Copy, scale=rsin[:, 0:1]).then_inc(v8_ready, 1)

                act.wait_ge(weights, 80)
                act.wait_ge(rsin_ready, 1)
                def step(i, par, more):
                    own.begin(i)
                    if more:
                        front(i + 1)
                    act.wait_ge(z_psum, i + 1)
                    act.wait_ge(z_st, 16 * i)
                    act.activation(zT[:], psZ[:], ACT.Copy).then_inc(z_ready, 1)
                    act.wait_ge(dt_psum, i + 1)
                    act.wait_ge(dt_ready, i)
                    for h in range(H):
                        act.activation(vb[:, h, :], psD[:, h, :], ACT.Identity, bias=bdt[:, h:h + 1]).then_inc(vb_ready, 1)
                    act.wait_ge(vb_ready, H * i + H)
                    own.link(act, act.activation(mag[:], vb[:], ACT.Abs))
                    own.link(act, act.activation(mag[:], mag[:], ACT.Exp, scale=-1.0))
                    act.activation(soft[:], mag[:], ACT.Ln, bias=1.0).then_inc(soft_ready, 1)
                    own.end()

                front(0)
                one_ahead(act, step)

            @block.tensor
            def _(pe):
                pe.wait_ge(ident_made, 2)
                pe.wait_ge(weights, 80)

                def transposes(i):
                    pe.wait_ge(xn_ready, i + 1)
                    pe.wait_ge(xnT_ready, i)
                    pe.wait_ge(xb_ready, i)
                    for s in range(SUB):
                        for h in range(H):
                            last = pe.transpose(psT[:, h, s * P:(s + 1) * P], xn[:, s, h * P:(h + 1) * P], ident[:])
                    last.then_inc(xT_psum, 1)

                def project(dst, weight, src):
                    for k in range(H):
                        out = pe.matmul(dst, weight[k], src[:, k, :], start=(k == 0), stop=(k == H - 1))
                    return out

                def step(i, par, more):
                    pe.wait_ge(xnT_ready, i + 1)
                    pe.wait_ge(x_ready, i)
                    for h in range(H):
                        last = project(psX[:, h, :], [wxz[:, k, h * P:(h + 1) * P] for k in range(H)], xnT)
                    last.then_inc(x_psum, 1)
                    pe.wait_ge(z_ready, i)
                    for h in range(H):
                        last = project(psZ[:, h, :], [wxz[:, k, D + h * P:D + (h + 1) * P] for k in range(H)], xnT)
                    last.then_inc(z_psum, 1)
                    pe.wait_ge(vb_ready, H * i)
                    project(psD[0:2 * S, 0, :], [wbc[:, k, :] for k in range(H)], xnT).then_inc(bc_psum, 1)
                    if more:
                        transposes(i + 1)
                    pe.wait_ge(bc_ready, i + 1)
                    pe.wait_ge(x_ready, i + 1)
                    for h in range(H):
                        last = project(psD[:, h, :], [wdt[:, k, h * P:(h + 1) * P] for k in range(H)], xT)
                    last.then_inc(dt_psum, 1)

                transposes(0)
                one_ahead(pe, step)


def ssm_scan(nc, A):
    with ExitStack() as ctx:
        m = Memory(nc, ctx, "sc")
        a_neg = m.sb("a_neg", [P, H, S])
        a_exp = m.sb("a_exp", [P, H, S])
        skip = m.sb("skip", [P, H])
        ident = m.sb("ident", [P, P])
        pick = m.sb("pick", [3 * 2 * S, 2 * S, P], BF16)
        bc = [m.sb(f"bc{k}", [3 * 2 * S, T], BF16) for k in range(2)]
        dt, u, x = ([m.sb(f"{n}{k}", [P, T]) for k in range(2)] for n in ("dt", "u", "x"))
        dec, prod = ([m.sb(f"{n}{k}", [P, T]) for k in range(2)] for n in ("dec", "prod"))
        inp, state, y = m.sb("inp", [P, T]), m.sb("state", [P, T]), m.sb("y", [P, T])
        psB = [m.ps(f"psB{k}", [P, T]) for k in range(2)]
        psC, psY = m.ps("psC", [P, T]), m.ps("psY", [P, T])
        weights, ident_made, pick_made = m.sem("weights"), m.sem("ident_made"), m.sem("pick_made")
        a_made, a_exp_made = m.sem("a_made"), m.sem("a_exp_made")
        loaded = [m.sem(f"loaded{k}") for k in range(2)]
        dec_ready, b_psum, c_psum = m.sem("dec"), m.sem("b_psum"), m.sem("c_psum")
        inp_ready, state_ready, prod_ready, y_added, y_ready, y_st = (
            m.sem(n) for n in ("inp", "state", "prod", "y_added", "y_ready", "y_st"))
        UNITS = B * H
        bank = T // TILE

        def unit(name, turn, h):
            return A[name].rearrange("h p (b t) -> b h p t", t=T)[turn, h, :, :]

        with nc.Block() as block:
            @block.sync
            def _(sp):
                with nc.allow_non_contiguous_dma(reason="small"):
                    sp.dma_start(a_exp[:], A["a_log"].rearrange("(h p) n -> p h n", p=P)).then_inc(weights, 16)
                    sp.dma_start(skip[:], column(A["d_skip"])).then_inc(weights, 16)

                def load(b, h):
                    parts = A["bc"].rearrange("k r (b t) -> b k r t", t=T)[b, :, :, :]
                    sp.dma_start(bc[h][:], parts.rearrange("k r t -> (k r) t")).then_inc(loaded[h], 16)
                    sp.dma_start(dt[h][:], unit("dt_t", b, h)).then_inc(loaded[h], 16)
                    sp.dma_start(u[h][:], unit("u_t", b, h)).then_inc(loaded[h], 16)
                    sp.dma_start(x[h][:], unit("x_t", b, h)).then_inc(loaded[h], 16)

                load(0, 0)
                with sp.Fori(0, B - 1) as b:
                    sp.wait_ge(y_ready, b * H)
                    m.settle(sp)
                    load(b, 1)
                    sp.wait_ge(y_ready, b * H + 1)
                    m.settle(sp)
                    load(b + 1, 0)
                sp.wait_ge(y_ready, (B - 1) * H)
                load(B - 1, 1)
                sp.wait_ge(y_st, 16 * UNITS)

            @block.gpsimd
            def _(pool):
                identity(nc, pool, ident, ident_made)
                pool.memset(pick[:], 0.0).then_inc(pick_made, 1)
                for k in range(3):
                    pool.wait_ge(pick_made, k + 1)
                    pool.affine_select(out=pick[:], in_=pick[:], compare_op=ALU.not_equal, fill=1.0,
                                       base=-2 * S * k, pattern=[[-1, 2 * S], [0, P]],
                                       channel_multiplier=1).then_inc(pick_made, 1)
                with pool.Fori(0, B) as b:
                    for h in range(H):
                        pool.wait_ge(y_ready, b * H + h + 1)
                        m.settle(pool)
                        pool.dma_start(unit("y_t", b, h), y[:]).then_inc(y_st, 16)

            @block.scalar
            def _(act):
                act.wait_ge(weights, 32)
                act.activation(a_neg[:], a_exp[:], ACT.Exp).then_inc(a_exp_made, 1)
                act.wait_ge(a_made, 1)
                with act.Fori(0, B) as b:
                    for h in range(H):
                        act.wait_ge(loaded[h], 64 * b + 64)
                        for n in range(S):
                            at = (b * H + h) * S + n
                            if n >= 2 or h > 0:
                                act.wait_ge(state_ready, at - 1)
                            else:
                                act.wait_ge(state_ready, b * H * S)
                            act.activation(dec[n % 2][:], dt[h][:], ACT.Exp,
                                           scale=a_exp[:, h, n:n + 1]).then_inc(dec_ready, 1)

            @block.tensor
            def _(pe):
                pe.wait_ge(ident_made, 2)
                pe.wait_ge(pick_made, 4)

                def broadcast(dst, h, row):
                    for k in range(bank):
                        out = pe.matmul(dst[:, k * TILE:(k + 1) * TILE], pick[:, row, :],
                                        bc[h][:, k * TILE:(k + 1) * TILE], start=True, stop=True)
                    return out

                def add(b, h, n):
                    at = (b * H + h) * S + n
                    pe.wait_ge(prod_ready, at + 1)
                    if n == 0:
                        pe.wait_ge(y_ready, b * H + h)
                    for k in range(bank):
                        out = pe.matmul(psY[:, k * TILE:(k + 1) * TILE], ident[:],
                                        prod[n % 2][:, k * TILE:(k + 1) * TILE], start=(n == 0), stop=(n == S - 1))
                    out.then_inc(y_added, 1)

                with pe.Fori(0, B) as b:
                    for h in range(H):
                        pe.wait_ge(loaded[h], 64 * b + 64)
                        for n in range(S):
                            at = (b * H + h) * S + n
                            if n >= 2 or h > 0:
                                pe.wait_ge(inp_ready, at - 1)
                            else:
                                pe.wait_ge(inp_ready, b * H * S)
                            broadcast(psB[n % 2], h, n).then_inc(b_psum, 1)
                            if n > 0:
                                add(b, h, n - 1)
                            else:
                                pe.wait_ge(prod_ready, at)
                            broadcast(psC, h, S + n).then_inc(c_psum, 1)
                        add(b, h, S - 1)

            @block.vector
            def _(dve):
                dve.wait_ge(a_exp_made, 1)
                dve.tensor_scalar(a_exp[:], a_neg[:], -1.0, None, ALU.mult).then_inc(a_made, 1)
                with dve.Fori(0, B) as b:
                    for h in range(H):
                        dve.wait_ge(loaded[h], 64 * b + 64)
                        for n in range(S):
                            at = (b * H + h) * S + n
                            dve.wait_ge(b_psum, at + 1)
                            dve.wait_ge(state_ready, at)
                            dve.tensor_tensor(inp[:], u[h][:], psB[n % 2][:], ALU.mult).then_inc(inp_ready, 1)
                            dve.wait_ge(inp_ready, at + 1)
                            dve.wait_ge(dec_ready, at + 1)
                            dve.wait_ge(prod_ready, at)
                            dve.tensor_tensor_scan(state[:], dec[n % 2][:], inp[:], 0.0, ALU.mult, ALU.add).then_inc(state_ready, 1)
                            dve.wait_ge(state_ready, at + 1)
                            dve.wait_ge(c_psum, at + 1)
                            if n >= 2 or h > 0:
                                dve.wait_ge(y_added, at - 1)
                            else:
                                dve.wait_ge(y_added, b * H * S)
                            dve.tensor_tensor(prod[n % 2][:], state[:], psC[:], ALU.mult).then_inc(prod_ready, 1)
                        dve.wait_ge(y_added, (b * H + h) * S + S)
                        dve.wait_ge(y_st, 16 * (b * H + h))
                        dve.scalar_tensor_tensor(out=y[:], in0=x[h][:], scalar=skip[:, h:h + 1], in1=psY[:],
                                                 op0=ALU.mult, op1=ALU.add).then_inc(y_ready, 1)


def ssm_output(nc, A):
    with ExitStack() as ctx:
        m = Memory(nc, ctx, "so")
        wout, kern, kq = m.sb("wout", [P, H, D]), m.sb("kern", [P, H, D], BF16), m.sb("kq", [P, H, D], BF16)
        kv, ke, kr = m.sb("kv", [P, H, D]), m.sb("ke", [P, H, D]), m.sb("kr", [P, H, D])
        vth, vbias = m.sb("vth", [P, H]), m.sb("vbias", [P, H])
        bias = m.sb("bias", [P, D], BF16)
        scales, rscale, both = m.sb("scales", [P, 2]), m.sb("rscale", [P, 2]), m.sb("both", [P, 1])
        xmax, per_tok, bad = m.sb("xmax", [P, NP]), m.sb("per_tok", [P, NP]), m.sb("bad", [P, NP])
        tok = m.sb("tok", [P, SUB])
        y, z, xq = ([m.sb(f"{n}{k}", [P, H, TILE], t) for k in range(2)] for n, t in (("y", F32), ("z", F32), ("xq", BF16)))
        x, xn = ([m.sb(f"{n}{k}", [P, SUB, D]) for k in range(2)] for n in ("x", "xn"))
        spike, open_ = m.sb("spike", [P, H, TILE]), m.sb("open", [P, H, TILE])
        ysp, zsp, a = m.sb("ysp", [P, H, TILE]), m.sb("zsp", [P, H, TILE]), [m.sb(f"a{k}", [P, H, TILE]) for k in range(2)]
        g0, g1 = m.sb("g0", [P, SUB, D], BF16), m.sb("g1", [P, SUB, D], BF16)
        gs, gden, grec, g = (m.sb(n, [P, SUB, D], BF16) for n in ("gs", "gden", "grec", "g"))
        s, sg = m.sb("s", [P, SUB, D]), m.sb("sg", [P, SUB, D])
        x1 = [m.sb(f"x1{k}", [P, SUB, D]) for k in range(2)]
        psO = [m.ps(f"psO{k}", [P, SUB, D]) for k in range(2)]
        psG = [m.ps(f"psG{k}", [P, SUB, D]) for k in range(2)]
        weights, loaded = m.sem("weights"), [m.sem(f"loaded{k}") for k in range(2)]
        prep, kq_ready, tok_ready = m.sem("prep"), m.sem("kq"), m.sem("tok_ready")
        vbias_ready = m.sem("vbias")
        spike_ready, open_ready, a_ready, o_psum, g_psum = (m.sem(n) for n in ("spike", "open", "a", "o_psum", "g_psum"))
        g0_ready, g1_ready, gs_ready, x1_ready = (m.sem(n) for n in ("g0", "g1", "gs", "x1_ready"))
        x1_st, gden_ready, grec_ready = m.sem("x1_st"), m.sem("gden"), m.sem("grec")
        step, dve_own, ysp_ready, zsp_ready = m.sem("step"), m.sem("dve_own"), m.sem("ysp"), m.sem("zsp")

        def tile(name, i):
            return A[name].rearrange("h p (i t) -> i p h t", t=TILE)[i, :, :, :]

        def rows(name, i):
            return A[name].rearrange("(i s p) d -> i p s d", p=P, s=SUB)[i, :, :, :]

        with nc.Block() as block:
            @block.sync
            def _(sp):
                sp.dma_start(wout[:], halves(A["w_out"])).then_inc(weights, 16)
                sp.dma_start(kern[:], halves(A["kern"])).then_inc(weights, 16)
                sp.dma_start(vth[:], column(A["v_th"])).then_inc(weights, 16)
                sp.dma_start(bias[:], spread(A["bias"], D)).then_inc(weights, 16)
                sp.dma_start(scales[:, 0:1], spread(A["s_in"], 1)).then_inc(weights, 16)
                sp.dma_start(scales[:, 1:2], spread(A["s_k"], 1)).then_inc(weights, 16)
                sp.dma_start(xmax[:], A["xmax"]).then_inc(weights, 16)

                def load(i, par):
                    sp.dma_start(y[par][:], tile("y_t", i)).then_inc(loaded[par], 16)
                    sp.dma_start(z[par][:], tile("z_t", i)).then_inc(loaded[par], 16)
                    sp.dma_start(xq[par][:], tile("xq_t", i)).then_inc(loaded[par], 16)
                    sp.dma_start(x[par][:], rows("x", i)).then_inc(loaded[par], 16)
                    sp.dma_start(xn[par][:], rows("xn0", i)).then_inc(loaded[par], 16)

                load_ahead(sp, NT, load, x1_ready)
                sp.wait_ge(x1_st, 16 * NT)

            @block.gpsimd
            def _(pool):
                for i, par in pairs(pool, NT):
                    pool.wait_ge(x1_ready, i + 1)
                    m.settle(pool)
                    pool.dma_start(rows("x1", i), x1[par][:]).then_inc(x1_st, 16)

            @block.scalar
            def _(act):
                act.wait_ge(vbias_ready, 1)
                for i, par in pairs(act, NT):
                    act.wait_ge(loaded[par], (i - par) * 40 + 80)
                    act.wait_ge(ysp_ready, i)
                    for h in range(H):
                        act.activation(spike[:, h, :], y[par][:, h, :], ACT.Tanh, bias=vbias[:, h:h + 1],
                                       scale=5.0).then_inc(spike_ready, 1)
                    act.wait_ge(zsp_ready, i)
                    act.activation(open_[:], z[par][:], ACT.Tanh, scale=0.5).then_inc(open_ready, 1)
                    act.wait_ge(g1_ready, i + 1)
                    act.activation(gs[:], g1[:], ACT.Exp, scale=-1.0).then_inc(gs_ready, 1)

            @block.tensor
            def _(pe):
                pe.wait_ge(weights, 112)
                pe.wait_ge(kq_ready, 1)
                for i, par in pairs(pe, NT):
                    pe.wait_ge(loaded[par], (i - par) * 40 + 80)
                    pe.wait_ge(x1_ready, i)
                    for k in range(SUB):
                        for h in range(H):
                            last = pe.matmul(psG[par][:, k, :], xq[par][:, h, k * P:(k + 1) * P], kq[:, h, :],
                                             start=(h == 0), stop=(h == H - 1))
                    last.then_inc(g_psum, 1)
                    pe.wait_ge(a_ready, i + 1)
                    for k in range(SUB):
                        for h in range(H):
                            last = pe.matmul(psO[par][:, k, :], a[par][:, h, k * P:(k + 1) * P], wout[:, h, :],
                                             start=(h == 0), stop=(h == H - 1))
                    last.then_inc(o_psum, 1)

            @block.vector
            def _(dve):
                dve.wait_ge(weights, 112)
                own = Chain(dve_own, 14)
                own.begin(0)
                own.link(dve, dve.reciprocal(rscale[:], scales[:]))
                own.link(dve, dve.tensor_scalar(kv[:], kern[:], rscale[:, 1:2], None, ALU.mult))
                own.link(dve, dve.tensor_single_scalar(ke[:].bitcast(I32), kv[:].bitcast(I32), 0x7F800000, ALU.bitwise_and))
                own.link(dve, dve.tensor_scalar(ke[:], ke[:], 2.0 ** -6, 1.5 * 2.0 ** 20, ALU.max, ALU.mult))
                own.link(dve, dve.tensor_tensor(kr[:], kv[:], ke[:], ALU.add))
                own.link(dve, dve.tensor_tensor(kr[:], kr[:], ke[:], ALU.subtract))
                own.link(dve, dve.tensor_tensor(kv[:], kv[:], kv[:], ALU.mult))
                own.link(dve, dve.tensor_scalar(kv[:], kv[:], FP8_MAX_TIE ** 2, 3e38, ALU.is_gt, ALU.mult))
                own.link(dve, dve.tensor_scalar(kv[:], kv[:], 3e38, 0.0, ALU.mult, ALU.mult))
                dve.tensor_tensor(kq[:], kr[:], kv[:], ALU.add).then_inc(kq_ready, 1)
                own.link(dve, dve.tensor_scalar(vth[:], vth[:], 0.1, -5.0, ALU.max, ALU.mult))
                dve.tensor_copy(vbias[:], vth[:]).then_inc(vbias_ready, 1)
                own.link(dve, dve.tensor_tensor(both[:], scales[:, 0:1], scales[:, 1:2], ALU.mult))
                own.link(dve, dve.tensor_scalar(bad[:], xmax[:], rscale[:, 0:1], None, ALU.mult))
                own.link(dve, dve.tensor_tensor(bad[:], bad[:], bad[:], ALU.mult))
                own.link(dve, dve.tensor_scalar(bad[:], bad[:], FP8_MAX_TIE ** 2, 3e38, ALU.is_gt, ALU.mult))
                own.n = own.per
                dve.tensor_scalar(bad[:], bad[:], 3e38, 0.0, ALU.mult, ALU.mult).then_inc(prep, 1)
                dve.wait_ge(prep, 1)
                dve.tensor_scalar(per_tok[:], bad[:], both[:, 0:1], None, ALU.add).then_inc(prep, 1)
                dve.wait_ge(prep, 2)
                for i, par in pairs(dve, NT):
                    dve.tensor_copy(tok[:], per_tok[:, bass.ds(i * SUB, SUB)]).then_inc(tok_ready, 1)
                    dve.wait_ge(loaded[par], (i - par) * 40 + 80)
                    dve.wait_ge(spike_ready, H * i + H)
                    dve.scalar_tensor_tensor(ysp[:], spike[:], 1.0, y[par][:], ALU.add, ALU.mult).then_inc(ysp_ready, 1)
                    dve.wait_ge(open_ready, i + 1)
                    dve.scalar_tensor_tensor(zsp[:], open_[:], 1.0, z[par][:], ALU.add, ALU.mult).then_inc(zsp_ready, 1)
                    dve.wait_ge(zsp_ready, i + 1)
                    dve.wait_ge(ysp_ready, i + 1)
                    dve.wait_ge(o_psum, i)
                    dve.scalar_tensor_tensor(a[par][:], ysp[:], 0.25, zsp[:], ALU.mult, ALU.mult).then_inc(a_ready, 1)
                    dve.wait_ge(g_psum, i + 1)
                    dve.wait_ge(tok_ready, i + 1)
                    for k in range(SUB):
                        dve.tensor_scalar(g0[:, k, :], psG[par][:, k, :], tok[:, k:k + 1], None, ALU.mult).then_inc(g0_ready, 1)
                    dve.wait_ge(g0_ready, SUB * i + SUB)
                    dve.tensor_tensor(g1[:], g0[:], bias[:].rearrange("p (a d) -> p a d", a=1).to_broadcast([P, SUB, D]), ALU.add).then_inc(g1_ready, 1)
                    dve.wait_ge(gs_ready, i + 1)
                    dve.tensor_scalar(gden[:], gs[:], 1.0, None, ALU.add).then_inc(gden_ready, 1)
                    dve.wait_ge(gden_ready, i + 1)
                    with nc.allow_low_precision(reason="the reference rounds to bfloat16 here"):
                        dve.reciprocal(grec[:], gden[:]).then_inc(grec_ready, 1)
                    dve.wait_ge(grec_ready, i + 1)
                    dve.tensor_tensor(g[:], g1[:], grec[:], ALU.mult).then_inc(step, 1)
                    dve.wait_ge(o_psum, i + 1)
                    dve.tensor_tensor(s[:], psO[par][:], xn[par][:], ALU.subtract).then_inc(step, 1)
                    dve.wait_ge(step, 3 * i + 2)
                    dve.tensor_tensor(sg[:], s[:], g[:], ALU.mult).then_inc(step, 1)
                    dve.wait_ge(step, 3 * i + 3)
                    dve.wait_ge(x1_st, 16 * i)
                    dve.tensor_tensor(x1[par][:], sg[:], x[par][:], ALU.add).then_inc(x1_ready, 1)
                    dve.wait_ge(x1_ready, i + 1)


class Stages:

    def __init__(self, sem, *names):
        self.sem, self.names, self.at = sem, names, 0

    def done(self, ins, name):
        assert self.names[self.at % len(self.names)] == name, (self.names[self.at % len(self.names)], name)
        self.at += 1
        ins.then_inc(self.sem, 1)

    def wait(self, eng, turn, name):
        eng.wait_ge(self.sem, turn * len(self.names) + (self.names.index(name) + 1))

    def wait_before(self, eng, turn):
        eng.wait_ge(self.sem, turn * len(self.names))


def over_chunks(ap, n=SUB):
    return ap.rearrange("p (a d) -> p a d", a=1).to_broadcast([P, n, ap.shape[-1]])


def delta_inputs(nc, A):
    TOK = 3 * C + 2
    with ExitStack() as ctx:
        m = Memory(nc, ctx, "di")
        wtok, btok = m.sb("wtok", [P, H, TOK]), m.sb("btok", [P, TOK])
        wg, bg = m.sb("wg", [P, H, C]), m.sb("bg", [P, 1])
        fq, fk, fv = m.sb("fq", [P, H, P]), m.sb("fk", [P, H, P]), m.sb("fv", [P, H, P])
        fqb, fkb, fvb = m.sb("fqb", [P, 1]), m.sb("fkb", [P, 1]), m.sb("fvb", [P, P])
        fqs = m.sb("fqs", [P, 1])
        ident, half = m.sb("ident", [P, P]), m.sb("half", [P, SUB])
        x = [m.sb(f"x{k}", [P, SUB, D]) for k in range(2)]
        xn = [m.sb(f"xn{k}", [P, SUB, D]) for k in range(2)]
        stats, mv = m.sb("stats", [P, SUB, 6]), m.sb("mv", [P, SUB, 2])
        ve, rstd = m.sb("ve", [P, SUB]), m.sb("rstd", [P, SUB])
        xnT = [m.sb(f"xnT{k}", [P, H, TILE]) for k in range(2)]
        tok = [m.sb(f"tok{k}", [P, SUB, TOK]) for k in range(2)]
        square, ss, rk = m.sb("square", [P, C]), m.sb("ss", [P, SUB]), m.sb("rk", [P, SUB])
        khat, gate, vf = m.sb("khat", [P, SUB, C]), m.sb("gate", [P, TILE]), m.sb("vf", [P, SUB, P])
        qk, rest = m.sb("qk", [P, 2, TILE]), m.sb("rest", [P, 2, 2, TILE])
        part = m.sb("part", [P, 3, 2, TILE], BF16)
        psT, psTok = m.ps("psT", [P, H, TILE]), m.ps("psTok", [P, 2, TILE])
        psV, psG, psQ, psK = (m.ps(n, [P, TILE]) for n in ("psV", "psG", "psQ", "psK"))
        weights, fqs_ready, ident_made, half_made = (m.sem(n) for n in ("weights", "fqs", "ident", "half"))
        loaded = [m.sem(f"loaded{k}") for k in range(2)]
        xn_st, khat_st, gate_st, vf_st, part_st = (m.sem(f"{n}_st") for n in ("xn", "khat", "gate", "vf", "part"))
        tok_st = [m.sem(f"tok_st{k}") for k in range(2)]
        pe_front, act_front = Stages(m.sem("pe_front"), "xT"), Stages(m.sem("act_front"), "xnT")
        dve_front, pool_front = Stages(m.sem("dve_front"), "stats", "var", "xn"), Stages(m.sem("pool_front"), "ve", "rstd")
        pe_at = Stages(m.sem("pe_at"), "tok01", "gate", "fq", "fk", "fv", "tok23")
        dve_own, khat_own, square_done = m.sem("dve_own"), m.sem("khat_own"), m.sem("square_done")
        dve_at = Stages(m.sem("dve_at"), "tok01", "vf", "tok23")
        dve_khat = Stages(m.sem("dve_khat"), "khat")
        act_qk = Stages(m.sem("act_qk"), "gate", "fq", "fk")
        act_at = Stages(m.sem("act_at"), "part0", "ss", "part1", "part2")
        pool_at = Stages(m.sem("pool_at"), "rest0", "rk0", "rk", "rest1")

        def rows(name, i):
            return A[name].rearrange("(i s p) d -> i p s d", p=P, s=SUB)[i, :, :, :]

        with nc.Block() as block:
            @block.sync
            def _(sp):
                with nc.allow_non_contiguous_dma(reason="small"):
                    for dst, src in ((wtok[:], halves(A["w_tok"])), (btok[:], spread(A["b_tok"], TOK)),
                                     (wg[:], halves(A["w_gate"])), (bg[:], A["b_gate"].rearrange("(p a) -> p a", a=1)),
                                     (fq[:], halves(A["fq"])), (fk[:], halves(A["fk"])), (fv[:], halves(A["fv"])),
                                     (fqb[:], A["fqb"].rearrange("(p a) -> p a", a=1)),
                                     (fkb[:], A["fkb"].rearrange("(p a) -> p a", a=1)), (fvb[:], spread(A["fvb"], P))):
                        sp.dma_start(dst, src).then_inc(weights, 16)

                def load(i, par):
                    sp.dma_start(x[par][:], rows("x1", i)).then_inc(loaded[par], 16)

                def front(i, par, loads=True):
                    dve_front.wait(sp, i, "xn")
                    m.settle(sp)
                    sp.dma_start(rows("xn1", i), xn[par][:]).then_inc(xn_st, 16)
                    if loads:
                        load(i + 2, par)

                def step(i, par, more):
                    if more:
                        front(i + 1, 1 - par, not isinstance(i, int) or i + 3 < NT)
                    dve_khat.wait(sp, i, "khat")
                    m.settle(sp)
                    sp.dma_start(rows("vf", i), vf[:]).then_inc(vf_st, 16)
                    sp.dma_start(rows("qd", i), tok[par][:, :, 0:C]).then_inc(tok_st[par], 16)
                    sp.dma_start(rows("vd", i), tok[par][:, :, 2 * C:3 * C]).then_inc(tok_st[par], 16)
                    sp.dma_start(A["ab"].rearrange("p (i s) c -> i p s c", s=SUB)[i, :, :, :],
                                 tok[par][:, :, 3 * C:TOK]).then_inc(tok_st[par], 16)
                    sp.dma_start(rows("kd", i), khat[:]).then_inc(khat_st, 16)

                load(0, 0)
                load(1, 1)
                front(0, 0)
                with sp.Fori(0, NT // 2 - 2) as turn:
                    for par in range(2):
                        step(turn * 2 + par, par, True)
                for i in range(NT - 4, NT):
                    step(i, i % 2, i < NT - 1)
                for sem, n in ((xn_st, NT), (tok_st[0], 3 * NT // 2), (tok_st[1], 3 * NT // 2), (khat_st, NT), (gate_st, NT),
                               (vf_st, NT), (part_st, 2 * (NH // 4) * NT)):
                    sp.wait_ge(sem, 16 * n)
                    m.settle(sp)

            @block.gpsimd
            def _(pool):
                identity(nc, pool, ident, ident_made)
                pool.memset(half[:], -0.5).then_inc(half_made, 1)
                pool.wait_ge(half_made, 1)

                def front(i):
                    dve_front.wait(pool, i, "var")
                    m.settle(pool)
                    pool_front.done(pool.tensor_scalar_add(ve[:], mv[:, :, 1], EPS), "ve")
                    pool_front.wait(pool, i, "ve")
                    pool_front.done(pool.tensor_tensor(rstd[:], ve[:], half[:], ALU.pow), "rstd")

                def step(i, par, more):
                    if more:
                        dve_front.wait(pool, i, "xn")
                        front(i + 1)
                    act_at.wait(pool, i, "part0")
                    dve_khat.wait_before(pool, i)
                    pool_at.done(pool.tensor_tensor(rest[:, 0, :, :], qk[:], part[:, 0, :, :], ALU.subtract), "rest0")
                    act_at.wait(pool, i, "ss")
                    pool_at.done(pool.tensor_tensor(rk[:], ss[:], half[:], ALU.pow), "rk0")
                    pool_at.wait(pool, i, "rk0")
                    m.settle(pool)
                    pool_at.done(pool.tensor_scalar_min(rk[:], rk[:], 1e12), "rk")
                    act_at.wait(pool, i, "part1")
                    pool_at.done(pool.tensor_tensor(rest[:, 1, :, :], rest[:, 0, :, :], part[:, 1, :, :], ALU.subtract), "rest1")

                front(0)
                one_ahead(pool, step)

            @block.scalar
            def _(act):
                act.wait_ge(fqs_ready, 1)
                act.wait_ge(weights, 160)
                def front(i, par):
                    pe_front.wait(act, i, "xT")
                    act_front.done(act.activation(xnT[par][:], psT[:], ACT.Copy), "xnT")

                def step(b, par, more=True):
                    i = b * 2 + par
                    pe_at.wait(act, i, "gate")
                    act.wait_ge(gate_st, 16 * i)
                    act_qk.done(act.activation(gate[:], psG[:], ACT.Sigmoid, bias=bg[:, 0:1]), "gate")
                    act_qk.wait(act, i, "gate")
                    act.dma_start(A["gate_t"].rearrange("c (i t) -> i c t", t=TILE)[i, :, :], gate[:]).then_inc(gate_st, 16)
                    pe_at.wait(act, i, "fq")
                    pool_at.wait_before(act, i)
                    act_qk.done(act.activation(qk[:, 0, :], psQ[:], ACT.Identity, bias=fqs[:, 0:1], scale=float(HD) ** -0.5), "fq")
                    pe_at.wait(act, i, "fk")
                    act_qk.done(act.activation(qk[:, 1, :], psK[:], ACT.Identity, bias=fkb[:, 0:1]), "fk")
                    act_qk.wait(act, i, "fk")
                    act.wait_ge(part_st, 2 * (NH // 4) * 16 * i)
                    act_at.done(act.activation(part[:, 0, :, :], qk[:], ACT.Copy), "part0")
                    if more:
                        front(i + 1, 1 - par)
                    dve_at.wait(act, i, "tok23")
                    for s in range(SUB):
                        if s:
                            act.wait_ge(square_done, i * (SUB - 1) + s)
                        ins = act.activation(square[:], tok[par][:, s, C:2 * C], ACT.Square, accum_out=ss[:, s:s + 1])
                        if s < SUB - 1:
                            ins.then_inc(square_done, 1)
                        else:
                            act_at.done(ins, "ss")
                    pool_at.wait(act, i, "rest0")
                    act_at.done(act.activation(part[:, 1, :, :], rest[:, 0, :, :], ACT.Copy), "part1")
                    pool_at.wait(act, i, "rest1")
                    act_at.done(act.activation(part[:, 2, :, :], rest[:, 1, :, :], ACT.Copy), "part2")
                    act_at.wait(act, i, "part2")
                    for n, name in enumerate(("qs", "ks")):
                        for j in range(NH // 4):
                            dst = A[name].rearrange("b j k q (s t) -> b j s q k t", t=TILE)[b, j, par, :, :, :]
                            act.dma_start(dst, part[j * 32:(j + 1) * 32, :, n, :]).then_inc(part_st, 16)

                front(0, 0)
                with act.Fori(0, B - 1) as b:
                    for par in range(T // TILE):
                        step(b, par)
                step(B - 1, 0)
                step(B - 1, 1, False)

            @block.tensor
            def _(pe):
                pe.wait_ge(ident_made, 2)
                pe.wait_ge(weights, 160)

                def front(i, par):
                    dve_front.wait(pe, i, "xn")
                    act_front.wait_before(pe, i)
                    for s in range(SUB):
                        for h in range(H):
                            last = pe.transpose(psT[:, h, s * P:(s + 1) * P], xn[par][:, s, h * P:(h + 1) * P], ident[:])
                    pe_front.done(last, "xT")

                def step(i, par, more):
                    act_front.wait(pe, i, "xnT")
                    act_qk.wait_before(pe, i)

                    def tokens(dst, weight, s):
                        for h in range(H):
                            out = pe.matmul(dst, xnT[par][:, h, s * P:(s + 1) * P], weight[:, h, :], start=(h == 0), stop=(h == H - 1))
                        return out

                    def features(dst, weight):
                        for h in range(H):
                            out = pe.matmul(dst, weight[:, h, :], xnT[par][:, h, :], start=(h == 0), stop=(h == H - 1))
                        return out

                    dve_at.wait_before(pe, i)
                    tokens(psTok[:, 0, 0:TOK], wtok, 0)
                    pe_at.done(tokens(psTok[:, 1, 0:TOK], wtok, 1), "tok01")
                    pe_at.done(features(psG[:], wg), "gate")
                    pe_at.done(features(psQ[:], fq), "fq")
                    pe_at.done(features(psK[:], fk), "fk")
                    for s in range(SUB):
                        last = tokens(psV[:, s * P:(s + 1) * P], fv, s)
                    pe_at.done(last, "fv")
                    if more:
                        front(i + 1, 1 - par)
                    dve_at.wait(pe, i, "tok01")
                    tokens(psTok[:, 0, 0:TOK], wtok, 2)
                    pe_at.done(tokens(psTok[:, 1, 0:TOK], wtok, 3), "tok23")

                front(0, 0)
                one_ahead(pe, step)

            @block.vector
            def _(dve):
                own, khat_chain = Chain(dve_own, 3 * (SUB - 1)), Chain(khat_own, SUB - 1)
                dve.wait_ge(weights, 160)
                dve.tensor_scalar(fqs[:], fqb[:], float(HD) ** -0.5, None, ALU.mult).then_inc(fqs_ready, 1)

                def variance(i, par):
                    own.begin(i)
                    dve.wait_ge(loaded[par], (i - par) * 8 + 16)
                    for s in range(SUB):
                        ins = dve.bn_stats(stats[:, s, :], x[par][:, s, :])
                        own.mark(ins) if s < SUB - 1 else dve_front.done(ins, "stats")
                    own.wait(dve)
                    dve_front.wait(dve, i, "stats")
                    pool_front.wait_before(dve, i)
                    for s in range(SUB):
                        m.settle(dve)
                        ins = dve.bn_aggr(mv[:, s, :], stats[:, s, :])
                        own.mark(ins) if s < SUB - 1 else dve_front.done(ins, "var")
                    own.wait(dve)

                def normalise(i, par):
                    own.base, own.n = i * own.per, 2 * (SUB - 1)
                    dve_front.wait(dve, i, "var")
                    pool_front.wait(dve, i, "rstd")
                    pe_front.wait_before(dve, i)
                    dve.wait_ge(xn_st, 16 * i)
                    for s in range(SUB):
                        ins = dve.tensor_scalar(xn[par][:, s, :], x[par][:, s, :], mv[:, s, 0:1], rstd[:, s:s + 1],
                                                ALU.subtract, ALU.mult)
                        own.mark(ins) if s < SUB - 1 else dve_front.done(ins, "xn")
                    own.end()

                def step(i, par, more):
                    pe_at.wait(dve, i, "tok01")
                    dve.wait_ge(tok_st[par], (i - par) * 24)
                    dve_at.done(dve.tensor_tensor(tok[par][:, 0:2, :], psTok[:, :, 0:TOK], over_chunks(btok[:], 2), ALU.add), "tok01")
                    if more:
                        normalise(i + 1, 1 - par)
                    pe_at.wait(dve, i, "fv")
                    dve.wait_ge(vf_st, 16 * i)
                    dve_at.done(dve.tensor_tensor(vf[:], psV[:].rearrange("p (s c) -> p s c", s=SUB), over_chunks(fvb[:]), ALU.add), "vf")
                    pe_at.wait(dve, i, "tok23")
                    dve_at.done(dve.tensor_tensor(tok[par][:, 2:4, :], psTok[:, :, 0:TOK], over_chunks(btok[:], 2), ALU.add), "tok23")
                    if more and not (isinstance(i, int) and i == NT - 2):
                        variance(i + 2, par)
                    pool_at.wait(dve, i, "rk")
                    dve.wait_ge(khat_st, 16 * i)
                    khat_chain.begin(i)
                    for s in range(SUB):
                        ins = dve.tensor_scalar(khat[:, s, :], tok[par][:, s, C:2 * C], rk[:, s:s + 1], None, ALU.mult)
                        khat_chain.mark(ins) if s < SUB - 1 else dve_khat.done(ins, "khat")
                    khat_chain.end()
                    khat_chain.wait(dve)

                variance(0, 0)
                normalise(0, 0)
                variance(1, 1)
                one_ahead(dve, step)


def delta_invert(nc, A):
    with ExitStack() as ctx:
        m = Memory(nc, ctx, "dv")
        ident, ones, tri, strict = (m.sb(n, [P, P]) for n in ("ident", "ones", "tri", "strict"))
        same = [m.sb(f"same{w}", [P, P]) for w in (16, 32, 64)]
        ring = [m.sb(f"ring{k}", [P, P]) for k in range(3)]
        ab = m.sb("ab", [P, NP, 2])
        mag, soft, la, be = (m.sb(n, [P, NP]) for n in ("mag", "soft", "la", "be"))
        g, gl, diff, dw = (m.sb(n, [P, NP]) for n in ("g", "gl", "diff", "dw"))
        dec = m.sb("dec", [P, NP, NDEC])
        W = [P, SUB, P]
        two = range(2)
        kd, qd, qg, c4 = ([m.sb(f"{n}{k}", W) for k in two] for n in ("kd", "qd", "qg", "c4"))
        col = [m.sb(f"col{k}", [P, SUB, NDEC]) for k in two]
        tl, df, dd, ds, dm = ([m.sb(f"{n}{k}", W) for k in two] for n in ("tl", "df", "dd", "ds", "dm"))
        kt, qt, qgt = ([m.sb(f"{n}{k}", W) for k in two] for n in ("kt", "qt", "qgt"))
        nf, ntf, nb, ntb = ([m.sb(f"{n}{k}", W) for k in two] for n in ("nf", "ntf", "nb", "ntb"))
        nto = [[m.sb(f"nto{k}{l}", W) for l in range(3)] for k in two]
        n2, n2t, n4, n4t, n8t = ([m.sb(f"{n}{k}", W) for k in two] for n in ("n2", "n2t", "n4", "n4t", "n8t"))
        z, xt = ([m.sb(f"{n}{k}", W) for k in two] for n in ("z", "xt"))
        X = [[m.sb(f"X{k}{l}", W) for l in range(2)] for k in two]
        ps = [[m.ps(f"ps{k}{l}", W) for l in range(4)] for k in two]
        loaded = [m.sem(f"loaded{k}") for k in two]
        ab_in, masks, pre_act, pre_dve, pre_pe = (m.sem(n) for n in ("ab_in", "masks", "pre_act", "pre_dve", "pre_pe"))
        own = [m.sem(f"own{k}") for k in two]
        act_own = [m.sem(f"act_own{k}") for k in two]
        st = [m.sem(f"st{k}") for k in two]
        dec_st = m.sem("dec_st")
        pe_at = [Stages(m.sem(f"pe_at{k}"), "kT", "qT", "gbc", "gram", "qgT", "nT", "n2", "n2t", "x1", "n4", "n4t", "x2", "n8t", "x3",
                        "z0", "xt0", "y0", "z1", "xt1", "y1", "z2", "xt2", "y2") for k in two]
        act_at = [Stages(m.sem(f"act_at{k}"), "qg", "qt", "dd", "qgt", "ntf", "n2", "n4", "n8t", "z0", "z1", "z2") for k in two]
        dve_at = [Stages(m.sem(f"dve_at{k}"), "col", "tl", "kt", "df", "nf", "nb", "x0", "ntb", "n2t", "x1", "n4t", "x2", "x3",
                         "xt0", "y0", "xt1", "y1", "xt2", "y2") for k in two]
        pool_at = [Stages(m.sem(f"pool_at{k}"), "ds", "dm", "nto0", "nto1", "nto2") for k in two]

        def rows(name, i):
            return A[name].rearrange("(i s p) d -> i p s d", p=P, s=SUB)[i, :, :, :]

        def mats(name, i):
            return A[name].rearrange("(i s) p d -> i p s d", s=SUB)[i, :, :, :]

        with nc.Block() as block:
            @block.sync
            def _(sp):
                sp.dma_start(ab[:], A["ab"]).then_inc(ab_in, 16)
                with sp.Fori(0, NT // 2) as turn:
                    for par in two:
                        i = turn * 2 + par
                        dve_at[par].wait_before(sp, turn)
                        m.settle(sp)
                        pe_at[par].wait_before(sp, turn)
                        m.settle(sp)
                        act_at[par].wait_before(sp, turn)
                        m.settle(sp)
                        sp.dma_start(kd[par][:], rows("kd", i)).then_inc(loaded[par], 16)
                        sp.dma_start(qd[par][:], rows("qd", i)).then_inc(loaded[par], 16)
                for par in two:
                    sp.wait_ge(st[par], 80 * (NT // 2))
                    m.settle(sp)
                sp.wait_ge(dec_st, 16)

            @block.gpsimd
            def _(pool):
                pool.memset(ones[:], 1.0).then_inc(masks, 1)
                pool.memset(ident[:], 0.0).then_inc(masks, 1)
                for t_ in same:
                    pool.memset(t_[:], 1.0).then_inc(masks, 1)
                pool.wait_ge(masks, 5)
                pool.affine_select(out=ident[:], in_=ident[:], compare_op=ALU.not_equal, fill=1.0, base=0,
                                   pattern=[[-1, P]], channel_multiplier=1).then_inc(masks, 1)
                pool.affine_select(out=tri[:], in_=ones[:], compare_op=ALU.is_ge, fill=0.0, base=0,
                                   pattern=[[1, P]], channel_multiplier=-1).then_inc(masks, 1)
                pool.affine_select(out=strict[:], in_=ones[:], compare_op=ALU.is_ge, fill=0.0, base=-1,
                                   pattern=[[1, P]], channel_multiplier=-1).then_inc(masks, 1)
                for w, t_ in zip((16, 32, 64), same):
                    view = t_[:].rearrange("p (n w) -> p n w", w=w)
                    pool.affine_select(out=view, in_=view, compare_op=ALU.is_ge, fill=0.0, base=0,
                                       pattern=[[-w, P // w], [0, w]], channel_multiplier=1).then_inc(masks, 1)
                pool.wait_ge(masks, 11)
                for w, t_ in zip((16, 32, 64), same):
                    view = t_[:].rearrange("p (n w) -> p n w", w=w)
                    pool.affine_select(out=view, in_=view, compare_op=ALU.is_ge, fill=0.0, base=w - 1,
                                       pattern=[[w, P // w], [0, w]], channel_multiplier=-1).then_inc(masks, 1)
                pool.wait_ge(masks, 14)
                wide = [same[1], same[2], ones]
                for k in range(3):
                    pool.tensor_tensor(ring[k][:], wide[k][:], same[k][:], ALU.subtract).then_inc(masks, 1)
                pool.wait_ge(masks, 17)
                pool.wait_ge(pre_dve, 10)
                m.settle(pool)
                pool.dma_start(A["dec"], dec[:]).then_inc(dec_st, 16)
                with pool.Fori(0, NT // 2) as turn:
                    for par in two:
                        act_at[par].wait(pool, turn, "dd")
                        dve_at[par].wait_before(pool, turn)
                        pool.wait_ge(st[par], turn * 80)
                        pool_at[par].done(pool.tensor_tensor(ds[par][:], dd[par][:], over_chunks(strict[:]), ALU.mult), "ds")
                        pool_at[par].wait(pool, turn, "ds")
                        pool_at[par].done(pool.tensor_tensor(dm[par][:], ds[par][:], over_chunks(ident[:]), ALU.add), "dm")
                    for par in two:
                        act_at[par].wait(pool, turn, "ntf")
                        pe_at[par].wait_before(pool, turn)
                        for l in range(3):
                            pool_at[par].done(pool.tensor_tensor(nto[par][l][:], ntf[par][:], over_chunks(ring[l][:]), ALU.mult), f"nto{l}")
                    for par in two:
                        i = turn * 2 + par
                        act_at[par].wait(pool, turn, "qgt")
                        dve_at[par].wait(pool, turn, "kt")
                        pool_at[par].wait(pool, turn, "dm")
                        m.settle(pool)
                        pool.dma_start(mats("dm", i), dm[par][:]).then_inc(st[par], 16)
                        m.settle(pool)
                        pool.dma_start(mats("kt", i), kt[par][:]).then_inc(st[par], 16)
                        m.settle(pool)
                        pool.dma_start(mats("qt", i), qt[par][:]).then_inc(st[par], 16)
                        m.settle(pool)
                        pool.dma_start(mats("qgt", i), qgt[par][:]).then_inc(st[par], 16)
                    for par in two:
                        dve_at[par].wait(pool, turn, "y2")
                        m.settle(pool)
                        pool.dma_start(mats("inv", turn * 2 + par), X[par][0][:]).then_inc(st[par], 16)

            @block.scalar
            def _(act):
                act.wait_ge(ab_in, 16)
                act.activation(mag[:], ab[:, :, 0], ACT.Abs).then_inc(pre_act, 1)
                act.wait_ge(pre_act, 1)
                act.activation(mag[:], mag[:], ACT.Exp, scale=-1.0).then_inc(pre_act, 1)
                act.activation(be[:], ab[:, :, 1], ACT.Exp, scale=-1.0).then_inc(pre_act, 1)
                act.wait_ge(pre_act, 2)
                act.activation(soft[:], mag[:], ACT.Ln, bias=1.0).then_inc(pre_act, 1)
                act.wait_ge(pre_dve, 5)
                act.activation(dec[:, :, EXP_G], g[:], ACT.Exp).then_inc(pre_act, 1)
                act.activation(dec[:, :, EXP_END], gl[:], ACT.Exp).then_inc(pre_act, 1)
                act.activation(dw[:], diff[:], ACT.Exp).then_inc(pre_act, 1)
                with act.Fori(0, NT // 2) as turn:
                    for par in two:
                        act.wait_ge(loaded[par], turn * 32 + 32)
                        dve_at[par].wait(act, turn, "col")
                        pe_at[par].wait_before(act, turn)
                        act.wait_ge(st[par], turn * 80)
                        for s in range(SUB):
                            ins = act.activation(qg[par][:, s, :], qd[par][:, s, :], ACT.Copy, scale=col[par][:, s, EXP_G:EXP_G + 1])
                            if s < SUB - 1:
                                ins.then_inc(act_own[par], 1)
                        act.wait_ge(act_own[par], turn * (SUB - 1) + SUB - 1)
                        act_at[par].done(ins, "qg")
                    for par in two:
                        pe_at[par].wait(act, turn, "qT")
                        act_at[par].done(act.activation(qt[par][:], ps[par][1][:], ACT.Copy), "qt")
                    for par in two:
                        dve_at[par].wait(act, turn, "df")
                        pool_at[par].wait_before(act, turn)
                        act_at[par].done(act.activation(dd[par][:], df[par][:], ACT.Exp), "dd")
                    for par in two:
                        pe_at[par].wait(act, turn, "qgT")
                        act_at[par].done(act.activation(qgt[par][:], ps[par][2][:], ACT.Copy), "qgt")
                    for par in two:
                        pe_at[par].wait(act, turn, "nT")
                        dve_at[par].wait_before(act, turn)
                        act_at[par].done(act.activation(ntf[par][:], ps[par][1][:], ACT.Copy), "ntf")
                    for name, dst, bank in (("n2", n2, 0), ("n4", n4, 3), ("n8t", n8t, 1)):
                        for par in two:
                            pe_at[par].wait(act, turn, name)
                            act_at[par].done(act.activation(dst[par][:], ps[par][bank][:], ACT.Copy), name)
                    for l in range(3):
                        for par in two:
                            pe_at[par].wait(act, turn, f"z{l}")
                            act_at[par].done(act.activation(z[par][:], ps[par][3][:], ACT.Copy), f"z{l}")

            @block.tensor
            def _(pe):
                pe.wait_ge(masks, 17)
                pe.wait_ge(pre_dve, 2)
                pe.matmul(ps[0][0][:, 0, 0:NP], tri[:], la[:], start=True, stop=True).then_inc(pre_pe, 1)
                pe.matmul(ps[0][1][:, 0, 0:NP], ones[:], la[:], start=True, stop=True).then_inc(pre_pe, 1)
                pe.wait_ge(pre_dve, 5)

                def each(par, bank, left, right, name):
                    for s in range(SUB):
                        out = pe.matmul(ps[par][bank][:, s, :], left[:, s, :], right[:, s, :], start=True, stop=True)
                    pe_at[par].done(out, name)

                def turned(par, bank, src, name):
                    for s in range(SUB):
                        out = pe.transpose(ps[par][bank][:, s, :], src[:, s, :], ident[:])
                    pe_at[par].done(out, name)

                with pe.Fori(0, NT // 2) as turn:
                    for par in two:
                        pe.wait_ge(loaded[par], turn * 32 + 32)
                        dve_at[par].wait_before(pe, turn)
                        act_at[par].wait_before(pe, turn)
                        turned(par, 0, kd[par], "kT")
                        turned(par, 1, qd[par], "qT")
                        dve_at[par].wait(pe, turn, "tl")
                        pe_at[par].done(pe.matmul(ps[par][3][:], ones[:], tl[par][:], start=True, stop=True), "gbc")
                    for par in two:
                        dve_at[par].wait(pe, turn, "kt")
                        each(par, 0, kt[par], kt[par], "gram")
                        act_at[par].wait(pe, turn, "qg")
                        turned(par, 2, qg[par], "qgT")
                    for par in two:
                        dve_at[par].wait(pe, turn, "nf")
                        act_at[par].wait(pe, turn, "qt")
                        turned(par, 1, nf[par], "nT")
                    for par in two:
                        dve_at[par].wait(pe, turn, "ntb")
                        each(par, 0, ntb[par], nb[par], "n2")
                        act_at[par].wait(pe, turn, "ntf")
                        each(par, 1, nb[par], ntb[par], "n2t")
                    for par in two:
                        dve_at[par].wait(pe, turn, "n2t")
                        act_at[par].wait(pe, turn, "n2")
                        each(par, 2, n2t[par], X[par][0], "x1")
                        each(par, 3, n2t[par], n2[par], "n4")
                        each(par, 0, n2[par], n2t[par], "n4t")
                    for par in two:
                        dve_at[par].wait(pe, turn, "n4t")
                        act_at[par].wait(pe, turn, "n4")
                        each(par, 2, n4t[par], X[par][1], "x2")
                        each(par, 1, n4[par], n4t[par], "n8t")
                    for par in two:
                        act_at[par].wait(pe, turn, "n8t")
                        dve_at[par].wait(pe, turn, "x2")
                        each(par, 2, n8t[par], X[par][0], "x3")
                    for l in range(3):
                        cur = (l + 1) % 2
                        for par in two:
                            dve_at[par].wait(pe, turn, "x3" if l == 0 else f"y{l - 1}")
                            pool_at[par].wait(pe, turn, f"nto{l}")
                            if l:
                                act_at[par].wait(pe, turn, f"z{l - 1}")
                            each(par, 3, nto[par][l], X[par][cur], f"z{l}")
                            turned(par, 1, X[par][cur], f"xt{l}")
                        for par in two:
                            act_at[par].wait(pe, turn, f"z{l}")
                            dve_at[par].wait(pe, turn, f"xt{l}")
                            each(par, 2, xt[par], z[par], f"y{l}")

            @block.vector
            def _(dve):
                dve.wait_ge(pre_act, 4)
                dve.scalar_tensor_tensor(out=la[:], in0=ab[:, :, 0], scalar=0.0, in1=soft[:], op0=ALU.min,
                                         op1=ALU.subtract).then_inc(pre_dve, 1)
                dve.tensor_scalar(be[:], be[:], 1.0, None, ALU.add).then_inc(pre_dve, 1)
                dve.wait_ge(pre_pe, 2)
                dve.tensor_copy(g[:], ps[0][0][:, 0, 0:NP]).then_inc(pre_dve, 1)
                dve.tensor_copy(gl[:], ps[0][1][:, 0, 0:NP]).then_inc(pre_dve, 1)
                dve.wait_ge(pre_dve, 4)
                dve.tensor_tensor(diff[:], gl[:], g[:], ALU.subtract).then_inc(pre_dve, 1)
                dve.reciprocal(dec[:, :, BETA], be[:]).then_inc(pre_dve, 1)
                dve.tensor_copy(dec[:, :, LOG_A], la[:]).then_inc(pre_dve, 1)
                dve.tensor_copy(dec[:, :, LOG_G], g[:]).then_inc(pre_dve, 1)
                dve.wait_ge(pre_act, 7)
                dve.tensor_scalar(dec[:, :, NEG_EXP_G], dec[:, :, EXP_G], -1.0, None, ALU.mult).then_inc(pre_dve, 1)
                dve.wait_ge(pre_dve, 6)
                dve.tensor_tensor(dec[:, :, TO_END_BETA], dw[:], dec[:, :, BETA], ALU.mult).then_inc(pre_dve, 1)
                dve.wait_ge(pre_dve, 10)
                dve.wait_ge(masks, 17)
                with dve.Fori(0, NT // 2) as turn:
                    def parts(par, op, count, name):
                        for s in range(SUB):
                            ins = op(s)
                            if s < SUB - 1:
                                ins.then_inc(own[par], 1)
                        dve.wait_ge(own[par], turn * 3 * (SUB - 1) + count * (SUB - 1))
                        dve_at[par].done(ins, name)

                    for par in two:
                        act_at[par].wait_before(dve, turn)
                        dve_at[par].done(dve.tensor_copy(col[par][:], dec[:, bass.ds((turn * 2 + par) * SUB, SUB), :]), "col")
                        dve_at[par].wait(dve, turn, "col")
                        pe_at[par].wait_before(dve, turn)
                        parts(par, lambda s: dve.tensor_scalar(tl[par][:, s, :], tri[:], col[par][:, s, LOG_A:LOG_A + 1], None, ALU.mult), 1, "tl")
                    for par in two:
                        pe_at[par].wait(dve, turn, "kT")
                        dve.wait_ge(st[par], turn * 80)
                        dve_at[par].done(dve.tensor_copy(kt[par][:], ps[par][0][:]), "kt")
                    for par in two:
                        pe_at[par].wait(dve, turn, "gbc")
                        parts(par, lambda s: dve.tensor_scalar(df[par][:, s, :], ps[par][3][:, s, :], col[par][:, s, LOG_G:LOG_G + 1],
                                                               0.0, ALU.subtract, ALU.min), 2, "df")
                    for par in two:
                        pe_at[par].wait(dve, turn, "gram")
                        pool_at[par].wait(dve, turn, "ds")
                        parts(par, lambda s: dve.scalar_tensor_tensor(
                            out=nf[par][:, s, :], in0=ps[par][0][:, s, :], scalar=col[par][:, s, BETA:BETA + 1],
                            in1=ds[par][:, s, :], op0=ALU.mult, op1=ALU.mult), 3, "nf")
                        dve_at[par].wait(dve, turn, "nf")
                        dve_at[par].done(dve.tensor_tensor(nb[par][:], nf[par][:], over_chunks(same[0][:]), ALU.mult), "nb")
                        dve_at[par].wait(dve, turn, "nb")
                        dve_at[par].done(dve.tensor_tensor(X[par][0][:], over_chunks(ident[:]), nb[par][:], ALU.subtract), "x0")
                    for par in two:
                        act_at[par].wait(dve, turn, "ntf")
                        dve_at[par].done(dve.tensor_tensor(ntb[par][:], ntf[par][:], over_chunks(same[0][:]), ALU.mult), "ntb")
                    for par in two:
                        pe_at[par].wait(dve, turn, "n2t")
                        dve_at[par].done(dve.tensor_copy(n2t[par][:], ps[par][1][:]), "n2t")
                    for k, (name, bank, last) in enumerate((("x1", 2, "n4t"), ("x2", 2, None), ("x3", 2, None))):
                        for par in two:
                            pe_at[par].wait(dve, turn, name)
                            dve_at[par].wait(dve, turn, "x0" if k == 0 else f"x{k}")
                            dve_at[par].done(dve.tensor_tensor(X[par][(k + 1) % 2][:], X[par][k % 2][:], ps[par][2][:], ALU.add), name)
                            if last:
                                pe_at[par].wait(dve, turn, last)
                                dve_at[par].done(dve.tensor_copy(n4t[par][:], ps[par][0][:]), last)
                    for l in range(3):
                        cur = (l + 1) % 2
                        for par in two:
                            pe_at[par].wait(dve, turn, f"xt{l}")
                            dve_at[par].done(dve.tensor_copy(xt[par][:], ps[par][1][:]), f"xt{l}")
                        for par in two:
                            pe_at[par].wait(dve, turn, f"y{l}")
                            dve_at[par].done(dve.tensor_tensor(X[par][1 - cur][:], X[par][cur][:], ps[par][2][:], ALU.subtract), f"y{l}")


def delta_chunks(nc, A):
    G = B // SUB
    Q = 2 * G
    TURNS = T // P // 2
    with ExitStack() as ctx:
        m = Memory(nc, ctx, "dc")
        W = [P, SUB, P]
        dec, wo, bo = m.sb("dec", [P, NP, NDEC]), m.sb("wo", [P, D]), m.sb("bo", [P, D])
        names = ("kd", "vd", "kt", "qt", "qgt", "inv", "dm", "gate")
        buf = {n: [m.sb(f"{n}{q}", W) for q in range(Q)] for n in names}
        state, stateT = ([m.sb(f"{n}{g}", W) for g in range(G)] for n in ("state", "stateT"))
        col = [m.sb(f"col{k}", [P, SUB, NDEC]) for k in range(Q)]
        r, wd, wt, am, og = (m.sb(n, W) for n in ("r", "wd", "wt", "am", "og"))
        out = [m.sb(f"out{k}", [P, SUB, D]) for k in range(2)]
        psK, psW, psWT, psA, psS, psO = (m.ps(n, W) for n in ("psK", "psW", "psWT", "psA", "psS", "psO"))
        psOut = m.ps("psOut", [P, SUB, D])
        weights, zeroed = m.sem("weights"), m.sem("zeroed")
        out_st = [m.sem(f"out_st{q}") for q in range(Q)]
        loaded = [m.sem(f"loaded{q}") for q in range(Q)]
        dve_own, act_own = m.sem("dve_own"), m.sem("act_own")
        pe_at = [Stages(m.sem(f"pe_at{q}"), "ks", "w", "wt", "a", "s", "st", "o", "out") for q in range(Q)]
        dve_at = [Stages(m.sem(f"dve_at{q}"), "col", "r", "wt", "am", "s", "st", "og", "out") for q in range(Q)]
        act_at = [Stages(m.sem(f"act_at{q}"), "wd") for q in range(Q)]

        def before(at, eng, turn, q, name):
            if q:
                at[q - 1].wait(eng, turn, name)
            else:
                at[Q - 1].wait_before(eng, turn)

        def place(name, c, g):
            if name == "gate":
                return A["gate_t"].rearrange("f (b c t) -> c f b t", b=B, t=P)[c, :, g * SUB:(g + 1) * SUB, :]
            if name in ("kd", "vd", "s1"):
                return A[name].rearrange("(b c p) d -> c p b d", b=B, p=P)[c, :, g * SUB:(g + 1) * SUB, :]
            return A[name].rearrange("(b c) p d -> c p b d", b=B)[c, :, g * SUB:(g + 1) * SUB, :]

        with nc.Block() as block:
            @block.sync
            def _(sp):
                sp.dma_start(dec[:], A["dec"]).then_inc(weights, 16)
                sp.dma_start(wo[:], A["w_o"]).then_inc(weights, 16)
                sp.dma_start(bo[:], spread(A["b_o"], D)).then_inc(weights, 16)
                with sp.Fori(0, TURNS) as turn:
                    for q in range(Q):
                        dve_at[q].wait_before(sp, turn)
                        m.settle(sp)
                        pe_at[q].wait_before(sp, turn)
                        m.settle(sp)
                        for n in names:
                            sp.dma_start(buf[n][q][:], place(n, turn * 2 + q // G, q % G)).then_inc(loaded[q], 16)
                for q in range(Q):
                    sp.wait_ge(out_st[q], 16 * TURNS)
                    m.settle(sp)

            @block.gpsimd
            def _(pool):
                for t_ in state + stateT:
                    pool.memset(t_[:], 0.0).then_inc(zeroed, 1)
                with pool.Fori(0, TURNS) as turn:
                    for q in range(Q):
                        dve_at[q].wait(pool, turn, "out")
                        m.settle(pool)
                        pool.dma_start(place("s1", turn * 2 + q // G, q % G), out[q % 2][:]).then_inc(out_st[q], 16)

            @block.scalar
            def _(act):
                with act.Fori(0, TURNS) as turn:
                    for q in range(Q):
                        pe_at[q].wait(act, turn, "w")
                        dve_at[q].wait(act, turn, "col")
                        before(pe_at, act, turn, q, "st")
                        for s in range(SUB):
                            ins = act.activation(wd[:, s, :], psW[:, s, :], ACT.Copy, scale=col[q][:, s, TO_END_BETA:TO_END_BETA + 1])
                            if s < SUB - 1:
                                ins.then_inc(act_own, 1)
                        act.wait_ge(act_own, (turn * Q + q + 1) * (SUB - 1))
                        act_at[q].done(ins, "wd")

            @block.tensor
            def _(pe):
                pe.wait_ge(weights, 48)
                pe.wait_ge(zeroed, 2 * G)

                def each(dst, left, right, **flags):
                    flags = flags or dict(start=True, stop=True)
                    for s in range(SUB):
                        last = pe.matmul(dst[:, s, :], left[:, s, :], right[:, s, :], **flags)
                    return last

                with pe.Fori(0, TURNS) as turn:
                    for q in range(Q):
                        g = q % G
                        pe.wait_ge(loaded[q], turn * 128 + 128)
                        if q >= G:
                            dve_at[q - G].wait(pe, turn, "st")
                        else:
                            dve_at[q + G].wait_before(pe, turn)
                        before(dve_at, pe, turn, q, "st")
                        pe_at[q].done(each(psK, buf["kt"][q], stateT[g]), "ks")
                        dve_at[q].wait(pe, turn, "r")
                        before(act_at, pe, turn, q, "wd")
                        pe_at[q].done(each(psW, buf["inv"][q], r), "w")
                        pe_at[q].done(each(psWT, r, buf["inv"][q]), "wt")
                        dve_at[q].wait(pe, turn, "wt")
                        pe_at[q].done(each(psA, wt, buf["qt"][q]), "a")
                        act_at[q].wait(pe, turn, "wd")
                        pe_at[q].done(each(psS, wd, buf["kd"][q]), "s")
                        pe_at[q].done(each(psK, buf["kd"][q], wd), "st")
                        dve_at[q].wait(pe, turn, "am")
                        for s in range(SUB):
                            pe.matmul(psO[:, s, :], state[g][:, s, :], buf["qgt"][q][:, s, :], start=True, stop=False)
                            last = pe.matmul(psO[:, s, :], buf["kd"][q][:, s, :], am[:, s, :], start=False, stop=True)
                        pe_at[q].done(last, "o")
                        dve_at[q].wait(pe, turn, "og")
                        before(dve_at, pe, turn, q, "out") if q == 0 else None
                        for s in range(SUB):
                            last = pe.matmul(psOut[:, s, :], og[:, s, :], wo[:], start=True, stop=True)
                        pe_at[q].done(last, "out")

            @block.vector
            def _(dve):
                dve.wait_ge(weights, 48)
                dve.wait_ge(zeroed, 2 * G)
                with dve.Fori(0, TURNS) as turn:
                    for q in range(Q):
                        g = q % G
                        count = [0]

                        def parts(op, name):
                            for s in range(SUB):
                                ins = op(s)
                                if s < SUB - 1:
                                    ins.then_inc(dve_own, 1)
                                    count[0] += 1
                            dve.wait_ge(dve_own, (turn * Q + q) * 4 * (SUB - 1) + count[0])
                            dve_at[q].done(ins, name)

                        view = dec[:].rearrange("p (b c) f -> p b c f", b=B)
                        c = turn * 2 + q // G
                        act_at[q].wait_before(dve, turn)
                        dve_at[q].done(dve.tensor_copy(col[q][:].rearrange("p b (a f) -> p b a f", a=1),
                                                       view[:, g * SUB:(g + 1) * SUB, bass.ds(c, 1), :]), "col")
                        dve.wait_ge(loaded[q], turn * 128 + 128)
                        pe_at[q].wait(dve, turn, "ks")
                        dve_at[q].wait(dve, turn, "col")
                        before(pe_at, dve, turn, q, "wt")

                        def scaled(dst, src, col_at, plus, op1=ALU.add):
                            return lambda s: dve.scalar_tensor_tensor(
                                out=dst[:, s, :], in0=src[:, s, :], scalar=col[q][:, s, col_at:col_at + 1],
                                in1=plus[:, s, :], op0=ALU.mult, op1=op1)

                        parts(scaled(r, psK, NEG_EXP_G, buf["vd"][q]), "r")
                        pe_at[q].wait(dve, turn, "wt")
                        dve_at[q].done(dve.tensor_copy(wt[:], psWT[:]), "wt")
                        pe_at[q].wait(dve, turn, "a")
                        parts(scaled(am, psA, BETA, buf["dm"][q], ALU.mult), "am")
                        pe_at[q].wait(dve, turn, "o")
                        parts(scaled(state[g], state[g], EXP_END, psS), "s")
                        parts(scaled(stateT[g], stateT[g], EXP_END, psK), "st")
                        dve_at[q].done(dve.tensor_tensor(og[:], psO[:], buf["gate"][q][:], ALU.mult), "og")
                        pe_at[q].wait(dve, turn, "out")
                        if q >= 2:
                            dve.wait_ge(out_st[q - 2], turn * 16 + 16)
                        else:
                            dve.wait_ge(out_st[q + 2], turn * 16)
                        dve_at[q].done(dve.tensor_tensor(out[q % 2][:], psOut[:], over_chunks(bo[:]), ALU.add), "out")


def attention(nc, A):
    QUAD = 4
    ROWS = 9 * HD
    MAXROW = 96
    ALL = MAXROW + 3
    NQ = NH // QUAD
    KC = T // P
    NHALF = T // TILE
    with ExitStack() as ctx:
        m = Memory(nc, ctx, "at")
        q4, k4 = ([m.sb(f"{n}{j}", [ALL, QUAD, T], BF16) for j in range(NQ)] for n in ("q4", "k4"))
        vraw = [m.sb(f"vraw{j}", [P, KC, QUAD * HD]) for j in range(NQ)]
        v4 = [m.sb(f"v4{j}", [P, KC, QUAD, 32]) for j in range(NQ)]
        ident = m.sb("ident", [P, P], BF16)
        half_max = m.sb("half_max", [P, QUAD, KC, NHALF])
        top = m.sb("top", [P, QUAD * KC])
        rest = m.sb("rest", [P, 2, QUAD * KC])
        top3 = m.sb("top3", [P, 4, QUAD * KC], BF16)
        topT = m.sb("topT", [P, P], BF16)
        probs = [m.sb(f"probs{j}", [P, 2, TILE]) for j in range(2 * QUAD)]
        sums = [m.sb(f"sums{j}", [P, TILE]) for j in range(NHALF)]
        psM = [m.ps(f"psM{j}", [P, TILE]) for j in range(2)]
        psS = [m.ps(f"psS{j}", [P, 2, TILE]) for j in range(2)]
        psT, psV = m.ps("psT", [P, P]), m.ps("psV", [P, TILE])
        ident_made, ready_made = m.sem("ident_made"), m.sem("ready_made")
        loaded = [m.sem(f"loaded{j}") for j in range(NQ)]
        top_in = [m.sem(f"top_in{j}") for j in range(NQ)]
        v_ready, scored, maxed = m.sem("v_ready"), m.sem("scored"), m.sem("maxed")
        top_at = Stages(m.sem("top_at"), "top", "part0", "rest0", "part1", "rest1", "part2")
        filled, turned, topT_ready = m.sem("filled"), m.sem("turned"), m.sem("topT_ready")
        keyed, probs_ready, summed, sums_ready = m.sem("keyed"), m.sem("probs_ready"), m.sem("summed"), m.sem("sums_ready")
        sums_st = [m.sem(f"sums_st{j}") for j in range(NHALF)]
        LOADS = 3 + 5 + 1
        TILES1 = QUAD * KC * NHALF
        TILES2 = NHALF * (KC // 2) * QUAD
        GROUPS = TILES2 // QUAD
        UNITS = B * NQ

        with nc.Block() as block:
            @block.sync
            def _(sp):
                def load(b, j):
                    for turned_by in range(3):
                        for name, buf, parts in (("qs", q4, (0, 3)), ("ks", k4, (turned_by, 3)), ("ks", k4, (0, turned_by))):
                            if parts[0] < parts[1]:
                                src = A[name][b, j, parts[0]:parts[1], :, :].rearrange("k (r h) t -> (k r) (h t)", h=QUAD)
                                first = turned_by * 3 + (0 if parts[1] == 3 else 3 - turned_by)
                                dst = buf[j][first * HD:(first + parts[1] - parts[0]) * HD, :, :]
                                sp.dma_start(dst.rearrange("n h t -> n (h t)"), src).then_inc(loaded[j], 16)
                    src = A["vf"].rearrange("(b c p) n -> b p c n", b=B, p=P)[b, :, :, j * QUAD * HD:(j + 1) * QUAD * HD]
                    sp.dma_start(vraw[j][:], src).then_inc(loaded[j], 16)

                for j in range(NQ):
                    sp.wait_ge(ready_made, 3 * j + 3)
                    m.settle(sp)
                    load(0, j)

                def sequence(b, final):
                    for j in range(NQ):
                        u = b * NQ + j
                        for half in range(NHALF):
                            sp.wait_ge(sums_ready, u * NHALF + half + 1)
                            m.settle(sp)
                            for h in range(QUAD):
                                dst = A["ao"].rearrange("h q (b s t) -> b h s q t", b=B, t=TILE)[b, j * QUAD + h, half, :, :]
                                sp.dma_start(dst, sums[half][32 * h:32 * h + 2 * HD, :]).then_inc(sums_st[half], 16)
                        if not final:
                            load(b + 1, j)

                with sp.Fori(0, B - 1) as b:
                    sequence(b, False)
                sequence(B - 1, True)
                for half in range(NHALF):
                    sp.wait_ge(sums_st[half], UNITS * QUAD * 16)
                    m.settle(sp)

            @block.gpsimd
            def _(pool):
                pool.memset(ident[:], 0.0).then_inc(ident_made, 1)
                pool.wait_ge(ident_made, 1)
                pool.affine_select(out=ident[:], in_=ident[:], compare_op=ALU.not_equal, fill=1.0, base=0,
                                   pattern=[[-1, P]], channel_multiplier=1).then_inc(ident_made, 1)
                pool.wait_ge(ident_made, 2)
                for j in range(NQ):
                    for n, (rows, value) in enumerate(((q4[j][64:96, :, :], 0.0), (k4[j][64:96, :, :], 0.0),
                                                       (k4[j][MAXROW:ALL, :, :], 1.0))):
                        pool.memset(rows, value).then_inc(ready_made, 1)
                        pool.wait_ge(ready_made, 3 * j + n + 1)
                for j in range(NQ):
                    pool.memset(v4[j][:], 0.0).then_inc(v_ready, 1)
                    pool.wait_ge(v_ready, 2 * j + 1)
                    pool.memset(v4[j][:, :, :, HD:2 * HD], 1.0).then_inc(v_ready, 1)
                    pool.wait_ge(v_ready, 2 * j + 2)
                with pool.Fori(0, B) as b:
                    for j in range(NQ):
                        pool.wait_ge(loaded[j], (b + 1) * 16 * LOADS)
                        pool.wait_ge(summed, (b * NQ + j) * GROUPS if j == 0 else (b * NQ + j) * GROUPS - GROUPS)
                        m.settle(pool)
                        pool.tensor_copy(v4[j][:, :, :, 0:HD], vraw[j][:].rearrange("p c (h r) -> p c h r", r=HD)).then_inc(v_ready, 1)

            LEAD = 12
            PER_STEP = TILES1 // TILES2
            TURN = (TILES1 - LEAD) // PER_STEP + 1

            def ahead(u, final, j, n):
                for k in range(LEAD + PER_STEP * n, LEAD + PER_STEP * (n + 1)):
                    d = 1 + k // TILES1
                    if not final or j + d < NQ:
                        yield u + d, (j + d) % NQ, k % TILES1

            @block.tensor
            def _(pe):
                pe.wait_ge(ident_made, 2)

                def maxima(u, j, t):
                    h, c, half = t // (KC * NHALF), t // NHALF % KC, t % NHALF
                    if t > 1:
                        pe.wait_ge(maxed, u * TILES1 + (t - 1))
                    elif not isinstance(u, int) or u:
                        pe.wait_ge(maxed, u * TILES1 + t - 1)
                    pe.matmul(psM[t % 2][:], q4[j][0:ROWS, h, c * P:(c + 1) * P],
                              k4[j][0:ROWS, h, half * TILE:(half + 1) * TILE], start=True, stop=True).then_inc(scored, 1)

                def turn(u):
                    top_at.wait(pe, u, "part2")
                    pe.wait_ge(topT_ready, u)
                    pe.matmul(psT[:], top3[:].rearrange("p k n -> p (k n)"), ident[:],
                              start=True, stop=True).then_inc(turned, 1)

                def second(u, j, g, h, between=()):
                    half, pair, n = g // (KC // 2), g % (KC // 2), g * QUAD + h
                    if n > 1:
                        pe.wait_ge(probs_ready, u * TILES2 + (n - 1))
                    elif not isinstance(u, int) or u:
                        pe.wait_ge(probs_ready, u * TILES2 + n - 1)
                    for k in range(2):
                        c = pair * 2 + k
                        last = pe.matmul(psS[h % 2][:, k, :], k4[j][:, h, c * P:(c + 1) * P],
                                         q4[j][:, h, half * TILE:(half + 1) * TILE], start=True, stop=True)
                        if k:
                            last.then_inc(keyed, 1)
                        for tile in between[k:k + 1]:
                            maxima(*tile)

                def values(u, j, g, k):
                    half, pair = g // (KC // 2), g % (KC // 2)
                    c = pair * 2 + k
                    pe.wait_ge(probs_ready, u * TILES2 + (g + 1) * QUAD)
                    if c == 0:
                        pe.wait_ge(sums_ready, u * NHALF + half)
                        pe.wait_ge(v_ready, 2 * NQ + u + 1)
                    for h in range(QUAD):
                        last = pe.matmul(psV[32 * h:32 * h + 32, :], v4[j][:, c, h, :], probs[(g % 2) * QUAD + h][:, k, :],
                                         start=(c == 0), stop=(c == KC - 1))
                    if k == 1:
                        last.then_inc(summed, 1)

                pe.wait_ge(loaded[0], 16 * LOADS)
                pe.wait_ge(loaded[1], 16 * LOADS)
                for t in range(TILES1):
                    maxima(0, 0, t)
                for t in range(LEAD):
                    maxima(1, 1, t)
                turn(0)
                pe.wait_ge(top_in[0], 16)
                for h in range(QUAD):
                    second(0, 0, 0, h, tuple(ahead(0, False, 0, h)))

                def sequence(b, final):
                    for j in range(NQ):
                        u = b * NQ + j
                        more = not (final and j == NQ - 1)
                        nj, nb = (j + 1) % NQ, b + (j + 1) // NQ
                        for g in range(1, GROUPS + 1):
                            for h in range(QUAD):
                                n = g * QUAD + h
                                between = tuple(ahead(u, final, j, n))
                                for _, aj, t in between:
                                    if t == 0:
                                        pe.wait_ge(loaded[aj], (b + (j + 2) // NQ + 1) * 16 * LOADS)
                                if g < GROUPS:
                                    second(u, j, g, h, between)
                                elif more:
                                    if h == 0:
                                        pe.wait_ge(top_in[nj], nb * 16 + 16)
                                    second(u + 1, nj, 0, h, between)
                                if n == TURN and more:
                                    turn(u + 1)
                                if h >= 2:
                                    values(u, j, g - 1, h - 2)

                with pe.Fori(0, B - 1) as b:
                    sequence(b, False)
                sequence(B - 1, True)

            @block.scalar
            def _(act):
                def turn(u, j, b):
                    act.wait_ge(turned, u + 1)
                    if j:
                        act.wait_ge(top_in[j - 1], b * 16 + 16)
                    elif not isinstance(b, int) or b:
                        act.wait_ge(top_in[NQ - 1], b * 16)
                    act.activation(topT[:], psT[:], ACT.Copy).then_inc(topT_ready, 1)
                    act.wait_ge(topT_ready, u + 1)
                    dst = q4[j][MAXROW:ALL, :, :].rearrange("k h (c s) -> k (h c) s", s=P)
                    act.dma_start(dst, topT[0:3 * QUAD * KC, :]).then_inc(top_in[j], 16)

                def exponentials(u, g, h):
                    act.wait_ge(keyed, u * TILES2 + (g * QUAD + h + 1))
                    act.activation(probs[(g % 2) * QUAD + h][:], psS[h % 2][:], ACT.Exp).then_inc(probs_ready, 1)

                def sequence(b, final):
                    for j in range(NQ):
                        u = b * NQ + j
                        more = not (final and j == NQ - 1)
                        for g in range(1, GROUPS + more):
                            act.wait_ge(summed, u * GROUPS + (g - 1))
                            for h in range(QUAD):
                                exponentials(u, g, h)
                                if g * QUAD + h == TURN + 1 and more:
                                    turn(u + 1, (j + 1) % NQ, b + (j + 1) // NQ)

                turn(0, 0, 0)
                for h in range(QUAD):
                    exponentials(0, 0, h)
                with act.Fori(0, B - 1) as b:
                    sequence(b, False)
                sequence(B - 1, True)

            @block.vector
            def _(dve):
                def maxima(u, t):
                    h, c, half = t // (KC * NHALF), t // NHALF % KC, t % NHALF
                    dve.wait_ge(scored, u * TILES1 + t + 1)
                    dve.reduce_max(half_max[:, h, c, half:half + 1], psM[t % 2][:], AX.X).then_inc(maxed, 1)

                def minus_max(u):
                    dve.wait_ge(maxed, u * TILES1 + TILES1)
                    dve.wait_ge(turned, u)
                    top_at.done(dve.tensor_reduce(top[:], half_max[:].rearrange("p h c n -> p (h c) n"), AX.X, ALU.max, negate=True), "top")
                    top_at.wait(dve, u, "top")
                    top_at.done(dve.tensor_copy(top3[:, 0, :], top[:]), "part0")
                    top_at.wait(dve, u, "part0")
                    top_at.done(dve.tensor_tensor(rest[:, 0, :], top[:], top3[:, 0, :], ALU.subtract), "rest0")
                    top_at.wait(dve, u, "rest0")
                    top_at.done(dve.tensor_copy(top3[:, 1, :], rest[:, 0, :]), "part1")
                    top_at.wait(dve, u, "part1")
                    top_at.done(dve.tensor_tensor(rest[:, 1, :], rest[:, 0, :], top3[:, 1, :], ALU.subtract), "rest1")
                    top_at.wait(dve, u, "rest1")
                    top_at.done(dve.tensor_copy(top3[:, 2, :], rest[:, 1, :]), "part2")
                    top_at.wait(dve, u, "part2")

                def collect(u, half):
                    dve.wait_ge(summed, u * GROUPS + (half + 1) * GROUPS // NHALF)
                    dve.wait_ge(sums_st[half], u * QUAD * 16)
                    dve.tensor_copy(sums[half][:], psV[:]).then_inc(sums_ready, 1)

                dve.memset(top3[:, 3, :], 0.0).then_inc(filled, 1)
                dve.wait_ge(filled, 1)
                for t in range(TILES1):
                    maxima(0, t)
                minus_max(0)
                for t in range(LEAD):
                    maxima(1, t)
                for h in range(QUAD):
                    for ahead_u, _, t in ahead(0, False, 0, h):
                        maxima(ahead_u, t)

                def sequence(b, final):
                    for j in range(NQ):
                        u = b * NQ + j
                        for g in range(1, GROUPS + 1):
                            for h in range(QUAD):
                                for ahead_u, _, t in ahead(u, final, j, g * QUAD + h):
                                    maxima(ahead_u, t)
                                    if t == TILES1 - 1:
                                        minus_max(ahead_u)
                            if g == GROUPS // NHALF:
                                collect(u, 0)
                        collect(u, 1)

                with dve.Fori(0, B - 1) as b:
                    sequence(b, False)
                sequence(B - 1, True)


def experts(nc, A):
    TILE, SUB = 256, 2
    NT = N // TILE
    FT = FF // P
    STAGED = max(H * FF, FT * D)
    with ExitStack() as ctx:
        m = Memory(nc, ctx, "ex")
        two = range(2)
        wo, ob, wr, br = m.sb("wo", [P, D]), m.sb("ob", [P, H]), m.sb("wr", [P, H, E]), m.sb("br", [P, E])
        b1, b2 = m.sb("b1", [P, E, FT]), m.sb("b2", [E, D])
        w1 = [m.sb(f"w1{k}", [P, E, H, FF], F32R) for k in two]
        w2 = [m.sb(f"w2{k}", [P, E, FT, D], F32R) for k in two]
        ident, number = m.sb("ident", [P, P]), m.sb("number", [P, E])
        ao = [m.sb(f"ao{k}", [P, 2, TILE]) for k in two]
        x1, xn, s1 = ([m.sb(f"{n}{k}", [P, SUB, D]) for k in two] for n in ("x1", "xn", "s1"))
        rs, aon = m.sb("rs", [P, TILE]), m.sb("aon", [P, TILE])
        mla = m.sb("mla", [P, H, TILE])
        mla2 = [[m.sb(f"mla2{k}{part}", [P, H, TILE], F32R) for part in two] for k in two]
        R = [P, SUB, E]
        lg, ex, pr, top, pick0, pick1 = (m.sb(n, R) for n in ("lg", "ex", "pr", "top", "pick0", "pick1"))
        index, indexf = m.sb("index", R, U32), m.sb("indexf", R)
        comb = [m.sb(f"comb{k}", R) for k in two]
        mx, total, share = m.sb("mx", [P, SUB]), m.sb("total", [P, SUB]), m.sb("share", [P, SUB, 2])
        combT = m.sb("combT", [E, SUB, P])
        hid = [m.sb(f"hid{k}", [P, FT, TILE]) for k in two]
        hid2 = [[m.sb(f"hid2{k}{part}", [P, FT, TILE], F32R) for part in two] for k in two]
        acc = [m.sb(f"acc{k}", [P, SUB, D]) for k in two]
        gin, th, res = (m.sb(n, [P, SUB, D]) for n in ("gin", "th", "res"))
        psH = [m.ps(f"psH{k}", [P, 2, TILE]) for k in range(FT)]
        psE = [m.ps(f"psE{k}", [P, SUB, D]) for k in two]
        psM, psB = m.ps("psM", [P, H, TILE]), m.ps("psB", [P, SUB, D])
        weights, consts, split = m.sem("weights"), m.sem("consts"), m.sem("split")
        staged = [m.sem(f"staged{k}") for k in two]
        ao_loaded = [m.sem(f"ao_loaded{k}") for k in two]
        end_loaded = [m.sem(f"end_loaded{k}") for k in two]
        out_st, half1 = m.sem("out_st"), m.sem("half1")
        pe_pre = Stages(m.sem("pe_pre"), "mla", "logits", "combT", "bias")
        act_pre = Stages(m.sem("act_pre"), "mla", "ex")
        dve_pre = Stages(m.sem("dve_pre"), "rs", "aon", "head", "rest", "lg", "mx", "sub", "total", "rtotal", "pr", "top",
                         "index", "indexf", "sum2", "rsum2", "share", "pick0", "pick1", "comb", "combT", "bias")
        hid_psum, hid_ready, out_psum, added = m.sem("hid_psum"), m.sem("hid_ready"), m.sem("out_psum"), m.sem("added")
        head_ready, rest_ready = m.sem("head_ready"), m.sem("rest_ready")
        gin_ready, th_ready, res_ready, act_own, dve_own, pre_own = (
            m.sem(n) for n in ("gin", "th", "res", "act_own", "dve_own", "pre_own"))
        NSTAGED = 2 * E

        def rows(ap, i):
            return ap.rearrange("(i s p) d -> i p s d", p=P, s=SUB)[i, :, :, :]

        def flat(ap):
            return ap.rearrange("p a b -> p (a b)")

        def products(pe, out, parts, start, stop):
            for n, (a, b) in enumerate(parts):
                last = pe.matmul(out, a, b, start=start and n == 0, stop=stop and n == len(parts) - 1)
            return last

        def run(eng, step):
            step(0, 0, True, True)
            with eng.Fori(0, NT // 2 - 1) as turn:
                step(turn * 2 + 1, 1, False, True)
                step(turn * 2 + 2, 0, False, True)
            step(NT - 1, 1, False, False)

        with nc.Block() as block:
            @block.sync
            def _(sp):
                with nc.allow_non_contiguous_dma(reason="small"):
                    for dst, src in ((wo[:], A["fo"][0:P, :]), (ob[:], column(A["fob"])), (wr[:], halves(A["rw"])),
                                     (br[:], spread(A["rb"], E)), (b2[:], A["b2"]),
                                     (b1[:], A["b1"].rearrange("e (f p) -> p e f", p=P))):
                        sp.dma_start(dst, src).then_inc(weights, 16)

                def load_ao(i, par):
                    src = A["ao"].rearrange("h (k r) (i t) -> i k h r t", k=2, t=TILE)
                    for k in two:
                        sp.dma_start(ao[par][:, k, :], src[i, k, :, :, :]).then_inc(ao_loaded[par], 16)

                def load_end(i, par):
                    for name, buf in (("xn1", xn), ("x1", x1), ("s1", s1)):
                        sp.dma_start(buf[par][:], rows(A[name], i)).then_inc(end_loaded[par], 16)

                for i in two:
                    load_ao(i, i)
                    load_end(i, i)
                w1_in = A["w1"].rearrange("e (h p) f -> e p h f", p=P)
                w2_in = A["w2"].rearrange("e (f p) d -> e p f d", p=P)
                for n in range(NSTAGED):
                    if n >= 2:
                        sp.wait_ge(split, 2 * n - 2)
                    src = w1_in[n // 2, :, :, :] if n % 2 == 0 else w2_in[n // 2, :, :, :]
                    dst = flat(hid[n % 2][:]).rearrange("p (a b) -> p a b", a=src.shape[1])
                    sp.dma_start(dst, src).then_inc(staged[n % 2], 16)

                with sp.Fori(0, NT // 2 - 1) as turn:
                    for par in two:
                        i = turn * 2 + par
                        dve_pre.wait(sp, i, "aon")
                        m.settle(sp)
                        load_ao(i + 2, par)
                        sp.wait_ge(res_ready, i + 1)
                        m.settle(sp)
                        load_end(i + 2, par)
                sp.wait_ge(out_st, 16 * NT)

            @block.gpsimd
            def _(pool):
                identity(nc, pool, ident, consts)
                pool.wait_ge(consts, 2)
                pool.iota(number[:], pattern=[[1, E]], base=0, channel_multiplier=0,
                          allow_small_or_imprecise_dtypes=True).then_inc(consts, 1)
                with pool.Fori(0, NT) as i:
                    pool.wait_ge(res_ready, i + 1)
                    m.settle(pool)
                    pool.dma_start(rows(A["out"], i), res[:]).then_inc(out_st, 16)

            @block.scalar
            def _(act):
                def prepare(i, slot):
                    if slot == 3:
                        pe_pre.wait(act, i, "mla")
                        if isinstance(i, int) and i == 0:
                            pass
                        else:
                            dve_pre.wait(act, i - 1, "rest")
                            pe_pre.wait(act, i - 1, "logits")
                        act.activation(mla[:, 0, :], psM[:, 0, :], ACT.Identity, bias=ob[:, 0:1]).then_inc(act_own, 1)
                        act_pre.done(act.activation(mla[:, 1, :], psM[:, 1, :], ACT.Identity, bias=ob[:, 1:2]), "mla")
                        act.wait_ge(act_own, i + 1)
                    if slot == 5:
                        dve_pre.wait(act, i, "sub")
                        act_pre.done(act.activation(ex[:], lg[:], ACT.Exp), "ex")

                def gelu(i, e):
                    if e >= 2:
                        act.wait_ge(rest_ready, i * E + (e - 1))
                    elif isinstance(i, int) and i == 0:
                        act.wait_ge(split, 2 * NSTAGED)
                    else:
                        act.wait_ge(rest_ready, i * E + e - 1)
                    for f in range(FT):
                        act.wait_ge(hid_psum, (i * E + e) * FT + f + 1)
                        act.activation(hid[e % 2][:, f, :], psH[f][:, 0, :], ACT.Gelu,
                                       bias=b1[:, e, f:f + 1]).then_inc(hid_ready, 1)

                def finish(i):
                    act.wait_ge(gin_ready, i + 1)
                    act.activation(th[:], gin[:], ACT.Tanh, scale=0.5).then_inc(th_ready, 1)

                def step(i, par, first, more):
                    for e in range(E):
                        if e + 1 < E:
                            gelu(i, e + 1)
                        elif more:
                            gelu(i + 1, 0)
                        if e == 1 and not first:
                            finish(i - 1)
                        if more:
                            prepare(i + 1, e)

                act.wait_ge(weights, 96)
                for slot in range(E):
                    prepare(0, slot)
                gelu(0, 0)
                run(act, step)
                finish(NT - 1)

            @block.tensor
            def _(pe):
                def prepare(i, par, slot):
                    if slot == 2:
                        dve_pre.wait(pe, i, "aon")
                        for h in range(H):
                            last = pe.matmul(psM[:, h, :], wo[:, h * P:(h + 1) * P], aon[:], start=True, stop=True)
                        pe_pre.done(last, "mla")
                    if slot == 4:
                        act_pre.wait(pe, i, "mla")
                        for s in range(SUB):
                            for h in range(H):
                                last = pe.matmul(psB[:, s, 0:E], mla[:, h, s * P:(s + 1) * P], wr[:, h, :],
                                                 start=(h == 0), stop=(h == H - 1))
                        pe_pre.done(last, "logits")
                    if slot == 6:
                        dve_pre.wait(pe, i, "comb")
                        for s in range(SUB):
                            last = pe.transpose(psM[0:E, 0, s * P:(s + 1) * P], comb[par][:, s, :], ident[:])
                        pe_pre.done(last, "combT")
                    if slot == 7:
                        dve_pre.wait(pe, i, "combT")
                        for s in range(SUB):
                            last = pe.matmul(psB[:, s, :], combT[:, s, :], b2[:], start=True, stop=True)
                        pe_pre.done(last, "bias")

                def hidden(i, par, e):
                    if e == 0:
                        dve_pre.wait(pe, i, "rest")
                    for f in range(FT):
                        if e:
                            pe.wait_ge(hid_ready, i * E * FT + ((e - 1) * FT + f + 1))
                        elif not (isinstance(i, int) and i == 0):
                            pe.wait_ge(hid_ready, i * E * FT + (f + 1) - FT)
                        fs = slice(f * P, (f + 1) * P)
                        for h in range(H):
                            xh, xl = (mla2[par][k][:, h, :] for k in two)
                            wh, wl = (w1[k][:, e, h, fs] for k in two)
                            last = products(pe, psH[f][:, 0, :], ((wh, xh), (wh, xl), (wl, xh)), h == 0, h == H - 1)
                        last.then_inc(hid_psum, 1)

                def output(i, e):
                    pe.wait_ge(rest_ready, i * E + (e + 1))
                    if e >= 2:
                        pe.wait_ge(added, i * E + (e - 1))
                    elif not (isinstance(i, int) and i == 0):
                        pe.wait_ge(added, i * E + e - 1)
                    for s in range(SUB):
                        ss = slice(s * P, (s + 1) * P)
                        for f in range(FT):
                            xh, xl = (hid2[e % 2][k][:, f, ss] for k in two)
                            wh, wl = (w2[k][:, e, f, :] for k in two)
                            last = products(pe, psE[e % 2][:, s, :], ((xh, wh), (xh, wl), (xl, wh)), f == 0, f == FT - 1)
                    last.then_inc(out_psum, 1)

                def step(i, par, first, more):
                    for e in range(E):
                        if e + 1 < E:
                            hidden(i, par, e + 1)
                        elif more:
                            hidden(i + 1, 1 - par, 0)
                        if more:
                            prepare(i + 1, 1 - par, e)
                        output(i, e)

                pe.wait_ge(weights, 96)
                pe.wait_ge(consts, 3)
                for slot in range(E):
                    prepare(0, 0, slot)
                pe.wait_ge(split, 2 * NSTAGED)
                hidden(0, 0, 0)
                run(pe, step)

            @block.vector
            def _(dve):
                def divide(head, rest, whole, head_sem, rest_sem, wait):
                    head_sem(dve.tensor_copy(head, whole))
                    wait()
                    rest_sem(dve.tensor_tensor(rest, whole, head.bitcast(F32), ALU.subtract))

                def prepare(i, par, slot):
                    own = Chain(pre_own, 2 * (SUB - 1) + 4)
                    if slot == 1:
                        dve.wait_ge(ao_loaded[par], (i - par) * 16 + 32)
                        dve_pre.done(dve.reciprocal(rs[:], ao[par][:, 1, :]), "rs")
                        dve_pre.wait(dve, i, "rs")
                        dve_pre.done(dve.tensor_tensor(aon[:], ao[par][:, 0, :], rs[:], ALU.mult), "aon")
                    if slot == 3:
                        act_pre.wait(dve, i, "mla")
                        head, rest = (flat(mla2[par][k][:]) for k in two)
                        divide(head, rest, flat(mla[:]), lambda ins: dve_pre.done(ins, "head"),
                               lambda ins: dve_pre.done(ins, "rest"), lambda: dve_pre.wait(dve, i, "head"))
                    if slot == 4:
                        pe_pre.wait(dve, i, "logits")
                        wide = lambda t: t[:].rearrange("p (s a) -> p s a", a=1).to_broadcast([P, SUB, E])
                        dve_pre.done(dve.tensor_tensor(lg[:], psB[:, :, 0:E], over_chunks(br[:], SUB), ALU.add), "lg")
                        dve_pre.wait(dve, i, "lg")
                        dve_pre.done(dve.tensor_reduce(mx[:], lg[:], AX.X, ALU.max), "mx")
                        dve_pre.wait(dve, i, "mx")
                        dve_pre.done(dve.tensor_tensor(lg[:], lg[:], wide(mx), ALU.subtract), "sub")
                    if slot == 5:
                        own.begin(i)
                        wide = lambda t: t[:].rearrange("p (s a) -> p s a", a=1).to_broadcast([P, SUB, E])
                        act_pre.wait(dve, i, "ex")
                        dve_pre.done(dve.tensor_reduce(total[:], ex[:], AX.X, ALU.add), "total")
                        dve_pre.wait(dve, i, "total")
                        dve_pre.done(dve.reciprocal(total[:], total[:]), "rtotal")
                        dve_pre.wait(dve, i, "rtotal")
                        dve_pre.done(dve.tensor_tensor(pr[:], ex[:], wide(total), ALU.mult), "pr")
                        dve_pre.wait(dve, i, "pr")
                        for s in range(SUB):
                            m.settle(dve)
                            ins = dve.max(top[:, s, :], pr[:, s, :])
                            own.mark(ins) if s < SUB - 1 else dve_pre.done(ins, "top")
                        own.wait(dve)
                        dve_pre.wait(dve, i, "top")
                        for s in range(SUB):
                            m.settle(dve)
                            ins = dve.max_index(index[:, s, :], top[:, s, :], pr[:, s, :])
                            own.mark(ins) if s < SUB - 1 else dve_pre.done(ins, "index")
                        own.wait(dve)
                        dve_pre.wait(dve, i, "index")
                        dve_pre.done(dve.tensor_copy(indexf[:], index[:]), "indexf")
                        dve_pre.done(dve.tensor_tensor(mx[:], top[:, :, 0], top[:, :, 1], ALU.add), "sum2")
                        dve_pre.wait(dve, i, "sum2")
                        dve_pre.done(dve.tensor_scalar(mx[:], mx[:], 1e-8, None, ALU.add), "rsum2")
                        dve_pre.wait(dve, i, "rsum2")
                        own.link(dve, dve.reciprocal(mx[:], mx[:]))
                        own.link(dve, dve.tensor_tensor(share[:, :, 0], top[:, :, 0], mx[:], ALU.mult))
                        dve_pre.done(dve.tensor_tensor(share[:, :, 1], top[:, :, 1], mx[:], ALU.mult), "share")
                        dve_pre.wait(dve, i, "share")
                        chosen = lambda t, k: t[:, :, k:k + 1].to_broadcast([P, SUB, E])
                        own.link(dve, dve.tensor_tensor(pick0[:], over_chunks(number[:], SUB), chosen(indexf, 0), ALU.is_equal))
                        own.link(dve, dve.tensor_tensor(pick1[:], over_chunks(number[:], SUB), chosen(indexf, 1), ALU.is_equal))
                        dve_pre.done(dve.tensor_tensor(pick0[:], pick0[:], chosen(share, 0), ALU.mult), "pick0")
                        dve_pre.done(dve.tensor_tensor(pick1[:], pick1[:], chosen(share, 1), ALU.mult), "pick1")
                        dve_pre.wait(dve, i, "pick1")
                        dve_pre.done(dve.tensor_tensor(comb[par][:], pick0[:], pick1[:], ALU.add), "comb")
                        own.end()
                    if slot == 6:
                        pe_pre.wait(dve, i, "combT")
                        dve_pre.done(dve.tensor_copy(combT[:].rearrange("e s t -> e (s t)"), psM[0:E, 0, :]), "combT")
                    if slot == 7:
                        pe_pre.wait(dve, i, "bias")
                        dve_pre.done(dve.tensor_copy(acc[par][:], psB[:]), "bias")

                def split_hidden(i, e):
                    dve.wait_ge(hid_ready, (i * E + e + 1) * FT)
                    if not (isinstance(i, int) and i == 0 and e < 2):
                        dve.wait_ge(out_psum, i * E + (e - 1) if e else i * E - 1)
                    head, rest = (flat(hid2[e % 2][k][:]) for k in two)
                    divide(head, rest, flat(hid[e % 2][:]), lambda ins: ins.then_inc(head_ready, 1),
                           lambda ins: ins.then_inc(rest_ready, 1), lambda: dve.wait_ge(head_ready, i * E + e + 1))

                def add(i, par, e):
                    dve.wait_ge(out_psum, i * E + e + 1)
                    if e == 0:
                        dve_pre.wait(dve, i, "bias")
                    else:
                        dve.wait_ge(added, i * E + e)
                    for s in range(SUB):
                        ins = dve.scalar_tensor_tensor(
                            out=acc[par][:, s, :], in0=psE[e % 2][:, s, :], scalar=comb[par][:, s, e:e + 1],
                            in1=acc[par][:, s, :], op0=ALU.mult, op1=ALU.add)
                        if s == 0:
                            ins.then_inc(dve_own, 1)
                    dve.wait_ge(dve_own, i * E + e + 1)
                    ins.then_inc(added, 1)

                def finish_a(i, par):
                    dve.wait_ge(added, (i + 1) * E)
                    dve.wait_ge(end_loaded[par], (i - par) * 24 + 48)
                    dve.scalar_tensor_tensor(out=gin[:], in0=acc[par][:], scalar=0.3, in1=xn[par][:],
                                             op0=ALU.mult, op1=ALU.add).then_inc(gin_ready, 1)

                def finish_b(i, par):
                    dve.wait_ge(gin_ready, i + 1)
                    dve.wait_ge(th_ready, i + 1)
                    dve.wait_ge(out_st, 16 * i)
                    dve.scalar_tensor_tensor(out=res[:], in0=th[:], scalar=1.0, in1=gin[:],
                                             op0=ALU.add, op1=ALU.mult).then_inc(half1, 1)
                    dve.wait_ge(half1, 2 * i + 1)
                    dve.scalar_tensor_tensor(out=res[:], in0=res[:], scalar=0.5, in1=s1[par][:],
                                             op0=ALU.mult, op1=ALU.mult).then_inc(half1, 1)
                    dve.wait_ge(half1, 2 * i + 2)
                    dve.tensor_tensor(res[:], res[:], x1[par][:], ALU.add).then_inc(res_ready, 1)

                def step(i, par, first, more):
                    for e in range(E):
                        if e + 1 < E:
                            split_hidden(i, e + 1)
                        elif more:
                            split_hidden(i + 1, 0)
                        add(i, par, e)
                        if more:
                            prepare(i + 1, 1 - par, e)
                        if not first and e == 0:
                            finish_a(i - 1, 1 - par)
                        if not first and e == 2:
                            finish_b(i - 1, 1 - par)

                for n in range(NSTAGED):
                    k, e = n % 2, n // 2
                    dve.wait_ge(staged[k], 16 * (e + 1))
                    head, rest = (((w2 if k else w1)[part][:, e, :, :].rearrange("p a b -> p (a b)")) for part in two)
                    divide(head, rest, flat(hid[k][:]), lambda ins: ins.then_inc(split, 1),
                           lambda ins: ins.then_inc(split, 1), lambda: dve.wait_ge(split, 2 * n + 1))
                dve.wait_ge(weights, 96)
                dve.wait_ge(consts, 3)
                for slot in range(E):
                    prepare(0, 0, slot)
                split_hidden(0, 0)
                run(dve, step)
                finish_a(NT - 1, 1)
                finish_b(NT - 1, 1)


PHASES = [ssm_inputs, ssm_scan, ssm_output, delta_inputs, delta_invert, delta_chunks, attention, experts]


def build(nc, A, phases=None):
    for phase in PHASES:
        if phases is None or phase.__name__ in phases:
            with nc.cleanup_on_exit(), nc.allow_non_contiguous_dma(reason="small vectors of weights"):
                phase(nc, A)


def _layout(inputs):
    a = {k: np.asarray(v) for k, v in inputs.items()}

    def of(block):
        return lambda name: a[f"{block}_{name}"]

    ssm, fp8, delta, moe = of("L0_attn"), of("L0_ffn"), of("L1_attn"), of("L1_ffn")
    keys = np.arange(P).reshape(NH // 4, 4, HD).transpose(0, 2, 1).reshape(-1)
    used = np.arange(2 * P).reshape(NH, 2 * HD)[:, :HD].reshape(-1)[keys]
    laid = dict(
        x=ssm("hidden_states").reshape(N, D), w_xz=ssm("W_xz"), w_dt=ssm("W_dt"), b_dt=ssm("b_dt"),
        w_bc=np.concatenate([ssm("W_B"), ssm("W_C")], 1), a_log=ssm("A_log"), d_skip=ssm("D_skip"),
        w_out=ssm("W_out"), v_th=ssm("v_th"),
        kern=fp8("kernel"), s_in=fp8("input_scale"), s_k=fp8("kernel_scale"), bias=fp8("bias"),
        w_tok=np.concatenate([delta(n) for n in ("Wq", "Wk", "Wv", "Wa", "Wb")], 0).T,
        b_tok=np.concatenate([delta(n) for n in ("bq", "bk", "bv", "ba", "bb")]),
        w_gate=delta("Wg").T, b_gate=delta("bg"), w_o=delta("Wo").T, b_o=delta("bo"),
        fq=moe("q_w")[:, used], fqb=moe("q_b")[used], fk=moe("k_w")[:, keys], fkb=moe("k_b")[keys], fv=moe("v_w"), fvb=moe("v_b"),
        fo=moe("o_w"), fob=moe("o_b"), rw=moe("router_w"), rb=moe("router_b"),
        w1=moe("w1"), b1=moe("b1"), w2=moe("w2"), b2=moe("b2"))
    return {k: np.ascontiguousarray(v) for k, v in laid.items()}


def kernel(**inputs):
    import concourse.bacc as bacc
    from concourse.bass_utils import run_bass_kernel_spmd

    nc = bacc.Bacc("TRN2", target_bir_lowering=False, num_devices=1)
    arrays, A = {}, {}
    for name, value in _layout(inputs).items():
        arrays[f"in_{name}"] = value
        A[name] = nc.dram_tensor(f"in_{name}", value.shape, mybir.dt.from_np(value.dtype), kind="ExternalInput").ap()
    kinds = {"float32": F32, "bfloat16": BF16}
    for name, (shape, dtype) in SCRATCH.items():
        A[name] = nc.dram_tensor(f"scratch_{name}", shape, kinds[dtype]).ap()
    A["out"] = nc.dram_tensor("out_dram", (N, D), F32, kind="ExternalOutput").ap()
    build(nc, A)
    r = run_bass_kernel_spmd(nc, [arrays], core_ids=[0])
    return r.results[0]["out_dram"].reshape(B, T, D)
```

```python
from contextlib import ExitStack

import numpy as np
import concourse.bass as bass
from concourse import mybir

F32 = mybir.dt.float32
F32R = mybir.dt.float32r
BF16 = mybir.dt.bfloat16
I32 = mybir.dt.int32
U32 = mybir.dt.uint32
ALU = mybir.AluOpType
ACT = mybir.ActivationFunctionType
AX = mybir.AxisListType

B, T, D = 8, 1024, 256
N = B * T
P = 128
H = D // P
S = 16
TILE = 512
SUB = TILE // P
NT = N // TILE
NP = N // P
C = 128
NH, HD = 16, 8
E, FF = 8, 512
EPS = 1e-5
FP8_MAX_TIE = 464.0

LOG_A, LOG_G, BETA, EXP_G, NEG_EXP_G, TO_END_BETA, EXP_END = range(7)
NDEC = 7

SCRATCH = {
    "dec": ([P, NP, 7], "float32"),
    "xn0": ([N, D], "float32"), "x_t": ([H, P, N], "float32"), "z_t": ([H, P, N], "float32"),
    "dt_t": ([H, P, N], "float32"), "u_t": ([H, P, N], "float32"), "xq_t": ([H, P, N], "bfloat16"),
    "bc": ([3, 2 * S, N], "bfloat16"), "y_t": ([H, P, N], "float32"), "xmax": ([P, NP], "float32"),
    "x1": ([N, D], "float32"), "xn1": ([N, D], "float32"),
    "qd": ([N, C], "float32"), "kd": ([N, C], "float32"), "vd": ([N, C], "float32"),
    "ab": ([P, NP, 2], "float32"), "gate_t": ([C, N], "float32"),
    "qs": ([B, NH // 4, 3, 32, T], "bfloat16"), "ks": ([B, NH // 4, 3, 32, T], "bfloat16"), "vf": ([N, P], "float32"),
    "inv": ([NP, P, P], "float32"), "dm": ([NP, P, P], "float32"), "kt": ([NP, P, P], "float32"),
    "qt": ([NP, P, P], "float32"), "qgt": ([NP, P, P], "float32"),
    "s1": ([N, D], "float32"), "ao": ([NH, 2 * HD, N], "float32"),
}


class Chain:

    def __init__(self, sem, per):
        self.sem, self.per, self.base, self.n = sem, per, 0, 0

    def begin(self, i):
        self.base, self.n = i * self.per, 0

    def end(self):
        assert self.n == self.per, (self.n, self.per)

    def link(self, eng, ins):
        self.mark(ins)
        self.wait(eng)

    def mark(self, ins):
        self.n += 1
        ins.then_inc(self.sem, 1)

    def wait(self, eng):
        eng.wait_ge(self.sem, self.base + self.n)


def pairs(eng, count):
    with eng.Fori(0, count // 2) as turn:
        for par in range(2):
            yield turn * 2 + par, par


def one_ahead(eng, step, count=NT):
    with eng.Fori(0, count // 2 - 1) as turn:
        for par in range(2):
            step(turn * 2 + par, par, True)
    step(count - 2, 0, True)
    step(count - 1, 1, False)


def well_ahead(eng, step, count=NT):
    with eng.Fori(0, count // 2 - 2) as turn:
        for par in range(2):
            step(turn * 2 + par, par, count)
    for i in range(count - 4, count):
        step(i, i % 2, count - 1 - i)


class Memory:

    def __init__(self, nc, ctx, phase):
        self.nc, self.ctx, self.phase = nc, ctx, phase
        self.settled = self.sem("settled")

    def settle(self, eng):
        eng.sem_inc(self.settled, 1)

    def sb(self, name, shape, dt=F32):
        return self.ctx.enter_context(self.nc.sbuf_tensor(f"{self.phase}_{name}", shape, dt))

    def ps(self, name, shape, dt=F32):
        return self.ctx.enter_context(self.nc.psum_tensor(f"{self.phase}_{name}", shape, dt))

    def sem(self, name):
        return self.nc.alloc_semaphore(name=f"{self.phase}_{name}")


def halves(ap):
    return ap.rearrange("(h p) n -> p h n", p=P)


def column(ap):
    return ap.rearrange("(h p) -> p h", p=P)


def spread(ap, n):
    return ap.rearrange("(a n) -> a n", a=1).to_broadcast([P, n])


def identity(nc, eng, ident, sem):
    eng.memset(ident[:], 0.0).then_inc(sem, 1)
    eng.wait_ge(sem, 1)
    eng.affine_select(out=ident[:], in_=ident[:], compare_op=ALU.not_equal, fill=1.0, base=0,
                      pattern=[[-1, P]], channel_multiplier=1).then_inc(sem, 1)


def ssm_inputs(nc, A):
    with ExitStack() as ctx:
        m = Memory(nc, ctx, "si")
        wxz, wdt, wbc = m.sb("wxz", [P, H, 2 * D]), m.sb("wdt", [P, H, D]), m.sb("wbc", [P, H, 2 * S])
        bdt, sin, rsin = m.sb("bdt", [P, H]), m.sb("sin", [P, 1]), m.sb("rsin", [P, 1])
        ident = m.sb("ident", [P, P])
        x = [m.sb(f"x{k}", [P, SUB, D]) for k in range(2)]
        xn = m.sb("xn", [P, SUB, D])
        stats, mv = m.sb("stats", [P, SUB, 6]), m.sb("mv", [P, SUB, 2])
        ve, half, rstd = m.sb("ve", [P, SUB]), m.sb("half", [P, SUB]), m.sb("rstd", [P, SUB])
        xmax = m.sb("xmax", [P, NP])
        xnT, xb = m.sb("xnT", [P, H, TILE]), m.sb("xb", [P, H, TILE], BF16)
        xT, zT = [m.sb(f"xT{k}", [P, H, TILE]) for k in range(2)], m.sb("zT", [P, H, TILE])
        vb, mag, soft = m.sb("vb", [P, H, TILE]), m.sb("mag", [P, H, TILE]), m.sb("soft", [P, H, TILE])
        dtT, uT = m.sb("dtT", [P, H, TILE]), m.sb("uT", [P, H, TILE])
        v8, e8, r8 = m.sb("v8", [P, H, TILE]), m.sb("e8", [P, H, TILE]), m.sb("r8", [P, H, TILE])
        xq = m.sb("xq", [P, H, TILE], BF16)
        b_part = m.sb("b_part", [2 * S, 3, TILE], BF16)
        b_rest = m.sb("b_rest", [2 * S, 2, TILE])
        psT, psX, psZ = m.ps("psT", [P, H, TILE]), m.ps("psX", [P, H, TILE]), m.ps("psZ", [P, H, TILE])
        psD = m.ps("psD", [P, H, TILE])

        weights, x_loaded = m.sem("weights"), [m.sem(f"x_loaded{k}") for k in range(2)]
        ident_made, consts = m.sem("ident_made"), m.sem("consts")
        var_ready, rstd_ready, xn_ready, xT_psum = m.sem("var"), m.sem("rstd"), m.sem("xn"), m.sem("xT_psum")
        xnT_ready, xb_ready = m.sem("xnT"), m.sem("xb")
        x_psum, z_psum, bc_psum, dt_psum = m.sem("x_psum"), m.sem("z_psum"), m.sem("bc_psum"), m.sem("dt_psum")
        x_ready, z_ready, bc_ready = m.sem("x_ready"), m.sem("z_ready"), m.sem("bc_ready")
        soft_ready, vb_ready, dt_ready, u_ready = m.sem("soft"), m.sem("vb"), m.sem("dt_ready"), m.sem("u_ready")
        v8_ready, e8_ready, xq_ready = m.sem("v8"), m.sem("e8"), m.sem("xq_ready")
        xn_st, x_st, z_st, bc_st, dt_st, u_st, xq_st = (m.sem(f"{n}_st") for n in ("xn", "x", "z", "bc", "dt", "u", "xq"))
        e8_and, rsin_ready = m.sem("e8_and"), m.sem("rsin_ready")
        max_st, max_ready = m.sem("max_st"), m.sem("max_ready")
        act_own, dve_own, dve_split, pool_own = (m.sem(n) for n in ("act_own", "dve_own", "dve_split", "pool_own"))
        x_in = A["x"].rearrange("(i s p) d -> i p s d", p=P, s=SUB)
        xn_out = A["xn0"].rearrange("(i s p) d -> i p s d", p=P, s=SUB)

        def tile(name, i):
            return A[name].rearrange("h p (i t) -> i p h t", t=TILE)[i, :, :, :]

        with nc.Block() as block:
            @block.sync
            def _(sp):
                sp.dma_start(wxz[:], halves(A["w_xz"])).then_inc(weights, 16)
                sp.dma_start(wdt[:], halves(A["w_dt"])).then_inc(weights, 16)
                sp.dma_start(wbc[:], halves(A["w_bc"])).then_inc(weights, 16)
                sp.dma_start(bdt[:], column(A["b_dt"])).then_inc(weights, 16)
                sp.dma_start(sin[:], spread(A["s_in"], 1)).then_inc(weights, 16)

                def load(i, par):
                    sp.dma_start(x[par][:], x_in[i, :, :, :]).then_inc(x_loaded[par], 16)

                def front(i, par, then_load):
                    sp.wait_ge(xn_ready, i + 1)
                    m.settle(sp)
                    sp.dma_start(xn_out[i, :, :, :], xn[:]).then_inc(xn_st, 16)
                    if then_load:
                        load(i + 2, par)

                def store(i, ready, name, buf, sem):
                    sp.wait_ge(ready, i + 1)
                    m.settle(sp)
                    sp.dma_start(tile(name, i), buf[:]).then_inc(sem, 16)

                def middle(i, par):
                    store(i, x_ready, "x_t", xT[par], x_st)
                    sp.wait_ge(bc_ready, i + 1)
                    m.settle(sp)
                    sp.dma_start(A["bc"].rearrange("k r (i t) -> i r k t", t=TILE)[i, :, :, :], b_part[:]).then_inc(bc_st, 16)
                    store(i, z_ready, "z_t", zT, z_st)

                def step(i, par, ahead):
                    if ahead >= 1:
                        middle(i + 1, 1 - par)
                    if ahead >= 2:
                        front(i + 2, par, ahead > 3)
                    if ahead >= 1:
                        store(i + 1, xq_ready, "xq_t", xq, xq_st)
                    store(i, dt_ready, "dt_t", dtT, dt_st)
                    store(i, u_ready, "u_t", uT, u_st)

                load(0, 0)
                load(1, 1)
                front(0, 0, True)
                middle(0, 0)
                front(1, 1, True)
                store(0, xq_ready, "xq_t", xq, xq_st)
                well_ahead(sp, step)
                sp.wait_ge(max_ready, NT)
                sp.dma_start(A["xmax"], xmax[:]).then_inc(max_st, 16)
                for sem in (xn_st, x_st, z_st, bc_st, dt_st, u_st, xq_st):
                    sp.wait_ge(sem, 16 * NT)
                    m.settle(sp)
                sp.wait_ge(max_st, 16)

            @block.gpsimd
            def _(pool):
                identity(nc, pool, ident, ident_made)
                pool.memset(half[:], -0.5).then_inc(consts, 1)
                pool.wait_ge(consts, 1)

                def front(i, par):
                    pool.wait_ge(var_ready, i + 1)
                    pool.wait_ge(xn_ready, i)
                    m.settle(pool)
                    pool.tensor_scalar_add(ve[:], mv[:, :, 1], EPS).then_inc(pool_own, 1)
                    pool.wait_ge(pool_own, 2 * i + 1)
                    pool.tensor_tensor(rstd[:], ve[:], half[:], ALU.pow).then_inc(rstd_ready, 1)
                    pool.wait_ge(e8_ready, i + 1)
                    pool.wait_ge(xq_st, 16 * i)
                    pool.tensor_tensor(r8[:], v8[:], e8[:], ALU.add).then_inc(pool_own, 1)
                    pool.wait_ge(pool_own, 2 * i + 2)
                    pool.tensor_tensor(xq[:], r8[:], e8[:], ALU.subtract).then_inc(xq_ready, 1)

                for i, par in pairs(pool, NT):
                    front(i, par)

            @block.vector
            def _(dve):
                own, split = Chain(dve_own, 3 * SUB - 2), Chain(dve_split, 4)
                dve.wait_ge(weights, 80)
                dve.reciprocal(rsin[:], sin[:]).then_inc(rsin_ready, 1)

                def variance(i, par):
                    own.begin(i)
                    dve.wait_ge(x_loaded[par], (i - par) * 8 + 16)
                    for s in range(SUB):
                        own.mark(dve.bn_stats(stats[:, s, :], x[par][:, s, :]))
                    own.wait(dve)
                    dve.wait_ge(rstd_ready, i)
                    for s in range(SUB):
                        m.settle(dve)
                        ins = dve.bn_aggr(mv[:, s, :], stats[:, s, :])
                        if s < SUB - 1:
                            own.mark(ins)
                        else:
                            ins.then_inc(var_ready, 1)
                    own.wait(dve)

                def normalise(i, par):
                    own.base, own.n = i * own.per, 2 * SUB - 1
                    dve.wait_ge(rstd_ready, i + 1)
                    dve.wait_ge(xn_st, 16 * i)
                    dve.wait_ge(xT_psum, i)
                    for s in range(SUB):
                        ins = dve.tensor_scalar(xn[:, s, :], x[par][:, s, :], mv[:, s, 0:1], rstd[:, s:s + 1],
                                                ALU.subtract, ALU.mult)
                        if s < SUB - 1:
                            own.mark(ins)
                        else:
                            ins.then_inc(xn_ready, 1)
                    own.wait(dve)
                    dve.wait_ge(xn_ready, i + 1)
                    dve.tensor_reduce(xmax[:, bass.ds(i * SUB, SUB)], xn[:], AX.X, ALU.max,
                                      apply_absolute_value=True).then_inc(max_ready, 1)

                def x_part(i, par):
                    dve.wait_ge(x_psum, i + 1)
                    if not isinstance(i, int) or i:
                        dve.wait_ge(x_st, 16 * (i - 1))
                        dve.wait_ge(u_ready, i - 1)
                    dve.tensor_copy(xT[par][:], psX[:]).then_inc(x_ready, 1)

                def bc_part(i):
                    split.begin(i)
                    dve.wait_ge(bc_psum, i + 1)
                    dve.wait_ge(bc_st, 16 * i)
                    bc = psD[0:2 * S, 0, :]
                    split.link(dve, dve.tensor_copy(b_part[:, 0, :], bc))
                    split.link(dve, dve.tensor_tensor(b_rest[:, 0, :], bc, b_part[:, 0, :], ALU.subtract))
                    split.link(dve, dve.tensor_copy(b_part[:, 1, :], b_rest[:, 0, :]))
                    split.link(dve, dve.tensor_tensor(b_rest[:, 1, :], b_rest[:, 0, :], b_part[:, 1, :], ALU.subtract))
                    dve.tensor_copy(b_part[:, 2, :], b_rest[:, 1, :]).then_inc(bc_ready, 1)
                    split.end()

                def fp8_step(i):
                    dve.wait_ge(v8_ready, i + 1)
                    dve.wait_ge(xq_ready, i)
                    dve.tensor_single_scalar(e8[:].bitcast(I32), v8[:].bitcast(I32), 0x7F800000,
                                             ALU.bitwise_and).then_inc(e8_and, 1)
                    dve.wait_ge(e8_and, i + 1)
                    dve.tensor_scalar(e8[:], e8[:], 2.0 ** -6, 1.5 * 2.0 ** 20, ALU.max, ALU.mult).then_inc(e8_ready, 1)

                def dt_part(i, par):
                    dve.wait_ge(soft_ready, i + 1)
                    dve.wait_ge(dt_st, 16 * i)
                    dve.wait_ge(u_ready, i)
                    dve.scalar_tensor_tensor(out=dtT[:], in0=vb[:], scalar=0.0, in1=soft[:],
                                             op0=ALU.max, op1=ALU.add).then_inc(dt_ready, 1)
                    dve.wait_ge(dt_ready, i + 1)
                    dve.wait_ge(x_ready, i + 1)
                    dve.wait_ge(u_st, 16 * i)
                    dve.tensor_tensor(uT[:], dtT[:], xT[par][:], ALU.mult).then_inc(u_ready, 1)

                def step(i, par, ahead):
                    if ahead >= 1:
                        x_part(i + 1, 1 - par)
                        bc_part(i + 1)
                    if ahead >= 2:
                        normalise(i + 2, par)
                        fp8_step(i + 2)
                    dt_part(i, par)
                    if ahead >= 3:
                        variance(i + 3, 1 - par)

                variance(0, 0)
                normalise(0, 0)
                fp8_step(0)
                variance(1, 1)
                x_part(0, 0)
                bc_part(0)
                normalise(1, 1)
                fp8_step(1)
                variance(2, 0)
                well_ahead(dve, step)

            @block.scalar
            def _(act):
                own = Chain(act_own, 2)

                def front(i):
                    act.wait_ge(xT_psum, i + 1)
                    act.wait_ge(z_psum, i)
                    act.activation(xnT[:], psT[:], ACT.Copy).then_inc(xnT_ready, 1)
                    act.wait_ge(v8_ready, i)
                    act.activation(xb[:], psT[:], ACT.Copy).then_inc(xb_ready, 1)
                    act.wait_ge(xb_ready, i + 1)
                    act.wait_ge(xq_ready, i)
                    act.activation(v8[:], xb[:], ACT.Copy, scale=rsin[:, 0:1]).then_inc(v8_ready, 1)

                act.wait_ge(weights, 80)
                act.wait_ge(rsin_ready, 1)
                def step(i, par, more):
                    own.begin(i)
                    if more:
                        front(i + 1)
                    act.wait_ge(z_psum, i + 1)
                    act.wait_ge(z_st, 16 * i)
                    act.activation(zT[:], psZ[:], ACT.Copy).then_inc(z_ready, 1)
                    act.wait_ge(dt_psum, i + 1)
                    act.wait_ge(dt_ready, i)
                    for h in range(H):
                        act.activation(vb[:, h, :], psD[:, h, :], ACT.Identity, bias=bdt[:, h:h + 1]).then_inc(vb_ready, 1)
                    act.wait_ge(vb_ready, H * i + H)
                    own.link(act, act.activation(mag[:], vb[:], ACT.Abs))
                    own.link(act, act.activation(mag[:], mag[:], ACT.Exp, scale=-1.0))
                    act.activation(soft[:], mag[:], ACT.Ln, bias=1.0).then_inc(soft_ready, 1)
                    own.end()

                front(0)
                one_ahead(act, step)

            @block.tensor
            def _(pe):
                pe.wait_ge(ident_made, 2)
                pe.wait_ge(weights, 80)

                def transposes(i):
                    pe.wait_ge(xn_ready, i + 1)
                    pe.wait_ge(xnT_ready, i)
                    pe.wait_ge(xb_ready, i)
                    for s in range(SUB):
                        for h in range(H):
                            last = pe.transpose(psT[:, h, s * P:(s + 1) * P], xn[:, s, h * P:(h + 1) * P], ident[:])
                    last.then_inc(xT_psum, 1)

                def project(dst, weight, src):
                    for k in range(H):
                        out = pe.matmul(dst, weight[k], src[:, k, :], start=(k == 0), stop=(k == H - 1))
                    return out

                def step(i, par, more):
                    pe.wait_ge(xnT_ready, i + 1)
                    pe.wait_ge(x_ready, i)
                    for h in range(H):
                        last = project(psX[:, h, :], [wxz[:, k, h * P:(h + 1) * P] for k in range(H)], xnT)
                    last.then_inc(x_psum, 1)
                    pe.wait_ge(vb_ready, H * i)
                    project(psD[0:2 * S, 0, :], [wbc[:, k, :] for k in range(H)], xnT).then_inc(bc_psum, 1)
                    pe.wait_ge(z_ready, i)
                    for h in range(H):
                        last = project(psZ[:, h, :], [wxz[:, k, D + h * P:D + (h + 1) * P] for k in range(H)], xnT)
                    last.then_inc(z_psum, 1)
                    if more:
                        transposes(i + 1)
                    pe.wait_ge(bc_ready, i + 1)
                    pe.wait_ge(x_ready, i + 1)
                    for h in range(H):
                        last = project(psD[:, h, :], [wdt[:, k, h * P:(h + 1) * P] for k in range(H)], xT[par])
                    last.then_inc(dt_psum, 1)

                transposes(0)
                one_ahead(pe, step)


def ssm_scan(nc, A):
    DVE_SHARE = T // 4
    with ExitStack() as ctx:
        m = Memory(nc, ctx, "sc")
        a_neg = m.sb("a_neg", [P, H, S])
        a_exp = m.sb("a_exp", [P, H, S])
        skip = m.sb("skip", [P, H])
        ident = m.sb("ident", [P, P])
        pick = m.sb("pick", [3 * 2 * S, 2 * S, P], BF16)
        bc = [m.sb(f"bc{k}", [3 * 2 * S, T], BF16) for k in range(2)]
        dt, u_in, x = ([m.sb(f"{n}{k}", [P, T]) for k in range(2)] for n in ("dt", "u", "x"))
        dec, prod = ([m.sb(f"{n}{k}", [P, T]) for k in range(2)] for n in ("dec", "prod"))
        inp, state = ([m.sb(f"{n}{k}", [P, T]) for k in range(2)] for n in ("inp", "state"))
        y = m.sb("y", [P, T])
        psB = [m.ps(f"psB{k}", [P, T]) for k in range(2)]
        c_row = [m.sb(f"c_row{k}", [P, T]) for k in range(2)]
        own_part, other_part = slice(0, DVE_SHARE), slice(DVE_SHARE, T)
        psC, psY = m.ps("psC", [P, T]), m.ps("psY", [P, T])
        weights, ident_made, pick_made = m.sem("weights"), m.sem("ident_made"), m.sem("pick_made")
        a_made, a_exp_made = m.sem("a_made"), m.sem("a_exp_made")
        loaded = [m.sem(f"loaded{k}") for k in range(2)]
        dec_ready, b_psum, c_psum = m.sem("dec"), m.sem("b_psum"), m.sem("c_psum")
        c_copied = m.sem("c_copied")
        inp_ready, state_ready, prod0_ready, prod1_ready, y_added, y_ready, y_st = (
            m.sem(n) for n in ("inp", "state", "prod0", "prod1", "y_added", "y_ready", "y_st"))
        UNITS = B * H
        bank = T // TILE

        def unit(name, turn, h):
            return A[name].rearrange("h p (b t) -> b h p t", t=T)[turn, h, :, :]

        def steps(eng, step):
            step(0, 0, 0)
            with eng.Fori(0, B - 1) as b:
                for h in range(H):
                    for n in range(1, S):
                        step(b * H + h, h, n)
                    step(b * H + (h + 1), (h + 1) % H, 0)
            for u in range(UNITS - H, UNITS):
                for n in range(1, S):
                    step(u, u % H, n)
                if u + 1 < UNITS:
                    step(u + 1, (u + 1) % H, 0)

        def wait(eng, sem, value):
            if not isinstance(value, int) or value > 0:
                eng.wait_ge(sem, value)

        def loads_of(u, h):
            return (u - h) * (64 // H) + 64

        with nc.Block() as block:
            @block.sync
            def _(sp):
                with nc.allow_non_contiguous_dma(reason="small"):
                    sp.dma_start(a_exp[:], A["a_log"].rearrange("(h p) n -> p h n", p=P)).then_inc(weights, 16)
                    sp.dma_start(skip[:], column(A["d_skip"])).then_inc(weights, 16)

                def load(b, h):
                    parts = A["bc"].rearrange("k r (b t) -> b k r t", t=T)[b, :, :, :]
                    sp.dma_start(bc[h][:], parts.rearrange("k r t -> (k r) t")).then_inc(loaded[h], 16)
                    sp.dma_start(dt[h][:], unit("dt_t", b, h)).then_inc(loaded[h], 16)
                    sp.dma_start(u_in[h][:], unit("u_t", b, h)).then_inc(loaded[h], 16)
                    sp.dma_start(x[h][:], unit("x_t", b, h)).then_inc(loaded[h], 16)

                def store(b, h):
                    sp.wait_ge(y_ready, b * H + (h + 1))
                    m.settle(sp)
                    sp.dma_start(unit("y_t", b, h), y[:]).then_inc(y_st, 16)

                for h in range(H):
                    load(0, h)
                with sp.Fori(0, B - 1) as b:
                    for h in range(H):
                        store(b, h)
                        load(b + 1, h)
                for h in range(H):
                    store(B - 1, h)
                sp.wait_ge(y_st, 16 * UNITS)

            @block.gpsimd
            def _(pool):
                identity(nc, pool, ident, ident_made)
                pool.memset(pick[:], 0.0).then_inc(pick_made, 1)
                for k in range(3):
                    pool.wait_ge(pick_made, k + 1)
                    pool.affine_select(out=pick[:], in_=pick[:], compare_op=ALU.not_equal, fill=1.0,
                                       base=-2 * S * k, pattern=[[-1, 2 * S], [0, P]],
                                       channel_multiplier=1).then_inc(pick_made, 1)

                def step(u, h, n):
                    at = u * S + n
                    pool.wait_ge(state_ready, at + 1)
                    pool.wait_ge(c_copied, at + 1)
                    wait(pool, y_added, at - 1)
                    pool.tensor_tensor(prod[n % 2][:, other_part], state[n % 2][:, other_part], c_row[n % 2][:, other_part],
                                       ALU.mult).then_inc(prod1_ready, 1)

                steps(pool, step)

            @block.scalar
            def _(act):
                act.wait_ge(weights, 32)
                act.activation(a_neg[:], a_exp[:], ACT.Exp).then_inc(a_exp_made, 1)
                act.wait_ge(a_made, 1)

                def step(u, h, n):
                    at = u * S + n
                    if n == 0:
                        act.wait_ge(loaded[h], loads_of(u, h))
                    wait(act, state_ready, at - 1)
                    act.activation(dec[n % 2][:], dt[h][:], ACT.Exp, scale=a_exp[:, h, n:n + 1]).then_inc(dec_ready, 1)
                    act.wait_ge(c_psum, at + 1)
                    wait(act, prod0_ready, at - 1)
                    wait(act, prod1_ready, at - 1)
                    act.activation(c_row[n % 2][:], psC[:], ACT.Copy).then_inc(c_copied, 1)

                steps(act, step)

            @block.tensor
            def _(pe):
                pe.wait_ge(ident_made, 2)
                pe.wait_ge(pick_made, 4)

                def broadcast(dst, h, row):
                    for k in range(bank):
                        out = pe.matmul(dst[:, k * TILE:(k + 1) * TILE], pick[:, row, :],
                                        bc[h][:, k * TILE:(k + 1) * TILE], start=True, stop=True)
                    return out

                def b_row(u, h, n):
                    at = u * S + n
                    if n == 0:
                        pe.wait_ge(loaded[h], loads_of(u, h))
                    wait(pe, inp_ready, at - 1)
                    broadcast(psB[n % 2], h, n).then_inc(b_psum, 1)

                def add(u, n):
                    if n == 0:
                        wait(pe, y_ready, u)
                    pe.wait_ge(prod0_ready, u * S + (n + 1))
                    pe.wait_ge(prod1_ready, u * S + (n + 1))
                    for k in range(bank):
                        out = pe.matmul(psY[:, k * TILE:(k + 1) * TILE], ident[:],
                                        prod[n % 2][:, k * TILE:(k + 1) * TILE], start=(n == 0), stop=(n == S - 1))
                    out.then_inc(y_added, 1)

                def step(u, h, n):
                    at = u * S + n
                    if n + 1 < S:
                        b_row(u, h, n + 1)
                    elif not isinstance(u, int) or u + 1 < UNITS:
                        b_row(u + 1, (h + 1) % H, 0)
                    wait(pe, c_copied, at)
                    broadcast(psC, h, S + n).then_inc(c_psum, 1)
                    if n > 0:
                        add(u, n - 1)
                    elif not isinstance(u, int) or u > 0:
                        add(u - 1, S - 1)

                b_row(0, 0, 0)
                steps(pe, step)
                add(UNITS - 1, S - 1)

            @block.vector
            def _(dve):
                dve.wait_ge(a_exp_made, 1)
                dve.tensor_scalar(a_exp[:], a_neg[:], -1.0, None, ALU.mult).then_inc(a_made, 1)

                def output(u, h):
                    dve.wait_ge(y_added, u * S + S)
                    wait(dve, y_st, 16 * u)
                    dve.scalar_tensor_tensor(out=y[:], in0=x[h][:], scalar=skip[:, h:h + 1], in1=psY[:],
                                             op0=ALU.mult, op1=ALU.add).then_inc(y_ready, 1)

                def scan_input(u, h, n):
                    at = u * S + n
                    if n == 0:
                        dve.wait_ge(loaded[h], loads_of(u, h))
                    dve.wait_ge(b_psum, at + 1)
                    wait(dve, state_ready, at - 1)
                    dve.tensor_tensor(inp[n % 2][:], u_in[h][:], psB[n % 2][:], ALU.mult).then_inc(inp_ready, 1)

                def step(u, h, n):
                    at = u * S + n
                    dve.wait_ge(inp_ready, at + 1)
                    dve.wait_ge(dec_ready, at + 1)
                    wait(dve, prod0_ready, at - 1)
                    wait(dve, prod1_ready, at - 1)
                    dve.tensor_tensor_scan(state[n % 2][:], dec[n % 2][:], inp[n % 2][:], 0.0, ALU.mult, ALU.add).then_inc(state_ready, 1)
                    if n + 1 < S:
                        scan_input(u, h, n + 1)
                    elif not isinstance(u, int) or u + 1 < UNITS:
                        scan_input(u + 1, (h + 1) % H, 0)
                    dve.wait_ge(state_ready, at + 1)
                    dve.wait_ge(c_copied, at + 1)
                    wait(dve, y_added, at - 1)
                    dve.tensor_tensor(prod[n % 2][:, own_part], state[n % 2][:, own_part], c_row[n % 2][:, own_part],
                                      ALU.mult).then_inc(prod0_ready, 1)
                    if n == 0 and (not isinstance(u, int) or u > 0):
                        output(u - 1, (h + 1) % H)

                scan_input(0, 0, 0)
                steps(dve, step)
                output(UNITS - 1, H - 1)


def ssm_output(nc, A):
    with ExitStack() as ctx:
        m = Memory(nc, ctx, "so")
        wout, kern, kq = m.sb("wout", [P, H, D]), m.sb("kern", [P, H, D], BF16), m.sb("kq", [P, H, D], BF16)
        kv, ke, kr = m.sb("kv", [P, H, D]), m.sb("ke", [P, H, D]), m.sb("kr", [P, H, D])
        vth, vbias = m.sb("vth", [P, H]), m.sb("vbias", [P, H])
        bias = m.sb("bias", [P, D], BF16)
        scales, rscale, both = m.sb("scales", [P, 2]), m.sb("rscale", [P, 2]), m.sb("both", [P, 1])
        xmax, per_tok, bad = m.sb("xmax", [P, NP]), m.sb("per_tok", [P, NP]), m.sb("bad", [P, NP])
        tok = [m.sb(f"tok{k}", [P, SUB]) for k in range(2)]
        y, z, xq = ([m.sb(f"{n}{k}", [P, H, TILE], t) for k in range(2)] for n, t in (("y", F32), ("z", F32), ("xq", BF16)))
        x, xn = ([m.sb(f"{n}{k}", [P, SUB, D]) for k in range(2)] for n in ("x", "xn"))
        spike, open_ = m.sb("spike", [P, H, TILE]), m.sb("open", [P, H, TILE])
        ysp, zsp, a = m.sb("ysp", [P, H, TILE]), m.sb("zsp", [P, H, TILE]), [m.sb(f"a{k}", [P, H, TILE]) for k in range(2)]
        g0, g1 = m.sb("g0", [P, SUB, D], BF16), m.sb("g1", [P, SUB, D], BF16)
        gs, gden, grec = (m.sb(n, [P, SUB, D], BF16) for n in ("gs", "gden", "grec"))
        g = [m.sb(f"g{k}_", [P, SUB, D], BF16) for k in range(2)]
        s, sg = [m.sb(f"s{k}", [P, SUB, D]) for k in range(2)], m.sb("sg", [P, SUB, D])
        x1 = [m.sb(f"x1{k}", [P, SUB, D]) for k in range(2)]
        psO = [m.ps(f"psO{k}", [P, SUB, D]) for k in range(2)]
        psG = [m.ps(f"psG{k}", [P, SUB, D]) for k in range(2)]
        weights = m.sem("weights")
        yz_loaded, x_loaded = ([m.sem(f"{n}_loaded{k}") for k in range(2)] for n in ("yz", "x"))
        prep, kq_ready, tok_ready = m.sem("prep"), m.sem("kq"), m.sem("tok_ready")
        vbias_ready = m.sem("vbias")
        spike_ready, open_ready, a_ready, o_psum, g_psum = (m.sem(n) for n in ("spike", "open", "a", "o_psum", "g_psum"))
        g0_ready, g1_ready, gs_ready, x1_ready = (m.sem(n) for n in ("g0", "g1", "gs", "x1_ready"))
        x1_st, gden_ready, grec_ready, g_ready, s_ready, sg_ready = (m.sem(n) for n in ("x1_st", "gden", "grec", "g", "s", "sg"))
        step, dve_own, ysp_ready, zsp_ready = m.sem("step"), m.sem("dve_own"), m.sem("ysp"), m.sem("zsp")

        def tile(name, i):
            return A[name].rearrange("h p (i t) -> i p h t", t=TILE)[i, :, :, :]

        def rows(name, i):
            return A[name].rearrange("(i s p) d -> i p s d", p=P, s=SUB)[i, :, :, :]

        with nc.Block() as block:
            @block.sync
            def _(sp):
                sp.dma_start(wout[:], halves(A["w_out"])).then_inc(weights, 16)
                sp.dma_start(kern[:], halves(A["kern"])).then_inc(weights, 16)
                sp.dma_start(vth[:], column(A["v_th"])).then_inc(weights, 16)
                sp.dma_start(bias[:], spread(A["bias"], D)).then_inc(weights, 16)
                sp.dma_start(scales[:, 0:1], spread(A["s_in"], 1)).then_inc(weights, 16)
                sp.dma_start(scales[:, 1:2], spread(A["s_k"], 1)).then_inc(weights, 16)
                sp.dma_start(xmax[:], A["xmax"]).then_inc(weights, 16)

                def load_yz(i, par):
                    sp.dma_start(y[par][:], tile("y_t", i)).then_inc(yz_loaded[par], 16)
                    sp.dma_start(z[par][:], tile("z_t", i)).then_inc(yz_loaded[par], 16)
                    sp.dma_start(xq[par][:], tile("xq_t", i)).then_inc(yz_loaded[par], 16)

                def load_x(i, par):
                    sp.dma_start(x[par][:], rows("x", i)).then_inc(x_loaded[par], 16)
                    sp.dma_start(xn[par][:], rows("xn0", i)).then_inc(x_loaded[par], 16)

                for i in range(2):
                    load_yz(i, i)
                    load_x(i, i)

                def step(i, par, loads):
                    if loads:
                        sp.wait_ge(o_psum, i + 1)
                        m.settle(sp)
                        load_yz(i + 2, par)
                    sp.wait_ge(x1_ready, i + 1)
                    m.settle(sp)
                    sp.dma_start(rows("x1", i), x1[par][:]).then_inc(x1_st, 16)
                    if loads:
                        load_x(i + 2, par)

                with sp.Fori(0, NT // 2 - 1) as turn:
                    for par in range(2):
                        step(turn * 2 + par, par, True)
                for par in range(2):
                    step(NT - 2 + par, par, False)
                sp.wait_ge(x1_st, 16 * NT)

            @block.gpsimd
            def _(pool):
                for i, par in pairs(pool, NT):
                    pool.wait_ge(s_ready, i + 1)
                    pool.wait_ge(g_ready, i + 1)
                    pool.wait_ge(x1_ready, i)
                    pool.tensor_tensor(sg[:], s[par][:], g[par][:], ALU.mult).then_inc(sg_ready, 1)
                    pool.wait_ge(sg_ready, i + 1)
                    pool.wait_ge(x1_st, 16 * i)
                    pool.tensor_tensor(x1[par][:], sg[:], x[par][:], ALU.add).then_inc(x1_ready, 1)

            @block.scalar
            def _(act):
                act.wait_ge(vbias_ready, 1)

                def front(i, par):
                    act.wait_ge(yz_loaded[par], (i - par) * 24 + 48)
                    act.wait_ge(ysp_ready, i)
                    for h in range(H):
                        act.activation(spike[:, h, :], y[par][:, h, :], ACT.Tanh, bias=vbias[:, h:h + 1],
                                       scale=5.0).then_inc(spike_ready, 1)
                    act.wait_ge(zsp_ready, i)
                    act.activation(open_[:], z[par][:], ACT.Tanh, scale=0.5).then_inc(open_ready, 1)

                def product(i, par):
                    act.wait_ge(g_psum, i + 1)
                    act.wait_ge(tok_ready, i + 1)
                    act.wait_ge(g1_ready, i)
                    for k in range(SUB):
                        act.activation(g0[:, k, :], psG[par][:, k, :], ACT.Copy, scale=tok[par][:, k:k + 1]).then_inc(g0_ready, 1)

                def step(i, par, more):
                    if more:
                        front(i + 1, 1 - par)
                    act.wait_ge(g1_ready, i + 1)
                    act.activation(gs[:], g1[:], ACT.Exp, scale=-1.0).then_inc(gs_ready, 1)
                    act.wait_ge(gs_ready, i + 1)
                    act.wait_ge(grec_ready, i)
                    act.activation(gden[:], gs[:], ACT.Identity, bias=1.0).then_inc(gden_ready, 1)
                    if more:
                        product(i + 1, 1 - par)

                front(0, 0)
                product(0, 0)
                one_ahead(act, step)

            @block.tensor
            def _(pe):
                pe.wait_ge(weights, 112)
                pe.wait_ge(kq_ready, 1)

                def front(i, par):
                    pe.wait_ge(yz_loaded[par], (i - par) * 24 + 48)
                    if not (isinstance(i, int) and i == 0):
                        pe.wait_ge(g0_ready, (i - 1) * SUB)
                    for k in range(SUB):
                        for h in range(H):
                            last = pe.matmul(psG[par][:, k, :], xq[par][:, h, k * P:(k + 1) * P], kq[:, h, :],
                                             start=(h == 0), stop=(h == H - 1))
                    last.then_inc(g_psum, 1)
                    pe.wait_ge(a_ready, i + 1)
                    if not (isinstance(i, int) and i == 0):
                        pe.wait_ge(s_ready, i - 1)
                    for k in range(SUB):
                        for h in range(H):
                            last = pe.matmul(psO[par][:, k, :], a[par][:, h, k * P:(k + 1) * P], wout[:, h, :],
                                             start=(h == 0), stop=(h == H - 1))
                    last.then_inc(o_psum, 1)

                front(0, 0)
                one_ahead(pe, lambda i, par, more: front(i + 1, 1 - par) if more else None)

            @block.vector
            def _(dve):
                dve.wait_ge(weights, 112)
                own = Chain(dve_own, 14)
                own.begin(0)
                own.link(dve, dve.reciprocal(rscale[:], scales[:]))
                own.link(dve, dve.tensor_scalar(kv[:], kern[:], rscale[:, 1:2], None, ALU.mult))
                own.link(dve, dve.tensor_single_scalar(ke[:].bitcast(I32), kv[:].bitcast(I32), 0x7F800000, ALU.bitwise_and))
                own.link(dve, dve.tensor_scalar(ke[:], ke[:], 2.0 ** -6, 1.5 * 2.0 ** 20, ALU.max, ALU.mult))
                own.link(dve, dve.tensor_tensor(kr[:], kv[:], ke[:], ALU.add))
                own.link(dve, dve.tensor_tensor(kr[:], kr[:], ke[:], ALU.subtract))
                own.link(dve, dve.tensor_tensor(kv[:], kv[:], kv[:], ALU.mult))
                own.link(dve, dve.tensor_scalar(kv[:], kv[:], FP8_MAX_TIE ** 2, 3e38, ALU.is_gt, ALU.mult))
                own.link(dve, dve.tensor_scalar(kv[:], kv[:], 3e38, 0.0, ALU.mult, ALU.mult))
                dve.tensor_tensor(kq[:], kr[:], kv[:], ALU.add).then_inc(kq_ready, 1)
                own.link(dve, dve.tensor_scalar(vth[:], vth[:], 0.1, -5.0, ALU.max, ALU.mult))
                dve.tensor_copy(vbias[:], vth[:]).then_inc(vbias_ready, 1)
                own.link(dve, dve.tensor_tensor(both[:], scales[:, 0:1], scales[:, 1:2], ALU.mult))
                own.link(dve, dve.tensor_scalar(bad[:], xmax[:], rscale[:, 0:1], None, ALU.mult))
                own.link(dve, dve.tensor_tensor(bad[:], bad[:], bad[:], ALU.mult))
                own.link(dve, dve.tensor_scalar(bad[:], bad[:], FP8_MAX_TIE ** 2, 3e38, ALU.is_gt, ALU.mult))
                own.n = own.per
                dve.tensor_scalar(bad[:], bad[:], 3e38, 0.0, ALU.mult, ALU.mult).then_inc(prep, 1)
                dve.wait_ge(prep, 1)
                dve.tensor_scalar(per_tok[:], bad[:], both[:, 0:1], None, ALU.add).then_inc(prep, 1)
                dve.wait_ge(prep, 2)

                def front(i, par):
                    dve.tensor_copy(tok[par][:], per_tok[:, bass.ds(i * SUB, SUB)]).then_inc(tok_ready, 1)
                    dve.wait_ge(yz_loaded[par], (i - par) * 24 + 48)
                    dve.wait_ge(spike_ready, H * i + H)
                    dve.wait_ge(a_ready, i)
                    dve.scalar_tensor_tensor(ysp[:], spike[:], 1.0, y[par][:], ALU.add, ALU.mult).then_inc(ysp_ready, 1)
                    dve.wait_ge(open_ready, i + 1)
                    dve.scalar_tensor_tensor(zsp[:], open_[:], 1.0, z[par][:], ALU.add, ALU.mult).then_inc(zsp_ready, 1)
                    dve.wait_ge(zsp_ready, i + 1)
                    dve.wait_ge(ysp_ready, i + 1)
                    dve.wait_ge(o_psum, i)
                    dve.scalar_tensor_tensor(a[par][:], ysp[:], 0.25, zsp[:], ALU.mult, ALU.mult).then_inc(a_ready, 1)

                def step(i, par, more):
                    dve.wait_ge(g0_ready, SUB * i + SUB)
                    dve.wait_ge(gs_ready, i)
                    dve.tensor_tensor(g1[:], g0[:], over_chunks(bias[:]), ALU.add).then_inc(g1_ready, 1)
                    if more:
                        front(i + 1, 1 - par)
                    dve.wait_ge(o_psum, i + 1)
                    dve.wait_ge(x_loaded[par], (i - par) * 16 + 32)
                    dve.wait_ge(sg_ready, i)
                    dve.tensor_tensor(s[par][:], psO[par][:], xn[par][:], ALU.subtract).then_inc(s_ready, 1)
                    dve.wait_ge(gden_ready, i + 1)
                    with nc.allow_low_precision(reason="the reference rounds to bfloat16 here"):
                        dve.reciprocal(grec[:], gden[:]).then_inc(grec_ready, 1)
                    dve.wait_ge(grec_ready, i + 1)
                    dve.tensor_tensor(g[par][:], g1[:], grec[:], ALU.mult).then_inc(g_ready, 1)
                    dve.wait_ge(g_ready, i + 1)

                front(0, 0)
                one_ahead(dve, step)


class Stages:

    def __init__(self, sem, *names):
        self.sem, self.names, self.at = sem, names, 0

    def done(self, ins, name):
        assert self.names[self.at % len(self.names)] == name, (self.names[self.at % len(self.names)], name)
        self.at += 1
        ins.then_inc(self.sem, 1)

    def wait(self, eng, turn, name):
        eng.wait_ge(self.sem, turn * len(self.names) + (self.names.index(name) + 1))

    def wait_before(self, eng, turn):
        eng.wait_ge(self.sem, turn * len(self.names))


def over_chunks(ap, n=SUB):
    return ap.rearrange("p (a d) -> p a d", a=1).to_broadcast([P, n, ap.shape[-1]])


def delta_inputs(nc, A):
    TOK = 3 * C + 2
    with ExitStack() as ctx:
        m = Memory(nc, ctx, "di")
        wtok, btok = m.sb("wtok", [P, H, TOK]), m.sb("btok", [P, TOK])
        wg, bg = m.sb("wg", [P, H, C]), m.sb("bg", [P, 1])
        fq, fk, fv = m.sb("fq", [P, H, P]), m.sb("fk", [P, H, P]), m.sb("fv", [P, H, P])
        fqb, fkb, fvb = m.sb("fqb", [P, 1]), m.sb("fkb", [P, 1]), m.sb("fvb", [P, P])
        fqs = m.sb("fqs", [P, 1])
        ident, half = m.sb("ident", [P, P]), m.sb("half", [P, SUB])
        x = [m.sb(f"x{k}", [P, SUB, D]) for k in range(2)]
        xn = [m.sb(f"xn{k}", [P, SUB, D]) for k in range(2)]
        stats, mv = m.sb("stats", [P, SUB, 6]), m.sb("mv", [P, SUB, 2])
        ve, rstd = m.sb("ve", [P, SUB]), m.sb("rstd", [P, SUB])
        xnT = [m.sb(f"xnT{k}", [P, H, TILE]) for k in range(2)]
        tok = [m.sb(f"tok{k}", [P, SUB, TOK]) for k in range(2)]
        square, ss, rk = m.sb("square", [P, C]), m.sb("ss", [P, SUB]), m.sb("rk", [P, SUB])
        khat, gate, vf = m.sb("khat", [P, SUB, C]), m.sb("gate", [P, TILE]), m.sb("vf", [P, SUB, P])
        qk, rest = m.sb("qk", [P, 2, TILE]), m.sb("rest", [P, 2, 2, TILE])
        part = m.sb("part", [P, 3, 2, TILE], BF16)
        psT, psTok = m.ps("psT", [P, H, TILE]), m.ps("psTok", [P, 2, TILE])
        psV, psG, psQ, psK = (m.ps(n, [P, TILE]) for n in ("psV", "psG", "psQ", "psK"))
        weights, fqs_ready, ident_made, half_made = (m.sem(n) for n in ("weights", "fqs", "ident", "half"))
        loaded = [m.sem(f"loaded{k}") for k in range(2)]
        xn_st, khat_st, gate_st, vf_st, part_st = (m.sem(f"{n}_st") for n in ("xn", "khat", "gate", "vf", "part"))
        tok_st = [m.sem(f"tok_st{k}") for k in range(2)]
        pe_front, act_front = Stages(m.sem("pe_front"), "xT"), Stages(m.sem("act_front"), "xnT")
        dve_front, pool_front = Stages(m.sem("dve_front"), "stats", "var", "xn"), Stages(m.sem("pool_front"), "ve", "rstd")
        pe_at = Stages(m.sem("pe_at"), "tok01", "gate", "fq", "fk", "fv", "tok23")
        dve_own, khat_own, square_done = m.sem("dve_own"), m.sem("khat_own"), m.sem("square_done")
        dve_at = Stages(m.sem("dve_at"), "tok01", "vf", "tok23")
        dve_khat = Stages(m.sem("dve_khat"), "khat")
        act_qk = Stages(m.sem("act_qk"), "gate", "fq", "fk")
        act_at = Stages(m.sem("act_at"), "part0", "ss", "part1", "part2")
        pool_at = Stages(m.sem("pool_at"), "rest0", "rk0", "rk", "rest1")

        def rows(name, i):
            return A[name].rearrange("(i s p) d -> i p s d", p=P, s=SUB)[i, :, :, :]

        with nc.Block() as block:
            @block.sync
            def _(sp):
                with nc.allow_non_contiguous_dma(reason="small"):
                    for dst, src in ((wtok[:], halves(A["w_tok"])), (btok[:], spread(A["b_tok"], TOK)),
                                     (wg[:], halves(A["w_gate"])), (bg[:], A["b_gate"].rearrange("(p a) -> p a", a=1)),
                                     (fq[:], halves(A["fq"])), (fk[:], halves(A["fk"])), (fv[:], halves(A["fv"])),
                                     (fqb[:], A["fqb"].rearrange("(p a) -> p a", a=1)),
                                     (fkb[:], A["fkb"].rearrange("(p a) -> p a", a=1)), (fvb[:], spread(A["fvb"], P))):
                        sp.dma_start(dst, src).then_inc(weights, 16)

                def load(i, par):
                    sp.dma_start(x[par][:], rows("x1", i)).then_inc(loaded[par], 16)

                def front(i, par, loads=True):
                    dve_front.wait(sp, i, "xn")
                    m.settle(sp)
                    sp.dma_start(rows("xn1", i), xn[par][:]).then_inc(xn_st, 16)
                    if loads:
                        load(i + 2, par)

                def step(i, par, more):
                    if more:
                        front(i + 1, 1 - par, not isinstance(i, int) or i + 3 < NT)
                    dve_khat.wait(sp, i, "khat")
                    m.settle(sp)
                    sp.dma_start(rows("vf", i), vf[:]).then_inc(vf_st, 16)
                    sp.dma_start(rows("qd", i), tok[par][:, :, 0:C]).then_inc(tok_st[par], 16)
                    sp.dma_start(rows("vd", i), tok[par][:, :, 2 * C:3 * C]).then_inc(tok_st[par], 16)
                    sp.dma_start(A["ab"].rearrange("p (i s) c -> i p s c", s=SUB)[i, :, :, :],
                                 tok[par][:, :, 3 * C:TOK]).then_inc(tok_st[par], 16)
                    sp.dma_start(rows("kd", i), khat[:]).then_inc(khat_st, 16)

                load(0, 0)
                load(1, 1)
                front(0, 0)
                with sp.Fori(0, NT // 2 - 2) as turn:
                    for par in range(2):
                        step(turn * 2 + par, par, True)
                for i in range(NT - 4, NT):
                    step(i, i % 2, i < NT - 1)
                for sem, n in ((xn_st, NT), (tok_st[0], 3 * NT // 2), (tok_st[1], 3 * NT // 2), (khat_st, NT), (gate_st, NT),
                               (vf_st, NT), (part_st, 2 * (NH // 4) * NT)):
                    sp.wait_ge(sem, 16 * n)
                    m.settle(sp)

            @block.gpsimd
            def _(pool):
                identity(nc, pool, ident, ident_made)
                pool.memset(half[:], -0.5).then_inc(half_made, 1)
                pool.wait_ge(half_made, 1)

                def front(i):
                    dve_front.wait(pool, i, "var")
                    m.settle(pool)
                    pool_front.done(pool.tensor_scalar_add(ve[:], mv[:, :, 1], EPS), "ve")
                    pool_front.wait(pool, i, "ve")
                    pool_front.done(pool.tensor_tensor(rstd[:], ve[:], half[:], ALU.pow), "rstd")

                def step(i, par, more):
                    if more:
                        dve_front.wait(pool, i, "xn")
                        front(i + 1)
                    act_at.wait(pool, i, "part0")
                    dve_khat.wait_before(pool, i)
                    pool_at.done(pool.tensor_tensor(rest[:, 0, :, :], qk[:], part[:, 0, :, :], ALU.subtract), "rest0")
                    act_at.wait(pool, i, "ss")
                    pool_at.done(pool.tensor_tensor(rk[:], ss[:], half[:], ALU.pow), "rk0")
                    pool_at.wait(pool, i, "rk0")
                    m.settle(pool)
                    pool_at.done(pool.tensor_scalar_min(rk[:], rk[:], 1e12), "rk")
                    act_at.wait(pool, i, "part1")
                    pool_at.done(pool.tensor_tensor(rest[:, 1, :, :], rest[:, 0, :, :], part[:, 1, :, :], ALU.subtract), "rest1")

                front(0)
                one_ahead(pool, step)

            @block.scalar
            def _(act):
                act.wait_ge(fqs_ready, 1)
                act.wait_ge(weights, 160)
                def front(i, par):
                    pe_front.wait(act, i, "xT")
                    act_front.done(act.activation(xnT[par][:], psT[:], ACT.Copy), "xnT")

                def step(b, par, more=True):
                    i = b * 2 + par
                    pe_at.wait(act, i, "gate")
                    act.wait_ge(gate_st, 16 * i)
                    act_qk.done(act.activation(gate[:], psG[:], ACT.Sigmoid, bias=bg[:, 0:1]), "gate")
                    act_qk.wait(act, i, "gate")
                    act.dma_start(A["gate_t"].rearrange("c (i t) -> i c t", t=TILE)[i, :, :], gate[:]).then_inc(gate_st, 16)
                    pe_at.wait(act, i, "fq")
                    pool_at.wait_before(act, i)
                    act_qk.done(act.activation(qk[:, 0, :], psQ[:], ACT.Identity, bias=fqs[:, 0:1], scale=float(HD) ** -0.5), "fq")
                    pe_at.wait(act, i, "fk")
                    act_qk.done(act.activation(qk[:, 1, :], psK[:], ACT.Identity, bias=fkb[:, 0:1]), "fk")
                    act_qk.wait(act, i, "fk")
                    act.wait_ge(part_st, 2 * (NH // 4) * 16 * i)
                    act_at.done(act.activation(part[:, 0, :, :], qk[:], ACT.Copy), "part0")
                    if more:
                        front(i + 1, 1 - par)
                    dve_at.wait(act, i, "tok23")
                    for s in range(SUB):
                        if s:
                            act.wait_ge(square_done, i * (SUB - 1) + s)
                        ins = act.activation(square[:], tok[par][:, s, C:2 * C], ACT.Square, accum_out=ss[:, s:s + 1])
                        if s < SUB - 1:
                            ins.then_inc(square_done, 1)
                        else:
                            act_at.done(ins, "ss")
                    pool_at.wait(act, i, "rest0")
                    act_at.done(act.activation(part[:, 1, :, :], rest[:, 0, :, :], ACT.Copy), "part1")
                    pool_at.wait(act, i, "rest1")
                    act_at.done(act.activation(part[:, 2, :, :], rest[:, 1, :, :], ACT.Copy), "part2")
                    act_at.wait(act, i, "part2")
                    for n, name in enumerate(("qs", "ks")):
                        for j in range(NH // 4):
                            dst = A[name].rearrange("b j k q (s t) -> b j s q k t", t=TILE)[b, j, par, :, :, :]
                            act.dma_start(dst, part[j * 32:(j + 1) * 32, :, n, :]).then_inc(part_st, 16)

                front(0, 0)
                with act.Fori(0, B - 1) as b:
                    for par in range(T // TILE):
                        step(b, par)
                step(B - 1, 0)
                step(B - 1, 1, False)

            @block.tensor
            def _(pe):
                pe.wait_ge(ident_made, 2)
                pe.wait_ge(weights, 160)

                def front(i, par):
                    dve_front.wait(pe, i, "xn")
                    act_front.wait_before(pe, i)
                    for s in range(SUB):
                        for h in range(H):
                            last = pe.transpose(psT[:, h, s * P:(s + 1) * P], xn[par][:, s, h * P:(h + 1) * P], ident[:])
                    pe_front.done(last, "xT")

                def step(i, par, more):
                    act_front.wait(pe, i, "xnT")
                    act_qk.wait_before(pe, i)

                    def tokens(dst, weight, s):
                        for h in range(H):
                            out = pe.matmul(dst, xnT[par][:, h, s * P:(s + 1) * P], weight[:, h, :], start=(h == 0), stop=(h == H - 1))
                        return out

                    def features(dst, weight):
                        for h in range(H):
                            out = pe.matmul(dst, weight[:, h, :], xnT[par][:, h, :], start=(h == 0), stop=(h == H - 1))
                        return out

                    dve_at.wait_before(pe, i)
                    tokens(psTok[:, 0, 0:TOK], wtok, 0)
                    pe_at.done(tokens(psTok[:, 1, 0:TOK], wtok, 1), "tok01")
                    pe_at.done(features(psG[:], wg), "gate")
                    pe_at.done(features(psQ[:], fq), "fq")
                    pe_at.done(features(psK[:], fk), "fk")
                    for s in range(SUB):
                        last = tokens(psV[:, s * P:(s + 1) * P], fv, s)
                    pe_at.done(last, "fv")
                    if more:
                        front(i + 1, 1 - par)
                    dve_at.wait(pe, i, "tok01")
                    tokens(psTok[:, 0, 0:TOK], wtok, 2)
                    pe_at.done(tokens(psTok[:, 1, 0:TOK], wtok, 3), "tok23")

                front(0, 0)
                one_ahead(pe, step)

            @block.vector
            def _(dve):
                own, khat_chain = Chain(dve_own, 3 * (SUB - 1)), Chain(khat_own, SUB - 1)
                dve.wait_ge(weights, 160)
                dve.tensor_scalar(fqs[:], fqb[:], float(HD) ** -0.5, None, ALU.mult).then_inc(fqs_ready, 1)

                def variance(i, par):
                    own.begin(i)
                    dve.wait_ge(loaded[par], (i - par) * 8 + 16)
                    for s in range(SUB):
                        ins = dve.bn_stats(stats[:, s, :], x[par][:, s, :])
                        own.mark(ins) if s < SUB - 1 else dve_front.done(ins, "stats")
                    own.wait(dve)
                    dve_front.wait(dve, i, "stats")
                    pool_front.wait_before(dve, i)
                    for s in range(SUB):
                        m.settle(dve)
                        ins = dve.bn_aggr(mv[:, s, :], stats[:, s, :])
                        own.mark(ins) if s < SUB - 1 else dve_front.done(ins, "var")
                    own.wait(dve)

                def normalise(i, par):
                    own.base, own.n = i * own.per, 2 * (SUB - 1)
                    dve_front.wait(dve, i, "var")
                    pool_front.wait(dve, i, "rstd")
                    pe_front.wait_before(dve, i)
                    dve.wait_ge(xn_st, 16 * i)
                    for s in range(SUB):
                        ins = dve.tensor_scalar(xn[par][:, s, :], x[par][:, s, :], mv[:, s, 0:1], rstd[:, s:s + 1],
                                                ALU.subtract, ALU.mult)
                        own.mark(ins) if s < SUB - 1 else dve_front.done(ins, "xn")
                    own.end()

                def step(i, par, more):
                    pe_at.wait(dve, i, "tok01")
                    dve.wait_ge(tok_st[par], (i - par) * 24)
                    dve_at.done(dve.tensor_tensor(tok[par][:, 0:2, :], psTok[:, :, 0:TOK], over_chunks(btok[:], 2), ALU.add), "tok01")
                    if more:
                        normalise(i + 1, 1 - par)
                    pe_at.wait(dve, i, "fv")
                    dve.wait_ge(vf_st, 16 * i)
                    dve_at.done(dve.tensor_tensor(vf[:], psV[:].rearrange("p (s c) -> p s c", s=SUB), over_chunks(fvb[:]), ALU.add), "vf")
                    pe_at.wait(dve, i, "tok23")
                    dve_at.done(dve.tensor_tensor(tok[par][:, 2:4, :], psTok[:, :, 0:TOK], over_chunks(btok[:], 2), ALU.add), "tok23")
                    if more and not (isinstance(i, int) and i == NT - 2):
                        variance(i + 2, par)
                    pool_at.wait(dve, i, "rk")
                    dve.wait_ge(khat_st, 16 * i)
                    khat_chain.begin(i)
                    for s in range(SUB):
                        ins = dve.tensor_scalar(khat[:, s, :], tok[par][:, s, C:2 * C], rk[:, s:s + 1], None, ALU.mult)
                        khat_chain.mark(ins) if s < SUB - 1 else dve_khat.done(ins, "khat")
                    khat_chain.end()
                    khat_chain.wait(dve)

                variance(0, 0)
                normalise(0, 0)
                variance(1, 1)
                one_ahead(dve, step)


def delta_invert(nc, A):
    with ExitStack() as ctx:
        m = Memory(nc, ctx, "dv")
        ident, ones, tri, strict = (m.sb(n, [P, P]) for n in ("ident", "ones", "tri", "strict"))
        same = [m.sb(f"same{w}", [P, P]) for w in (16, 32, 64)]
        ring = [m.sb(f"ring{k}", [P, P]) for k in range(3)]
        ab = m.sb("ab", [P, NP, 2])
        mag, soft, la, be = (m.sb(n, [P, NP]) for n in ("mag", "soft", "la", "be"))
        g, gl, diff, dw = (m.sb(n, [P, NP]) for n in ("g", "gl", "diff", "dw"))
        dec = m.sb("dec", [P, NP, NDEC])
        W = [P, SUB, P]
        two = range(2)
        kd, qd, qg = ([m.sb(f"{n}{k}", W) for k in two] for n in ("kd", "qd", "qg"))
        col = [m.sb(f"col{k}", [P, SUB, NDEC]) for k in two]
        tl, df, dd, ds, dm = ([m.sb(f"{n}{k}", W) for k in two] for n in ("tl", "df", "dd", "ds", "dm"))
        kt, qt, qgt = ([m.sb(f"{n}{k}", W) for k in two] for n in ("kt", "qt", "qgt"))
        nf, ntf, nb, ntb = ([m.sb(f"{n}{k}", W) for k in two] for n in ("nf", "ntf", "nb", "ntb"))
        nto = [[m.sb(f"nto{k}{l}", W) for l in range(3)] for k in two]
        n2, n2t, n4, n4t, n8t = ([m.sb(f"{n}{k}", W) for k in two] for n in ("n2", "n2t", "n4", "n4t", "n8t"))
        z, xt = ([m.sb(f"{n}{k}", W) for k in two] for n in ("z", "xt"))
        X = [[m.sb(f"X{k}{l}", W) for l in range(2)] for k in two]
        ps = [[m.ps(f"ps{k}{l}", W) for l in range(4)] for k in two]
        loaded = [m.sem(f"loaded{k}") for k in two]
        ab_in, masks, pre_act, pre_dve, pre_pe = (m.sem(n) for n in ("ab_in", "masks", "pre_act", "pre_dve", "pre_pe"))
        own = [m.sem(f"own{k}") for k in two]
        act_own = [m.sem(f"act_own{k}") for k in two]
        st = [m.sem(f"st{k}") for k in two]
        dec_st = m.sem("dec_st")
        pe_at = [Stages(m.sem(f"pe_at{k}"), "kT", "qT", "gbc", "gram", "qgT", "nT", "n2", "n2t", "x1", "n4", "n4t", "x2", "n8t", "x3",
                        "z0", "xt0", "y0", "z1", "xt1", "y1", "z2", "xt2", "y2") for k in two]
        act_at = [Stages(m.sem(f"act_at{k}"), "qg", "qt", "dd", "qgt", "ntf", "n2", "n4", "n8t", "z0", "z1", "z2") for k in two]
        dve_at = [Stages(m.sem(f"dve_at{k}"), "col", "tl", "kt", "df", "nf", "nb", "x0", "ntb", "n2t", "x1", "n4t", "x2", "x3",
                         "xt0", "y0", "xt1", "y1", "xt2", "y2") for k in two]
        pool_at = [Stages(m.sem(f"pool_at{k}"), "ds", "dm", "nto0", "nto1", "nto2") for k in two]

        def rows(name, i):
            return A[name].rearrange("(i s p) d -> i p s d", p=P, s=SUB)[i, :, :, :]

        def mats(name, i):
            return A[name].rearrange("(i s) p d -> i p s d", s=SUB)[i, :, :, :]

        with nc.Block() as block:
            @block.sync
            def _(sp):
                sp.dma_start(ab[:], A["ab"]).then_inc(ab_in, 16)

                def load(turn, par):
                    i = turn * 2 + par
                    sp.dma_start(kd[par][:], rows("kd", i)).then_inc(loaded[par], 16)
                    sp.dma_start(qd[par][:], rows("qd", i)).then_inc(loaded[par], 16)

                def step(turn, more):
                    for par in two:
                        i = turn * 2 + par
                        pe_at[par].wait(sp, turn, "qgT")
                        m.settle(sp)
                        if more:
                            load(turn + 1, par)
                        for at, stage, name, buf in ((pool_at, "dm", "dm", dm), (dve_at, "kt", "kt", kt), (act_at, "qt", "qt", qt),
                                                     (act_at, "qgt", "qgt", qgt)):
                            at[par].wait(sp, turn, stage)
                            m.settle(sp)
                            sp.dma_start(mats(name, i), buf[par][:]).then_inc(st[par], 16)
                    for par in two:
                        dve_at[par].wait(sp, turn, "y2")
                        m.settle(sp)
                        sp.dma_start(mats("inv", turn * 2 + par), X[par][0][:]).then_inc(st[par], 16)

                for par in two:
                    load(0, par)
                with sp.Fori(0, NT // 2 - 1) as turn:
                    step(turn, True)
                step(NT // 2 - 1, False)
                for par in two:
                    sp.wait_ge(st[par], 80 * (NT // 2))
                    m.settle(sp)
                sp.wait_ge(dec_st, 16)

            @block.gpsimd
            def _(pool):
                pool.memset(ones[:], 1.0).then_inc(masks, 1)
                pool.memset(ident[:], 0.0).then_inc(masks, 1)
                for t_ in same:
                    pool.memset(t_[:], 1.0).then_inc(masks, 1)
                pool.wait_ge(masks, 5)
                pool.affine_select(out=ident[:], in_=ident[:], compare_op=ALU.not_equal, fill=1.0, base=0,
                                   pattern=[[-1, P]], channel_multiplier=1).then_inc(masks, 1)
                pool.affine_select(out=tri[:], in_=ones[:], compare_op=ALU.is_ge, fill=0.0, base=0,
                                   pattern=[[1, P]], channel_multiplier=-1).then_inc(masks, 1)
                pool.affine_select(out=strict[:], in_=ones[:], compare_op=ALU.is_ge, fill=0.0, base=-1,
                                   pattern=[[1, P]], channel_multiplier=-1).then_inc(masks, 1)
                for w, t_ in zip((16, 32, 64), same):
                    view = t_[:].rearrange("p (n w) -> p n w", w=w)
                    pool.affine_select(out=view, in_=view, compare_op=ALU.is_ge, fill=0.0, base=0,
                                       pattern=[[-w, P // w], [0, w]], channel_multiplier=1).then_inc(masks, 1)
                pool.wait_ge(masks, 11)
                for w, t_ in zip((16, 32, 64), same):
                    view = t_[:].rearrange("p (n w) -> p n w", w=w)
                    pool.affine_select(out=view, in_=view, compare_op=ALU.is_ge, fill=0.0, base=w - 1,
                                       pattern=[[w, P // w], [0, w]], channel_multiplier=-1).then_inc(masks, 1)
                pool.wait_ge(masks, 14)
                wide = [same[1], same[2], ones]
                for k in range(3):
                    pool.tensor_tensor(ring[k][:], wide[k][:], same[k][:], ALU.subtract).then_inc(masks, 1)
                pool.wait_ge(masks, 17)
                pool.wait_ge(pre_dve, 10)
                m.settle(pool)
                pool.dma_start(A["dec"], dec[:]).then_inc(dec_st, 16)
                with pool.Fori(0, NT // 2) as turn:
                    for par in two:
                        act_at[par].wait(pool, turn, "dd")
                        dve_at[par].wait_before(pool, turn)
                        pool.wait_ge(st[par], turn * 80)
                        pool_at[par].done(pool.tensor_tensor(ds[par][:], dd[par][:], over_chunks(strict[:]), ALU.mult), "ds")
                        pool_at[par].wait(pool, turn, "ds")
                        pool_at[par].done(pool.tensor_tensor(dm[par][:], ds[par][:], over_chunks(ident[:]), ALU.add), "dm")
                    for par in two:
                        act_at[par].wait(pool, turn, "ntf")
                        pe_at[par].wait_before(pool, turn)
                        for l in range(3):
                            pool_at[par].done(pool.tensor_tensor(nto[par][l][:], ntf[par][:], over_chunks(ring[l][:]), ALU.mult), f"nto{l}")

            @block.scalar
            def _(act):
                act.wait_ge(ab_in, 16)
                act.activation(mag[:], ab[:, :, 0], ACT.Abs).then_inc(pre_act, 1)
                act.wait_ge(pre_act, 1)
                act.activation(mag[:], mag[:], ACT.Exp, scale=-1.0).then_inc(pre_act, 1)
                act.activation(be[:], ab[:, :, 1], ACT.Exp, scale=-1.0).then_inc(pre_act, 1)
                act.wait_ge(pre_act, 2)
                act.activation(soft[:], mag[:], ACT.Ln, bias=1.0).then_inc(pre_act, 1)
                act.wait_ge(pre_dve, 5)
                act.activation(dec[:, :, EXP_G], g[:], ACT.Exp).then_inc(pre_act, 1)
                act.activation(dec[:, :, EXP_END], gl[:], ACT.Exp).then_inc(pre_act, 1)
                act.activation(dw[:], diff[:], ACT.Exp).then_inc(pre_act, 1)
                with act.Fori(0, NT // 2) as turn:
                    for par in two:
                        act.wait_ge(loaded[par], turn * 32 + 32)
                        dve_at[par].wait(act, turn, "col")
                        pe_at[par].wait_before(act, turn)
                        act.wait_ge(st[par], turn * 80)
                        for s in range(SUB):
                            ins = act.activation(qg[par][:, s, :], qd[par][:, s, :], ACT.Copy, scale=col[par][:, s, EXP_G:EXP_G + 1])
                            if s < SUB - 1:
                                ins.then_inc(act_own[par], 1)
                        act.wait_ge(act_own[par], turn * (SUB - 1) + SUB - 1)
                        act_at[par].done(ins, "qg")
                    for par in two:
                        pe_at[par].wait(act, turn, "qT")
                        act_at[par].done(act.activation(qt[par][:], ps[par][1][:], ACT.Copy), "qt")
                    for par in two:
                        dve_at[par].wait(act, turn, "df")
                        pool_at[par].wait_before(act, turn)
                        act_at[par].done(act.activation(dd[par][:], df[par][:], ACT.Exp), "dd")
                    for par in two:
                        pe_at[par].wait(act, turn, "qgT")
                        act_at[par].done(act.activation(qgt[par][:], ps[par][2][:], ACT.Copy), "qgt")
                    for par in two:
                        pe_at[par].wait(act, turn, "nT")
                        dve_at[par].wait_before(act, turn)
                        act_at[par].done(act.activation(ntf[par][:], ps[par][1][:], ACT.Copy), "ntf")
                    for name, dst, bank in (("n2", n2, 0), ("n4", n4, 3), ("n8t", n8t, 1)):
                        for par in two:
                            pe_at[par].wait(act, turn, name)
                            act_at[par].done(act.activation(dst[par][:], ps[par][bank][:], ACT.Copy), name)
                    for l in range(3):
                        for par in two:
                            pe_at[par].wait(act, turn, f"z{l}")
                            act_at[par].done(act.activation(z[par][:], ps[par][3][:], ACT.Copy), f"z{l}")

            @block.tensor
            def _(pe):
                pe.wait_ge(masks, 17)
                pe.wait_ge(pre_dve, 2)
                pe.matmul(ps[0][0][:, 0, 0:NP], tri[:], la[:], start=True, stop=True).then_inc(pre_pe, 1)
                pe.matmul(ps[0][1][:, 0, 0:NP], ones[:], la[:], start=True, stop=True).then_inc(pre_pe, 1)
                pe.wait_ge(pre_dve, 5)

                def each(par, bank, left, right, name):
                    for s in range(SUB):
                        out = pe.matmul(ps[par][bank][:, s, :], left[:, s, :], right[:, s, :], start=True, stop=True)
                    pe_at[par].done(out, name)

                def turned(par, bank, src, name):
                    for s in range(SUB):
                        out = pe.transpose(ps[par][bank][:, s, :], src[:, s, :], ident[:])
                    pe_at[par].done(out, name)

                with pe.Fori(0, NT // 2) as turn:
                    for par in two:
                        pe.wait_ge(loaded[par], turn * 32 + 32)
                        dve_at[par].wait_before(pe, turn)
                        act_at[par].wait_before(pe, turn)
                        turned(par, 0, kd[par], "kT")
                        turned(par, 1, qd[par], "qT")
                        dve_at[par].wait(pe, turn, "tl")
                        pe_at[par].done(pe.matmul(ps[par][3][:], ones[:], tl[par][:], start=True, stop=True), "gbc")
                    for par in two:
                        dve_at[par].wait(pe, turn, "kt")
                        each(par, 0, kt[par], kt[par], "gram")
                        act_at[par].wait(pe, turn, "qg")
                        turned(par, 2, qg[par], "qgT")
                    for par in two:
                        dve_at[par].wait(pe, turn, "nf")
                        act_at[par].wait(pe, turn, "qt")
                        turned(par, 1, nf[par], "nT")
                    for par in two:
                        dve_at[par].wait(pe, turn, "ntb")
                        each(par, 0, ntb[par], nb[par], "n2")
                        act_at[par].wait(pe, turn, "ntf")
                        each(par, 1, nb[par], ntb[par], "n2t")
                    for par in two:
                        dve_at[par].wait(pe, turn, "n2t")
                        act_at[par].wait(pe, turn, "n2")
                        each(par, 2, n2t[par], X[par][0], "x1")
                        each(par, 3, n2t[par], n2[par], "n4")
                        each(par, 0, n2[par], n2t[par], "n4t")
                    for par in two:
                        dve_at[par].wait(pe, turn, "n4t")
                        act_at[par].wait(pe, turn, "n4")
                        each(par, 2, n4t[par], X[par][1], "x2")
                        each(par, 1, n4[par], n4t[par], "n8t")
                    for par in two:
                        act_at[par].wait(pe, turn, "n8t")
                        dve_at[par].wait(pe, turn, "x2")
                        each(par, 2, n8t[par], X[par][0], "x3")
                    for l in range(3):
                        cur = (l + 1) % 2
                        for par in two:
                            dve_at[par].wait(pe, turn, "x3" if l == 0 else f"y{l - 1}")
                            pool_at[par].wait(pe, turn, f"nto{l}")
                            if l:
                                act_at[par].wait(pe, turn, f"z{l - 1}")
                            each(par, 3, nto[par][l], X[par][cur], f"z{l}")
                            turned(par, 1, X[par][cur], f"xt{l}")
                        for par in two:
                            act_at[par].wait(pe, turn, f"z{l}")
                            dve_at[par].wait(pe, turn, f"xt{l}")
                            each(par, 2, xt[par], z[par], f"y{l}")

            @block.vector
            def _(dve):
                dve.wait_ge(pre_act, 4)
                dve.scalar_tensor_tensor(out=la[:], in0=ab[:, :, 0], scalar=0.0, in1=soft[:], op0=ALU.min,
                                         op1=ALU.subtract).then_inc(pre_dve, 1)
                dve.tensor_scalar(be[:], be[:], 1.0, None, ALU.add).then_inc(pre_dve, 1)
                dve.wait_ge(pre_pe, 2)
                dve.tensor_copy(g[:], ps[0][0][:, 0, 0:NP]).then_inc(pre_dve, 1)
                dve.tensor_copy(gl[:], ps[0][1][:, 0, 0:NP]).then_inc(pre_dve, 1)
                dve.wait_ge(pre_dve, 4)
                dve.tensor_tensor(diff[:], gl[:], g[:], ALU.subtract).then_inc(pre_dve, 1)
                dve.reciprocal(dec[:, :, BETA], be[:]).then_inc(pre_dve, 1)
                dve.tensor_copy(dec[:, :, LOG_A], la[:]).then_inc(pre_dve, 1)
                dve.tensor_copy(dec[:, :, LOG_G], g[:]).then_inc(pre_dve, 1)
                dve.wait_ge(pre_act, 7)
                dve.tensor_scalar(dec[:, :, NEG_EXP_G], dec[:, :, EXP_G], -1.0, None, ALU.mult).then_inc(pre_dve, 1)
                dve.wait_ge(pre_dve, 6)
                dve.tensor_tensor(dec[:, :, TO_END_BETA], dw[:], dec[:, :, BETA], ALU.mult).then_inc(pre_dve, 1)
                dve.wait_ge(pre_dve, 10)
                dve.wait_ge(masks, 17)
                with dve.Fori(0, NT // 2) as turn:
                    def parts(par, op, count, name):
                        for s in range(SUB):
                            ins = op(s)
                            if s < SUB - 1:
                                ins.then_inc(own[par], 1)
                        dve.wait_ge(own[par], turn * 3 * (SUB - 1) + count * (SUB - 1))
                        dve_at[par].done(ins, name)

                    for par in two:
                        act_at[par].wait_before(dve, turn)
                        dve_at[par].done(dve.tensor_copy(col[par][:], dec[:, bass.ds((turn * 2 + par) * SUB, SUB), :]), "col")
                        dve_at[par].wait(dve, turn, "col")
                        pe_at[par].wait_before(dve, turn)
                        parts(par, lambda s: dve.tensor_scalar(tl[par][:, s, :], tri[:], col[par][:, s, LOG_A:LOG_A + 1], None, ALU.mult), 1, "tl")
                    for par in two:
                        pe_at[par].wait(dve, turn, "kT")
                        dve.wait_ge(st[par], turn * 80)
                        dve_at[par].done(dve.tensor_copy(kt[par][:], ps[par][0][:]), "kt")
                    for par in two:
                        pe_at[par].wait(dve, turn, "gbc")
                        parts(par, lambda s: dve.tensor_scalar(df[par][:, s, :], ps[par][3][:, s, :], col[par][:, s, LOG_G:LOG_G + 1],
                                                               0.0, ALU.subtract, ALU.min), 2, "df")
                    for par in two:
                        pe_at[par].wait(dve, turn, "gram")
                        pool_at[par].wait(dve, turn, "ds")
                        parts(par, lambda s: dve.scalar_tensor_tensor(
                            out=nf[par][:, s, :], in0=ps[par][0][:, s, :], scalar=col[par][:, s, BETA:BETA + 1],
                            in1=ds[par][:, s, :], op0=ALU.mult, op1=ALU.mult), 3, "nf")
                        dve_at[par].wait(dve, turn, "nf")
                        dve_at[par].done(dve.tensor_tensor(nb[par][:], nf[par][:], over_chunks(same[0][:]), ALU.mult), "nb")
                        dve_at[par].wait(dve, turn, "nb")
                        dve_at[par].done(dve.tensor_tensor(X[par][0][:], over_chunks(ident[:]), nb[par][:], ALU.subtract), "x0")
                    for par in two:
                        act_at[par].wait(dve, turn, "ntf")
                        dve_at[par].done(dve.tensor_tensor(ntb[par][:], ntf[par][:], over_chunks(same[0][:]), ALU.mult), "ntb")
                    for par in two:
                        pe_at[par].wait(dve, turn, "n2t")
                        dve_at[par].done(dve.tensor_copy(n2t[par][:], ps[par][1][:]), "n2t")
                    for k, (name, bank, last) in enumerate((("x1", 2, "n4t"), ("x2", 2, None), ("x3", 2, None))):
                        for par in two:
                            pe_at[par].wait(dve, turn, name)
                            dve_at[par].wait(dve, turn, "x0" if k == 0 else f"x{k}")
                            dve_at[par].done(dve.tensor_tensor(X[par][(k + 1) % 2][:], X[par][k % 2][:], ps[par][2][:], ALU.add), name)
                            if last:
                                pe_at[par].wait(dve, turn, last)
                                dve_at[par].done(dve.tensor_copy(n4t[par][:], ps[par][0][:]), last)
                    for l in range(3):
                        cur = (l + 1) % 2
                        for par in two:
                            pe_at[par].wait(dve, turn, f"xt{l}")
                            dve_at[par].done(dve.tensor_copy(xt[par][:], ps[par][1][:]), f"xt{l}")
                        for par in two:
                            pe_at[par].wait(dve, turn, f"y{l}")
                            dve_at[par].done(dve.tensor_tensor(X[par][1 - cur][:], X[par][cur][:], ps[par][2][:], ALU.subtract), f"y{l}")


def delta_chunks(nc, A):
    G = B // SUB
    Q = 2 * G
    TURNS = T // P // 2
    with ExitStack() as ctx:
        m = Memory(nc, ctx, "dc")
        W = [P, SUB, P]
        dec, wo, bo = m.sb("dec", [P, NP, NDEC]), m.sb("wo", [P, D]), m.sb("bo", [P, D])
        names = ("kd", "vd", "kt", "qt", "qgt", "inv", "dm", "gate")
        buf = {n: [m.sb(f"{n}{q}", W) for q in range(Q)] for n in names}
        state, stateT = ([m.sb(f"{n}{g}", W) for g in range(G)] for n in ("state", "stateT"))
        col = [m.sb(f"col{k}", [P, SUB, NDEC]) for k in range(Q)]
        r, wd, wt, am, og = (m.sb(n, W) for n in ("r", "wd", "wt", "am", "og"))
        out = [m.sb(f"out{k}", [P, SUB, D]) for k in range(2)]
        psK, psW, psWT, psA, psS, psO = (m.ps(n, W) for n in ("psK", "psW", "psWT", "psA", "psS", "psO"))
        psOut = m.ps("psOut", [P, SUB, D])
        weights, zeroed = m.sem("weights"), m.sem("zeroed")
        out_st = [m.sem(f"out_st{q}") for q in range(Q)]
        loaded = [m.sem(f"loaded{q}") for q in range(Q)]
        dve_own, act_own = m.sem("dve_own"), m.sem("act_own")
        pe_at = [Stages(m.sem(f"pe_at{q}"), "ks", "w", "wt", "old", "a", "s", "st", "o", "out") for q in range(Q)]
        dve_at = [Stages(m.sem(f"dve_at{q}"), "col", "r", "wt", "am", "st", "s", "og", "out") for q in range(Q)]
        act_at = [Stages(m.sem(f"act_at{q}"), "wd") for q in range(Q)]

        def before(at, eng, turn, q, name, steps=1):
            if q >= steps:
                at[q - steps].wait(eng, turn, name)
            elif not isinstance(turn, int) or turn:
                at[q - steps + Q].wait(eng, turn - 1, name)

        def steps(eng, step, finish):
            for q in range(Q):
                step(0, q, (lambda q=q: finish(0, q - 1)) if q else lambda: None)
            with eng.Fori(1, TURNS) as turn:
                for q in range(Q):
                    step(turn, q, lambda: finish(turn, q - 1) if q else finish(turn - 1, Q - 1))
            finish(TURNS - 1, Q - 1)

        def place(name, c, g):
            if name == "gate":
                return A["gate_t"].rearrange("f (b c t) -> c f b t", b=B, t=P)[c, :, g * SUB:(g + 1) * SUB, :]
            if name in ("kd", "vd", "s1"):
                return A[name].rearrange("(b c p) d -> c p b d", b=B, p=P)[c, :, g * SUB:(g + 1) * SUB, :]
            return A[name].rearrange("(b c) p d -> c p b d", b=B)[c, :, g * SUB:(g + 1) * SUB, :]

        with nc.Block() as block:
            @block.sync
            def _(sp):
                sp.dma_start(dec[:], A["dec"]).then_inc(weights, 16)
                sp.dma_start(wo[:], A["w_o"]).then_inc(weights, 16)
                sp.dma_start(bo[:], spread(A["b_o"], D)).then_inc(weights, 16)
                with sp.Fori(0, TURNS) as turn:
                    for q in range(Q):
                        dve_at[q].wait_before(sp, turn)
                        m.settle(sp)
                        pe_at[q].wait_before(sp, turn)
                        m.settle(sp)
                        for n in names:
                            sp.dma_start(buf[n][q][:], place(n, turn * 2 + q // G, q % G)).then_inc(loaded[q], 16)
                for q in range(Q):
                    sp.wait_ge(out_st[q], 16 * TURNS)
                    m.settle(sp)

            @block.gpsimd
            def _(pool):
                for t_ in state + stateT:
                    pool.memset(t_[:], 0.0).then_inc(zeroed, 1)
                with pool.Fori(0, TURNS) as turn:
                    for q in range(Q):
                        dve_at[q].wait(pool, turn, "out")
                        m.settle(pool)
                        pool.dma_start(place("s1", turn * 2 + q // G, q % G), out[q % 2][:]).then_inc(out_st[q], 16)

            @block.scalar
            def _(act):
                def step(turn, q, _):
                    pe_at[q].wait(act, turn, "w")
                    dve_at[q].wait(act, turn, "col")
                    before(pe_at, act, turn, q, "st")
                    for s in range(SUB):
                        ins = act.activation(wd[:, s, :], psW[:, s, :], ACT.Copy, scale=col[q][:, s, TO_END_BETA:TO_END_BETA + 1])
                        if s < SUB - 1:
                            ins.then_inc(act_own, 1)
                    act.wait_ge(act_own, (turn * Q + (q + 1)) * (SUB - 1))
                    act_at[q].done(ins, "wd")

                steps(act, step, lambda turn, q: None)

            @block.tensor
            def _(pe):
                pe.wait_ge(weights, 48)
                pe.wait_ge(zeroed, 2 * G)

                def each(dst, left, right, **flags):
                    flags = flags or dict(start=True, stop=True)
                    for s in range(SUB):
                        last = pe.matmul(dst[:, s, :], left[:, s, :], right[:, s, :], **flags)
                    return last

                def finish(turn, q):
                    dve_at[q].wait(pe, turn, "og")
                    before(dve_at, pe, turn, q, "out")
                    for s in range(SUB):
                        last = pe.matmul(psOut[:, s, :], og[:, s, :], wo[:], start=True, stop=True)
                    pe_at[q].done(last, "out")

                def step(turn, q, finish_last):
                    g = q % G
                    pe.wait_ge(loaded[q], turn * 128 + 128)
                    before(dve_at, pe, turn, q, "st", G)
                    before(dve_at, pe, turn, q, "st")
                    pe_at[q].done(each(psK, buf["kt"][q], stateT[g]), "ks")
                    finish_last()
                    dve_at[q].wait(pe, turn, "r")
                    before(act_at, pe, turn, q, "wd")
                    pe_at[q].done(each(psW, buf["inv"][q], r), "w")
                    pe_at[q].done(each(psWT, r, buf["inv"][q]), "wt")
                    before(dve_at, pe, turn, q, "s", G)
                    for s in range(SUB):
                        last = pe.matmul(psO[:, s, :], state[g][:, s, :], buf["qgt"][q][:, s, :], start=(s == 0), stop=False)
                    pe_at[q].done(last, "old")
                    dve_at[q].wait(pe, turn, "wt")
                    pe_at[q].done(each(psA, wt, buf["qt"][q]), "a")
                    act_at[q].wait(pe, turn, "wd")
                    before(dve_at, pe, turn, q, "s")
                    pe_at[q].done(each(psS, wd, buf["kd"][q]), "s")
                    pe_at[q].done(each(psK, buf["kd"][q], wd), "st")
                    dve_at[q].wait(pe, turn, "am")
                    for s in range(SUB):
                        last = pe.matmul(psO[:, s, :], buf["kd"][q][:, s, :], am[:, s, :], start=False, stop=(s == SUB - 1))
                    pe_at[q].done(last, "o")

                steps(pe, step, finish)

            @block.vector
            def _(dve):
                dve.wait_ge(weights, 48)
                dve.wait_ge(zeroed, 2 * G)
                def finish(turn, q):
                    pe_at[q].wait(dve, turn, "out")
                    if q >= 2:
                        dve.wait_ge(out_st[q - 2], turn * 16 + 16)
                    elif not isinstance(turn, int) or turn:
                        dve.wait_ge(out_st[q + 2], turn * 16)
                    dve_at[q].done(dve.tensor_tensor(out[q % 2][:], psOut[:], over_chunks(bo[:]), ALU.add), "out")

                def step(turn, q, finish_last):
                    g = q % G
                    count = [0]

                    def parts(op, name):
                        for s in range(SUB):
                            ins = op(s)
                            if s < SUB - 1:
                                ins.then_inc(dve_own, 1)
                                count[0] += 1
                        dve.wait_ge(dve_own, turn * (Q * 4 * (SUB - 1)) + (q * 4 * (SUB - 1) + count[0]))
                        dve_at[q].done(ins, name)

                    def scaled(dst, src, col_at, plus, op1=ALU.add):
                        return lambda s: dve.scalar_tensor_tensor(
                            out=dst[:, s, :], in0=src[:, s, :], scalar=col[q][:, s, col_at:col_at + 1],
                            in1=plus[:, s, :], op0=ALU.mult, op1=op1)

                    view = dec[:].rearrange("p (b c) f -> p b c f", b=B)
                    c = turn * 2 + q // G
                    if not isinstance(turn, int) or turn:
                        act_at[q].wait_before(dve, turn)
                    dve_at[q].done(dve.tensor_copy(col[q][:].rearrange("p b (a f) -> p b a f", a=1),
                                                   view[:, g * SUB:(g + 1) * SUB, bass.ds(c, 1), :]), "col")
                    dve.wait_ge(loaded[q], turn * 128 + 128)
                    pe_at[q].wait(dve, turn, "ks")
                    dve_at[q].wait(dve, turn, "col")
                    before(pe_at, dve, turn, q, "wt")
                    parts(scaled(r, psK, NEG_EXP_G, buf["vd"][q]), "r")
                    pe_at[q].wait(dve, turn, "wt")
                    before(pe_at, dve, turn, q, "a")
                    dve_at[q].done(dve.tensor_copy(wt[:], psWT[:]), "wt")
                    pe_at[q].wait(dve, turn, "a")
                    before(pe_at, dve, turn, q, "o")
                    parts(scaled(am, psA, BETA, buf["dm"][q], ALU.mult), "am")
                    pe_at[q].wait(dve, turn, "st")
                    before(dve_at, dve, turn, q, "st", G)
                    parts(scaled(stateT[g], stateT[g], EXP_END, psK), "st")
                    finish_last()
                    pe_at[q].wait(dve, turn, "old")
                    before(dve_at, dve, turn, q, "s", G)
                    parts(scaled(state[g], state[g], EXP_END, psS), "s")
                    pe_at[q].wait(dve, turn, "o")
                    before(pe_at, dve, turn, q, "out")
                    dve_at[q].done(dve.tensor_tensor(og[:], psO[:], buf["gate"][q][:], ALU.mult), "og")

                steps(dve, step, finish)


def attention(nc, A):
    QUAD = 4
    ROWS = 9 * HD
    MAXROW = 96
    ALL = MAXROW + 3
    NQ = NH // QUAD
    KC = T // P
    NHALF = T // TILE
    with ExitStack() as ctx:
        m = Memory(nc, ctx, "at")
        q4, k4 = ([m.sb(f"{n}{j}", [ALL, QUAD, T], BF16) for j in range(NQ)] for n in ("q4", "k4"))
        vraw = [m.sb(f"vraw{j}", [P, KC, QUAD * HD]) for j in range(NQ)]
        v4 = [m.sb(f"v4{j}", [P, KC, QUAD, 32]) for j in range(NQ)]
        ident = m.sb("ident", [P, P], BF16)
        half_max = m.sb("half_max", [P, QUAD, KC, NHALF])
        top = m.sb("top", [P, QUAD * KC])
        rest = m.sb("rest", [P, 2, QUAD * KC])
        top3 = m.sb("top3", [P, 4, QUAD * KC], BF16)
        topT = m.sb("topT", [P, P], BF16)
        probs = [m.sb(f"probs{j}", [P, 2, TILE]) for j in range(2 * QUAD)]
        sums = [m.sb(f"sums{j}", [P, TILE]) for j in range(NHALF)]
        psM = [m.ps(f"psM{j}", [P, TILE]) for j in range(2)]
        psS = [m.ps(f"psS{j}", [P, 2, TILE]) for j in range(2)]
        psT, psV = m.ps("psT", [P, P]), m.ps("psV", [P, TILE])
        ident_made, first_made, ready_made = m.sem("ident_made"), m.sem("first_made"), m.sem("ready_made")
        loaded = [m.sem(f"loaded{j}") for j in range(NQ)]
        top_in = [m.sem(f"top_in{j}") for j in range(NQ)]
        v_ready, scored, maxed = m.sem("v_ready"), m.sem("scored"), m.sem("maxed")
        top_at = Stages(m.sem("top_at"), "top", "part0", "rest0", "part1", "rest1", "part2")
        filled, turned, topT_ready = m.sem("filled"), m.sem("turned"), m.sem("topT_ready")
        keyed, probs_ready, summed, sums_ready = m.sem("keyed"), m.sem("probs_ready"), m.sem("summed"), m.sem("sums_ready")
        sums_st = [m.sem(f"sums_st{j}") for j in range(NHALF)]
        LOADS = 3 + 5 + 1
        TILES1 = QUAD * KC * NHALF
        TILES2 = NHALF * (KC // 2) * QUAD
        GROUPS = TILES2 // QUAD
        UNITS = B * NQ

        def constant_rows(j):
            return (q4[j][64:96, :, :], 0.0), (k4[j][64:96, :, :], 0.0), (k4[j][MAXROW:ALL, :, :], 1.0)

        with nc.Block() as block:
            @block.sync
            def _(sp):
                def load(b, j):
                    for turned_by in range(3):
                        for name, buf, parts in (("qs", q4, (0, 3)), ("ks", k4, (turned_by, 3)), ("ks", k4, (0, turned_by))):
                            if parts[0] < parts[1]:
                                src = A[name][b, j, parts[0]:parts[1], :, :].rearrange("k (r h) t -> (k r) (h t)", h=QUAD)
                                first = turned_by * 3 + (0 if parts[1] == 3 else 3 - turned_by)
                                dst = buf[j][first * HD:(first + parts[1] - parts[0]) * HD, :, :]
                                sp.dma_start(dst.rearrange("n h t -> n (h t)"), src).then_inc(loaded[j], 16)
                    src = A["vf"].rearrange("(b c p) n -> b p c n", b=B, p=P)[b, :, :, j * QUAD * HD:(j + 1) * QUAD * HD]
                    sp.dma_start(vraw[j][:], src).then_inc(loaded[j], 16)

                for j in range(NQ):
                    if j:
                        sp.wait_ge(ready_made, 3 * j)
                    else:
                        sp.wait_ge(first_made, 3)
                    m.settle(sp)
                    load(0, j)

                def sequence(b, final):
                    for j in range(NQ):
                        u = b * NQ + j
                        for half in range(NHALF):
                            sp.wait_ge(sums_ready, u * NHALF + half + 1)
                            m.settle(sp)
                            for h in range(QUAD):
                                dst = A["ao"].rearrange("h q (b s t) -> b h s q t", b=B, t=TILE)[b, j * QUAD + h, half, :, :]
                                sp.dma_start(dst, sums[half][32 * h:32 * h + 2 * HD, :]).then_inc(sums_st[half], 16)
                        if not final:
                            load(b + 1, j)

                with sp.Fori(0, B - 1) as b:
                    sequence(b, False)
                sequence(B - 1, True)
                for half in range(NHALF):
                    sp.wait_ge(sums_st[half], UNITS * QUAD * 16)
                    m.settle(sp)

            @block.gpsimd
            def _(pool):
                pool.memset(ident[:], 0.0).then_inc(ident_made, 1)
                pool.wait_ge(ident_made, 1)
                pool.affine_select(out=ident[:], in_=ident[:], compare_op=ALU.not_equal, fill=1.0, base=0,
                                   pattern=[[-1, P]], channel_multiplier=1).then_inc(ident_made, 1)
                pool.wait_ge(ident_made, 2)
                for j in range(1, NQ):
                    for n, (rows, value) in enumerate(constant_rows(j)):
                        pool.memset(rows, value).then_inc(ready_made, 1)
                        pool.wait_ge(ready_made, 3 * (j - 1) + n + 1)
                for j in range(NQ):
                    pool.memset(v4[j][:], 0.0).then_inc(v_ready, 1)
                    pool.wait_ge(v_ready, 2 * j + 1)
                    pool.memset(v4[j][:, :, :, HD:2 * HD], 1.0).then_inc(v_ready, 1)
                    pool.wait_ge(v_ready, 2 * j + 2)
                with pool.Fori(0, B) as b:
                    for j in range(NQ):
                        pool.wait_ge(loaded[j], (b + 1) * 16 * LOADS)
                        pool.wait_ge(summed, (b * NQ + j) * GROUPS if j == 0 else (b * NQ + j) * GROUPS - GROUPS)
                        m.settle(pool)
                        pool.tensor_copy(v4[j][:, :, :, 0:HD], vraw[j][:].rearrange("p c (h r) -> p c h r", r=HD)).then_inc(v_ready, 1)

            LEAD = 12
            PER_STEP = TILES1 // TILES2
            PACE = ((0, 1, 0), (1, 1, 0), (0, 1, 1), (1, 1, 1))
            TURN = (TILES1 - LEAD) // PER_STEP + 1

            def ahead(u, final, j, n):
                first = LEAD + PER_STEP * (n - n % QUAD) + sum(map(sum, PACE[:n % QUAD]))
                for k in range(first, first + sum(PACE[n % QUAD])):
                    d = 1 + k // TILES1
                    if not final or j + d < NQ:
                        yield u + d, (j + d) % NQ, k % TILES1

            @block.tensor
            def _(pe):
                pe.wait_ge(ident_made, 2)

                def maxima(u, j, t):
                    h, c, half = t // (KC * NHALF), t // NHALF % KC, t % NHALF
                    if t > 1:
                        pe.wait_ge(maxed, u * TILES1 + (t - 1))
                    elif not isinstance(u, int) or u:
                        pe.wait_ge(maxed, u * TILES1 + t - 1)
                    pe.matmul(psM[t % 2][:], q4[j][0:ROWS, h, c * P:(c + 1) * P],
                              k4[j][0:ROWS, h, half * TILE:(half + 1) * TILE], start=True, stop=True).then_inc(scored, 1)

                def turn(u):
                    top_at.wait(pe, u, "part2")
                    pe.wait_ge(topT_ready, u)
                    pe.matmul(psT[:], top3[:].rearrange("p k n -> p (k n)"), ident[:],
                              start=True, stop=True).then_inc(turned, 1)

                def second(u, j, g, h, between=()):
                    half, pair, n = g // (KC // 2), g % (KC // 2), g * QUAD + h
                    if n > 1:
                        pe.wait_ge(probs_ready, u * TILES2 + (n - 1))
                    elif not isinstance(u, int) or u:
                        pe.wait_ge(probs_ready, u * TILES2 + n - 1)
                    for k in range(2):
                        c = pair * 2 + k
                        last = pe.matmul(psS[h % 2][:, k, :], k4[j][:, h, c * P:(c + 1) * P],
                                         q4[j][:, h, half * TILE:(half + 1) * TILE], start=True, stop=True)
                        if k:
                            last.then_inc(keyed, 1)
                        before = sum(PACE[h][:k])
                        for tile in between[before:before + PACE[h][k]]:
                            maxima(*tile)

                def values(u, j, g, k):
                    half, pair = g // (KC // 2), g % (KC // 2)
                    c = pair * 2 + k
                    pe.wait_ge(probs_ready, u * TILES2 + (g + 1) * QUAD)
                    if c == 0:
                        pe.wait_ge(sums_ready, u * NHALF + half)
                        pe.wait_ge(v_ready, 2 * NQ + u + 1)
                    for h in range(QUAD):
                        last = pe.matmul(psV[32 * h:32 * h + 32, :], v4[j][:, c, h, :], probs[(g % 2) * QUAD + h][:, k, :],
                                         start=(c == 0), stop=(c == KC - 1))
                    if k == 1:
                        last.then_inc(summed, 1)

                pe.wait_ge(loaded[0], 16 * LOADS)
                pe.wait_ge(loaded[1], 16 * LOADS)
                for t in range(TILES1):
                    maxima(0, 0, t)
                for t in range(LEAD):
                    maxima(1, 1, t)
                turn(0)
                pe.wait_ge(top_in[0], 16)
                for h in range(QUAD):
                    between = tuple(ahead(0, False, 0, h))
                    second(0, 0, 0, h, between)
                    for tile in between[sum(PACE[h][:2]):]:
                        maxima(*tile)

                def sequence(b, final):
                    for j in range(NQ):
                        u = b * NQ + j
                        more = not (final and j == NQ - 1)
                        nj, nb = (j + 1) % NQ, b + (j + 1) // NQ
                        for g in range(1, GROUPS + 1):
                            for h in range(QUAD):
                                n = g * QUAD + h
                                between = tuple(ahead(u, final, j, n))
                                for _, aj, t in between:
                                    if t == 0:
                                        pe.wait_ge(loaded[aj], (b + (j + 2) // NQ + 1) * 16 * LOADS)
                                if g < GROUPS:
                                    second(u, j, g, h, between)
                                elif more:
                                    if h == 0:
                                        pe.wait_ge(top_in[nj], nb * 16 + 16)
                                    second(u + 1, nj, 0, h, between)
                                if n == TURN and more:
                                    turn(u + 1)
                                if h >= 2:
                                    values(u, j, g - 1, h - 2)
                                for tile in between[sum(PACE[h][:2]):]:
                                    maxima(*tile)

                with pe.Fori(0, B - 1) as b:
                    sequence(b, False)
                sequence(B - 1, True)

            @block.scalar
            def _(act):
                def turn(u, j, b):
                    act.wait_ge(turned, u + 1)
                    if j:
                        act.wait_ge(top_in[j - 1], b * 16 + 16)
                    elif not isinstance(b, int) or b:
                        act.wait_ge(top_in[NQ - 1], b * 16)
                    act.activation(topT[:], psT[:], ACT.Copy).then_inc(topT_ready, 1)
                    act.wait_ge(topT_ready, u + 1)
                    dst = q4[j][MAXROW:ALL, :, :].rearrange("k h (c s) -> k (h c) s", s=P)
                    act.dma_start(dst, topT[0:3 * QUAD * KC, :]).then_inc(top_in[j], 16)

                def collect(u, half):
                    act.wait_ge(summed, u * GROUPS + (half + 1) * GROUPS // NHALF)
                    act.wait_ge(sums_st[half], u * QUAD * 16)
                    act.activation(sums[half][:], psV[:], ACT.Copy).then_inc(sums_ready, 1)

                def exponentials(u, g, h):
                    act.wait_ge(keyed, u * TILES2 + (g * QUAD + h + 1))
                    act.activation(probs[(g % 2) * QUAD + h][:], psS[h % 2][:], ACT.Exp).then_inc(probs_ready, 1)

                def sequence(b, final):
                    for j in range(NQ):
                        u = b * NQ + j
                        more = not (final and j == NQ - 1)
                        for g in range(1, GROUPS + more):
                            act.wait_ge(summed, u * GROUPS + (g - 1))
                            for h in range(QUAD):
                                exponentials(u, g, h)
                                if g * QUAD + h == TURN + 1 and more:
                                    turn(u + 1, (j + 1) % NQ, b + (j + 1) // NQ)
                            if g == GROUPS // NHALF:
                                collect(u, 0)
                        collect(u, 1)

                turn(0, 0, 0)
                for h in range(QUAD):
                    exponentials(0, 0, h)
                with act.Fori(0, B - 1) as b:
                    sequence(b, False)
                sequence(B - 1, True)

            @block.vector
            def _(dve):
                def maxima(u, t):
                    h, c, half = t // (KC * NHALF), t // NHALF % KC, t % NHALF
                    dve.wait_ge(scored, u * TILES1 + t + 1)
                    dve.reduce_max(half_max[:, h, c, half:half + 1], psM[t % 2][:], AX.X).then_inc(maxed, 1)

                def minus_max(u):
                    dve.wait_ge(maxed, u * TILES1 + TILES1)
                    dve.wait_ge(turned, u)
                    top_at.done(dve.tensor_reduce(top[:], half_max[:].rearrange("p h c n -> p (h c) n"), AX.X, ALU.max, negate=True), "top")
                    top_at.wait(dve, u, "top")
                    top_at.done(dve.tensor_copy(top3[:, 0, :], top[:]), "part0")
                    top_at.wait(dve, u, "part0")
                    top_at.done(dve.tensor_tensor(rest[:, 0, :], top[:], top3[:, 0, :], ALU.subtract), "rest0")
                    top_at.wait(dve, u, "rest0")
                    top_at.done(dve.tensor_copy(top3[:, 1, :], rest[:, 0, :]), "part1")
                    top_at.wait(dve, u, "part1")
                    top_at.done(dve.tensor_tensor(rest[:, 1, :], rest[:, 0, :], top3[:, 1, :], ALU.subtract), "rest1")
                    top_at.wait(dve, u, "rest1")
                    top_at.done(dve.tensor_copy(top3[:, 2, :], rest[:, 1, :]), "part2")
                    top_at.wait(dve, u, "part2")

                for n, (rows, value) in enumerate(constant_rows(0)):
                    dve.memset(rows, value).then_inc(first_made, 1)
                    dve.wait_ge(first_made, n + 1)
                dve.memset(top3[:, 3, :], 0.0).then_inc(filled, 1)
                dve.wait_ge(filled, 1)
                for t in range(TILES1):
                    maxima(0, t)
                minus_max(0)
                for t in range(LEAD):
                    maxima(1, t)
                for h in range(QUAD):
                    for ahead_u, _, t in ahead(0, False, 0, h):
                        maxima(ahead_u, t)

                def sequence(b, final):
                    for j in range(NQ):
                        u = b * NQ + j
                        for g in range(1, GROUPS + 1):
                            for h in range(QUAD):
                                for ahead_u, _, t in ahead(u, final, j, g * QUAD + h):
                                    maxima(ahead_u, t)
                                    if t == TILES1 - 1:
                                        minus_max(ahead_u)

                with dve.Fori(0, B - 1) as b:
                    sequence(b, False)
                sequence(B - 1, True)


def experts(nc, A):
    TILE, SUB = 256, 2
    NT = N // TILE
    FT = FF // P
    STAGED = max(H * FF, FT * D)
    with ExitStack() as ctx:
        m = Memory(nc, ctx, "ex")
        two = range(2)
        wo, ob, wr, br = m.sb("wo", [P, D]), m.sb("ob", [P, H]), m.sb("wr", [P, H, E]), m.sb("br", [P, E])
        b1, b2 = m.sb("b1", [P, E, FT]), m.sb("b2", [E, D])
        w1 = [m.sb(f"w1{k}", [P, E, H, FF], F32R) for k in two]
        w2 = [m.sb(f"w2{k}", [P, E, FT, D], F32R) for k in two]
        ident, number = m.sb("ident", [P, P]), m.sb("number", [P, E])
        ao = [m.sb(f"ao{k}", [P, 2, TILE]) for k in two]
        x1, xn, s1 = ([m.sb(f"{n}{k}", [P, SUB, D]) for k in two] for n in ("x1", "xn", "s1"))
        rs, aon = m.sb("rs", [P, TILE]), m.sb("aon", [P, TILE])
        mla = m.sb("mla", [P, H, TILE])
        mla2 = [[m.sb(f"mla2{k}{part}", [P, H, TILE], F32R) for part in two] for k in two]
        R = [P, SUB, E]
        lg, ex, pr, top, pick0, pick1 = (m.sb(n, R) for n in ("lg", "ex", "pr", "top", "pick0", "pick1"))
        index, indexf = m.sb("index", R, U32), m.sb("indexf", R)
        comb = [m.sb(f"comb{k}", R) for k in two]
        mx, total, share = m.sb("mx", [P, SUB]), m.sb("total", [P, SUB]), m.sb("share", [P, SUB, 2])
        combT = m.sb("combT", [E, SUB, P])
        hid = [m.sb(f"hid{k}", [P, FT, TILE]) for k in two]
        stage = [m.sb(f"stage{k}", [P, STAGED]) for k in two]
        hid2 = [[m.sb(f"hid2{k}{part}", [P, FT, TILE], F32R) for part in two] for k in two]
        acc = [m.sb(f"acc{k}", [P, SUB, D]) for k in two]
        gin, th, res = (m.sb(n, [P, SUB, D]) for n in ("gin", "th", "res"))
        psH = [m.ps(f"psH{k}", [P, 2, TILE]) for k in range(FT)]
        psE = [m.ps(f"psE{k}", [P, SUB, D]) for k in two]
        psM, psB = m.ps("psM", [P, H, TILE]), m.ps("psB", [P, SUB, D])
        weights, consts, split = m.sem("weights"), m.sem("consts"), m.sem("split")
        staged = [m.sem(f"staged{k}") for k in two]
        ao_loaded = [m.sem(f"ao_loaded{k}") for k in two]
        end_loaded = [m.sem(f"end_loaded{k}") for k in two]
        out_st, half1 = m.sem("out_st"), m.sem("half1")
        pe_pre = Stages(m.sem("pe_pre"), "mla", "logits", "combT", "bias")
        act_pre = Stages(m.sem("act_pre"), "mla", "ex")
        dve_pre = Stages(m.sem("dve_pre"), "rs", "aon", "head", "rest", "lg", "mx", "sub", "total", "rtotal", "pr", "top",
                         "index", "indexf", "sum2", "rsum2", "share", "pick0", "pick1", "comb", "combT", "bias")
        hid_psum, hid_ready, out_psum, added = m.sem("hid_psum"), m.sem("hid_ready"), m.sem("out_psum"), m.sem("added")
        head_ready, rest_ready = m.sem("head_ready"), m.sem("rest_ready")
        gin_ready, th_ready, res_ready, act_own, dve_own, pre_own = (
            m.sem(n) for n in ("gin", "th", "res", "act_own", "dve_own", "pre_own"))
        NSTAGED = 2 * E

        def rows(ap, i):
            return ap.rearrange("(i s p) d -> i p s d", p=P, s=SUB)[i, :, :, :]

        def flat(ap):
            return ap.rearrange("p a b -> p (a b)")

        def products(pe, out, parts, start, stop):
            for n, (a, b) in enumerate(parts):
                last = pe.matmul(out, a, b, start=start and n == 0, stop=stop and n == len(parts) - 1)
            return last

        def run(eng, step):
            step(0, 0, True, True)
            with eng.Fori(0, NT // 2 - 1) as turn:
                step(turn * 2 + 1, 1, False, True)
                step(turn * 2 + 2, 0, False, True)
            step(NT - 1, 1, False, False)

        with nc.Block() as block:
            @block.sync
            def _(sp):
                with nc.allow_non_contiguous_dma(reason="small"):
                    for dst, src in ((wo[:], A["fo"][0:P, :]), (ob[:], column(A["fob"])), (wr[:], halves(A["rw"])),
                                     (br[:], spread(A["rb"], E)), (b2[:], A["b2"]),
                                     (b1[:], A["b1"].rearrange("e (f p) -> p e f", p=P))):
                        sp.dma_start(dst, src).then_inc(weights, 16)

                def load_ao(i, par):
                    src = A["ao"].rearrange("h (k r) (i t) -> i k h r t", k=2, t=TILE)
                    for k in two:
                        sp.dma_start(ao[par][:, k, :], src[i, k, :, :, :]).then_inc(ao_loaded[par], 16)

                def load_end(i, par):
                    for name, buf in (("xn1", xn), ("x1", x1), ("s1", s1)):
                        sp.dma_start(buf[par][:], rows(A[name], i)).then_inc(end_loaded[par], 16)

                for i in two:
                    load_ao(i, i)
                w1_in = A["w1"].rearrange("e (h p) f -> e p h f", p=P)
                w2_in = A["w2"].rearrange("e (f p) d -> e p f d", p=P)
                for n in range(NSTAGED):
                    if n >= 2:
                        sp.wait_ge(split, 2 * n - 2)
                    src = w1_in[n // 2, :, :, :] if n % 2 == 0 else w2_in[n // 2, :, :, :]
                    dst = stage[n % 2][:].rearrange("p (a b) -> p a b", a=src.shape[1])
                    sp.dma_start(dst, src).then_inc(staged[n % 2], 16)
                for i in two:
                    load_end(i, i)

                with sp.Fori(0, NT // 2 - 1) as turn:
                    for par in two:
                        i = turn * 2 + par
                        dve_pre.wait(sp, i, "aon")
                        m.settle(sp)
                        load_ao(i + 2, par)
                        sp.wait_ge(res_ready, i + 1)
                        m.settle(sp)
                        load_end(i + 2, par)
                sp.wait_ge(out_st, 16 * NT)

            @block.gpsimd
            def _(pool):
                identity(nc, pool, ident, consts)
                pool.wait_ge(consts, 2)
                pool.iota(number[:], pattern=[[1, E]], base=0, channel_multiplier=0,
                          allow_small_or_imprecise_dtypes=True).then_inc(consts, 1)
                with pool.Fori(0, NT) as i:
                    pool.wait_ge(res_ready, i + 1)
                    m.settle(pool)
                    pool.dma_start(rows(A["out"], i), res[:]).then_inc(out_st, 16)

            @block.scalar
            def _(act):
                def prepare(i, slot):
                    if slot == 2:
                        pe_pre.wait(act, i, "mla")
                        if isinstance(i, int) and i == 0:
                            pass
                        else:
                            dve_pre.wait(act, i - 1, "rest")
                            pe_pre.wait(act, i - 1, "logits")
                        act.activation(mla[:, 0, :], psM[:, 0, :], ACT.Identity, bias=ob[:, 0:1]).then_inc(act_own, 1)
                        act_pre.done(act.activation(mla[:, 1, :], psM[:, 1, :], ACT.Identity, bias=ob[:, 1:2]), "mla")
                        act.wait_ge(act_own, i + 1)
                    if slot == 4:
                        dve_pre.wait(act, i, "sub")
                        act_pre.done(act.activation(ex[:], lg[:], ACT.Exp), "ex")

                def gelu(i, e):
                    if e >= 2:
                        act.wait_ge(rest_ready, i * E + (e - 1))
                    elif not (isinstance(i, int) and i == 0):
                        act.wait_ge(rest_ready, i * E + e - 1)
                    for f in range(FT):
                        act.wait_ge(hid_psum, (i * E + e) * FT + f + 1)
                        act.activation(hid[e % 2][:, f, :], psH[f][:, 0, :], ACT.Gelu,
                                       bias=b1[:, e, f:f + 1]).then_inc(hid_ready, 1)

                def finish(i):
                    act.wait_ge(gin_ready, i + 1)
                    act.activation(th[:], gin[:], ACT.Tanh, scale=0.5).then_inc(th_ready, 1)

                def step(i, par, first, more):
                    for e in range(E):
                        if e + 1 < E:
                            gelu(i, e + 1)
                        elif more:
                            gelu(i + 1, 0)
                        if e == 2 and not first:
                            finish(i - 1)
                        if more:
                            prepare(i + 1, e)

                act.wait_ge(weights, 96)
                for slot in range(E):
                    prepare(0, slot)
                gelu(0, 0)
                run(act, step)
                finish(NT - 1)

            @block.tensor
            def _(pe):
                def prepare(i, par, slot):
                    if slot == 1:
                        dve_pre.wait(pe, i, "aon")
                        for h in range(H):
                            last = pe.matmul(psM[:, h, :], wo[:, h * P:(h + 1) * P], aon[:], start=True, stop=True)
                        pe_pre.done(last, "mla")
                    if slot == 3:
                        act_pre.wait(pe, i, "mla")
                        for s in range(SUB):
                            for h in range(H):
                                last = pe.matmul(psB[:, s, 0:E], mla[:, h, s * P:(s + 1) * P], wr[:, h, :],
                                                 start=(h == 0), stop=(h == H - 1))
                        pe_pre.done(last, "logits")
                    if slot == 6:
                        dve_pre.wait(pe, i, "comb")
                        for s in range(SUB):
                            last = pe.transpose(psM[0:E, 0, s * P:(s + 1) * P], comb[par][:, s, :], ident[:])
                        pe_pre.done(last, "combT")
                    if slot == 7:
                        dve_pre.wait(pe, i, "combT")
                        for s in range(SUB):
                            last = pe.matmul(psB[:, s, :], combT[:, s, :], b2[:], start=True, stop=True)
                        pe_pre.done(last, "bias")

                def hidden(i, par, e):
                    if e == 0:
                        dve_pre.wait(pe, i, "rest")
                    if isinstance(i, int) and i == 0:
                        pe.wait_ge(split, 4 * e + 2)
                    for f in range(FT):
                        if e:
                            pe.wait_ge(hid_ready, i * E * FT + ((e - 1) * FT + f + 1))
                        elif not (isinstance(i, int) and i == 0):
                            pe.wait_ge(hid_ready, i * E * FT + (f + 1) - FT)
                        fs = slice(f * P, (f + 1) * P)
                        for h in range(H):
                            xh, xl = (mla2[par][k][:, h, :] for k in two)
                            wh, wl = (w1[k][:, e, h, fs] for k in two)
                            last = products(pe, psH[f][:, 0, :], ((wh, xh), (wh, xl), (wl, xh)), h == 0, h == H - 1)
                        last.then_inc(hid_psum, 1)

                def output(i, e):
                    pe.wait_ge(rest_ready, i * E + (e + 1))
                    if isinstance(i, int) and i == 0:
                        pe.wait_ge(split, 4 * e + 4)
                    if e >= 2:
                        pe.wait_ge(added, i * E + (e - 1))
                    elif not (isinstance(i, int) and i == 0):
                        pe.wait_ge(added, i * E + e - 1)
                    for s in range(SUB):
                        ss = slice(s * P, (s + 1) * P)
                        for f in range(FT):
                            xh, xl = (hid2[e % 2][k][:, f, ss] for k in two)
                            wh, wl = (w2[k][:, e, f, :] for k in two)
                            last = products(pe, psE[e % 2][:, s, :], ((xh, wh), (xh, wl), (xl, wh)), f == 0, f == FT - 1)
                    last.then_inc(out_psum, 1)

                def step(i, par, first, more):
                    for e in range(E):
                        if e + 1 < E:
                            hidden(i, par, e + 1)
                        elif more:
                            hidden(i + 1, 1 - par, 0)
                        if more:
                            prepare(i + 1, 1 - par, e)
                        output(i, e)

                pe.wait_ge(weights, 96)
                pe.wait_ge(consts, 3)
                for slot in range(E):
                    prepare(0, 0, slot)
                hidden(0, 0, 0)
                run(pe, step)

            @block.vector
            def _(dve):
                def divide(head, rest, whole, head_sem, rest_sem, wait):
                    head_sem(dve.tensor_copy(head, whole))
                    wait()
                    rest_sem(dve.tensor_tensor(rest, whole, head.bitcast(F32), ALU.subtract))

                def prepare(i, par, slot):
                    own = Chain(pre_own, 2 * (SUB - 1) + 4)
                    if slot == 0:
                        dve.wait_ge(ao_loaded[par], (i - par) * 16 + 32)
                        dve_pre.done(dve.reciprocal(rs[:], ao[par][:, 1, :]), "rs")
                        dve_pre.wait(dve, i, "rs")
                        dve_pre.done(dve.tensor_tensor(aon[:], ao[par][:, 0, :], rs[:], ALU.mult), "aon")
                    if slot == 2:
                        act_pre.wait(dve, i, "mla")
                        head, rest = (flat(mla2[par][k][:]) for k in two)
                        divide(head, rest, flat(mla[:]), lambda ins: dve_pre.done(ins, "head"),
                               lambda ins: dve_pre.done(ins, "rest"), lambda: dve_pre.wait(dve, i, "head"))
                    if slot == 3:
                        pe_pre.wait(dve, i, "logits")
                        wide = lambda t: t[:].rearrange("p (s a) -> p s a", a=1).to_broadcast([P, SUB, E])
                        dve_pre.done(dve.tensor_tensor(lg[:], psB[:, :, 0:E], over_chunks(br[:], SUB), ALU.add), "lg")
                        dve_pre.wait(dve, i, "lg")
                        dve_pre.done(dve.tensor_reduce(mx[:], lg[:], AX.X, ALU.max), "mx")
                        dve_pre.wait(dve, i, "mx")
                        dve_pre.done(dve.tensor_tensor(lg[:], lg[:], wide(mx), ALU.subtract), "sub")
                    if slot == 4:
                        own.begin(i)
                        wide = lambda t: t[:].rearrange("p (s a) -> p s a", a=1).to_broadcast([P, SUB, E])
                        act_pre.wait(dve, i, "ex")
                        dve_pre.done(dve.tensor_reduce(total[:], ex[:], AX.X, ALU.add), "total")
                        dve_pre.wait(dve, i, "total")
                        dve_pre.done(dve.reciprocal(total[:], total[:]), "rtotal")
                        dve_pre.wait(dve, i, "rtotal")
                        dve_pre.done(dve.tensor_tensor(pr[:], ex[:], wide(total), ALU.mult), "pr")
                        dve_pre.wait(dve, i, "pr")
                        for s in range(SUB):
                            m.settle(dve)
                            ins = dve.max(top[:, s, :], pr[:, s, :])
                            own.mark(ins) if s < SUB - 1 else dve_pre.done(ins, "top")
                        own.wait(dve)
                        dve_pre.wait(dve, i, "top")
                        for s in range(SUB):
                            m.settle(dve)
                            ins = dve.max_index(index[:, s, :], top[:, s, :], pr[:, s, :])
                            own.mark(ins) if s < SUB - 1 else dve_pre.done(ins, "index")
                        own.wait(dve)
                        dve_pre.wait(dve, i, "index")
                        dve_pre.done(dve.tensor_copy(indexf[:], index[:]), "indexf")
                    if slot == 5:
                        own.base, own.n = i * own.per, 2 * (SUB - 1)
                        dve_pre.done(dve.tensor_tensor(mx[:], top[:, :, 0], top[:, :, 1], ALU.add), "sum2")
                        dve_pre.wait(dve, i, "sum2")
                        dve_pre.done(dve.tensor_scalar(mx[:], mx[:], 1e-8, None, ALU.add), "rsum2")
                        dve_pre.wait(dve, i, "rsum2")
                        own.link(dve, dve.reciprocal(mx[:], mx[:]))
                        own.link(dve, dve.tensor_tensor(share[:, :, 0], top[:, :, 0], mx[:], ALU.mult))
                        dve_pre.done(dve.tensor_tensor(share[:, :, 1], top[:, :, 1], mx[:], ALU.mult), "share")
                        dve_pre.wait(dve, i, "share")
                        chosen = lambda t, k: t[:, :, k:k + 1].to_broadcast([P, SUB, E])
                        own.link(dve, dve.tensor_tensor(pick0[:], over_chunks(number[:], SUB), chosen(indexf, 0), ALU.is_equal))
                        own.link(dve, dve.tensor_tensor(pick1[:], over_chunks(number[:], SUB), chosen(indexf, 1), ALU.is_equal))
                        dve_pre.done(dve.tensor_tensor(pick0[:], pick0[:], chosen(share, 0), ALU.mult), "pick0")
                        dve_pre.done(dve.tensor_tensor(pick1[:], pick1[:], chosen(share, 1), ALU.mult), "pick1")
                        dve_pre.wait(dve, i, "pick1")
                        dve_pre.done(dve.tensor_tensor(comb[par][:], pick0[:], pick1[:], ALU.add), "comb")
                        own.end()
                    if slot == 6:
                        pe_pre.wait(dve, i, "combT")
                        dve_pre.done(dve.tensor_copy(combT[:].rearrange("e s t -> e (s t)"), psM[0:E, 0, :]), "combT")
                    if slot == 7:
                        pe_pre.wait(dve, i, "bias")
                        dve_pre.done(dve.tensor_copy(acc[par][:], psB[:]), "bias")

                def split_hidden(i, e):
                    dve.wait_ge(hid_ready, (i * E + e + 1) * FT)
                    if not (isinstance(i, int) and i == 0 and e < 2):
                        dve.wait_ge(out_psum, i * E + (e - 1) if e else i * E - 1)
                    head, rest = (flat(hid2[e % 2][k][:]) for k in two)
                    divide(head, rest, flat(hid[e % 2][:]), lambda ins: ins.then_inc(head_ready, 1),
                           lambda ins: ins.then_inc(rest_ready, 1), lambda: dve.wait_ge(head_ready, i * E + e + 1))

                def add(i, par, e):
                    dve.wait_ge(out_psum, i * E + e + 1)
                    if e == 0:
                        dve_pre.wait(dve, i, "bias")
                    else:
                        dve.wait_ge(added, i * E + e)
                    for s in range(SUB):
                        ins = dve.scalar_tensor_tensor(
                            out=acc[par][:, s, :], in0=psE[e % 2][:, s, :], scalar=comb[par][:, s, e:e + 1],
                            in1=acc[par][:, s, :], op0=ALU.mult, op1=ALU.add)
                        if s == 0:
                            ins.then_inc(dve_own, 1)
                    dve.wait_ge(dve_own, i * E + e + 1)
                    ins.then_inc(added, 1)

                def finish_a(i, par):
                    dve.wait_ge(added, (i + 1) * E)
                    dve.wait_ge(end_loaded[par], (i - par) * 24 + 48)
                    dve.scalar_tensor_tensor(out=gin[:], in0=acc[par][:], scalar=0.3, in1=xn[par][:],
                                             op0=ALU.mult, op1=ALU.add).then_inc(gin_ready, 1)

                def finish_b(i, par):
                    dve.wait_ge(gin_ready, i + 1)
                    dve.wait_ge(th_ready, i + 1)
                    dve.wait_ge(out_st, 16 * i)
                    dve.scalar_tensor_tensor(out=res[:], in0=th[:], scalar=1.0, in1=gin[:],
                                             op0=ALU.add, op1=ALU.mult).then_inc(half1, 1)
                    dve.wait_ge(half1, 2 * i + 1)
                    dve.scalar_tensor_tensor(out=res[:], in0=res[:], scalar=0.5, in1=s1[par][:],
                                             op0=ALU.mult, op1=ALU.mult).then_inc(half1, 1)
                    dve.wait_ge(half1, 2 * i + 2)
                    dve.tensor_tensor(res[:], res[:], x1[par][:], ALU.add).then_inc(res_ready, 1)

                def split_weights(e):
                    for k in two:
                        dve.wait_ge(staged[k], 16 * (e + 1))
                        head, rest = (((w2 if k else w1)[part][:, e, :, :].rearrange("p a b -> p (a b)")) for part in two)
                        divide(head, rest, stage[k][:], lambda ins: ins.then_inc(split, 1),
                               lambda ins: ins.then_inc(split, 1), lambda: dve.wait_ge(split, 4 * e + 2 * k + 1))

                def step(i, par, first, more):
                    for e in range(E):
                        if first and e + 2 < E:
                            split_weights(e + 2)
                        if e + 1 < E:
                            split_hidden(i, e + 1)
                        elif more:
                            split_hidden(i + 1, 0)
                        add(i, par, e)
                        if more:
                            prepare(i + 1, 1 - par, e)
                        if not first and e == 1:
                            finish_a(i - 1, 1 - par)
                        if not first and e == 6:
                            finish_b(i - 1, 1 - par)

                dve.wait_ge(weights, 96)
                dve.wait_ge(consts, 3)
                for slot in range(E):
                    prepare(0, 0, slot)
                split_weights(0)
                split_weights(1)
                split_hidden(0, 0)
                run(dve, step)
                finish_a(NT - 1, 1)
                finish_b(NT - 1, 1)


PHASES = [ssm_inputs, ssm_scan, ssm_output, delta_inputs, delta_invert, delta_chunks, attention, experts]


def build(nc, A, phases=None):
    for phase in PHASES:
        if phases is None or phase.__name__ in phases:
            with nc.cleanup_on_exit(), nc.allow_non_contiguous_dma(reason="small vectors of weights"):
                phase(nc, A)


def _layout(inputs):
    a = {k: np.asarray(v) for k, v in inputs.items()}

    def of(block):
        return lambda name: a[f"{block}_{name}"]

    ssm, fp8, delta, moe = of("L0_attn"), of("L0_ffn"), of("L1_attn"), of("L1_ffn")
    keys = np.arange(P).reshape(NH // 4, 4, HD).transpose(0, 2, 1).reshape(-1)
    used = np.arange(2 * P).reshape(NH, 2 * HD)[:, :HD].reshape(-1)[keys]
    laid = dict(
        x=ssm("hidden_states").reshape(N, D), w_xz=ssm("W_xz"), w_dt=ssm("W_dt"), b_dt=ssm("b_dt"),
        w_bc=np.concatenate([ssm("W_B"), ssm("W_C")], 1), a_log=ssm("A_log"), d_skip=ssm("D_skip"),
        w_out=ssm("W_out"), v_th=ssm("v_th"),
        kern=fp8("kernel"), s_in=fp8("input_scale"), s_k=fp8("kernel_scale"), bias=fp8("bias"),
        w_tok=np.concatenate([delta(n) for n in ("Wq", "Wk", "Wv", "Wa", "Wb")], 0).T,
        b_tok=np.concatenate([delta(n) for n in ("bq", "bk", "bv", "ba", "bb")]),
        w_gate=delta("Wg").T, b_gate=delta("bg"), w_o=delta("Wo").T, b_o=delta("bo"),
        fq=moe("q_w")[:, used], fqb=moe("q_b")[used], fk=moe("k_w")[:, keys], fkb=moe("k_b")[keys], fv=moe("v_w"), fvb=moe("v_b"),
        fo=moe("o_w"), fob=moe("o_b"), rw=moe("router_w"), rb=moe("router_b"),
        w1=moe("w1"), b1=moe("b1"), w2=moe("w2"), b2=moe("b2"))
    return {k: np.ascontiguousarray(v) for k, v in laid.items()}


def kernel(**inputs):
    import concourse.bacc as bacc
    from concourse.bass_utils import run_bass_kernel_spmd

    nc = bacc.Bacc("TRN2", target_bir_lowering=False, num_devices=1)
    arrays, A = {}, {}
    for name, value in _layout(inputs).items():
        arrays[f"in_{name}"] = value
        A[name] = nc.dram_tensor(f"in_{name}", value.shape, mybir.dt.from_np(value.dtype), kind="ExternalInput").ap()
    kinds = {"float32": F32, "bfloat16": BF16}
    for name, (shape, dtype) in SCRATCH.items():
        A[name] = nc.dram_tensor(f"scratch_{name}", shape, kinds[dtype]).ap()
    A["out"] = nc.dram_tensor("out_dram", (N, D), F32, kind="ExternalOutput").ap()
    build(nc, A)
    r = run_bass_kernel_spmd(nc, [arrays], core_ids=[0])
    return r.results[0]["out_dram"].reshape(B, T, D)
```
